# Optimizing a Trainium2 kernel written in Bass

```python
import numpy as np
import jax
import jax.numpy as jnp

def _softmax(x, axis=-1):
    return jax.nn.softmax(x, axis=axis)

def _gelu(x):
    return jax.nn.gelu(x, approximate=True)

def _silu(x):
    return jax.nn.silu(x)

def _sigmoid(x):
    return jax.nn.sigmoid(x)

def _layernorm(x, axis=-1, eps=1e-05):
    m = jnp.mean(x, axis=axis, keepdims=True)
    v = jnp.var(x, axis=axis, keepdims=True)
    return (x - m) / jnp.sqrt(v + eps)

def _scatter_add(tgt, idx, src, axis=0):
    return tgt.at[idx].add(src)

def _segment_sum(src, seg, n):
    return jax.ops.segment_sum(src, seg, n)
kernel_name = 'mk_sandwich_d2_jaxref_r8_14acb0'

def setup_inputs(seed: int=0):
    np.random.seed(seed)
    _w = jnp.asarray

    def _L0_attn_setup():
        import jax, jax.numpy as jnp
        import numpy as np
        D_MODEL = 128
        N_HEADS = 16
        D_LATENT = 32
        HEAD_DIM = D_MODEL // N_HEADS

        def apply_rope(x):
            B, T, H, D = x.shape
            inv_freq = 1.0 / 10000.0 ** (jnp.arange(0, D, 2, dtype=jnp.float32) / D)
            t = jnp.arange(T, dtype=jnp.float32)
            freqs = t[:, None] * inv_freq[None, :]
            sin_f = jnp.sin(freqs)[None, :, None, :]
            cos_f = jnp.cos(freqs)[None, :, None, :]
            x1, x2 = jnp.split(x, 2, axis=-1)
            return jnp.concatenate([x1 * cos_f - x2 * sin_f, x1 * sin_f + x2 * cos_f], axis=-1)
        key = jax.random.key(seed)
        ks = jax.random.split(key, 10)
        B, T = (4, 512)
        s = lambda fan_in: 1.0 / np.sqrt(fan_in)
        return {'x': jax.random.normal(ks[0], (B, T, D_MODEL), dtype=jnp.float32), 'Wq': jax.random.normal(ks[1], (D_MODEL, D_MODEL), dtype=jnp.float32) * s(D_MODEL), 'bq': jnp.zeros((D_MODEL,), jnp.float32), 'Wdown': jax.random.normal(ks[2], (D_MODEL, D_LATENT), dtype=jnp.float32) * s(D_MODEL), 'bdown': jnp.zeros((D_LATENT,), jnp.float32), 'Wup': jax.random.normal(ks[3], (D_LATENT, 2 * D_MODEL), dtype=jnp.float32) * s(D_LATENT), 'bup': jnp.zeros((2 * D_MODEL,), jnp.float32), 'Wout': jax.random.normal(ks[4], (D_MODEL, D_MODEL), dtype=jnp.float32) * s(D_MODEL), 'bout': jnp.zeros((D_MODEL,), jnp.float32)}
    _L0_attn_in = _L0_attn_setup()

    def _L0_ffn_setup():
        import jax, jax.numpy as jnp
        import numpy as np
        DIM = 128
        DEPTH = 2
        HEADS = 8
        DIM_HEAD = 64
        WINDOW = 64
        INNER = HEADS * DIM_HEAD
        HID = int(DIM * 4 * 2 / 3)
        B, N = (2, 1024)
        QK_SCALE = 8.0

        def shift_token(t):
            t1, t2 = jnp.split(t, 2, axis=-1)
            t2 = jnp.pad(t2, ((0, 0), (1, 0), (0, 0)))[:, :-1]
            return jnp.concatenate([t1, t2], axis=-1)

        def l2norm(t):
            return t / jnp.clip(jnp.linalg.norm(t, axis=-1, keepdims=True), 1e-12)

        def rotate_half(x):
            x1, x2 = jnp.split(x, 2, axis=-1)
            return jnp.concatenate([-x2, x1], axis=-1)

        def rotary_xpos(q, k):
            n = q.shape[-2]
            half_idx = jnp.arange(0, DIM_HEAD, 2, dtype=jnp.float32)
            inv_freq = 1.0 / 10000.0 ** (half_idx / DIM_HEAD)
            t = jnp.arange(n, dtype=jnp.float32)
            freqs = t[:, None] * inv_freq[None, :]
            freqs = jnp.concatenate([freqs, freqs], axis=-1)
            base = (half_idx + 0.4 * DIM_HEAD) / (1.4 * DIM_HEAD)
            power = (t - n // 2) / float(WINDOW // 2)
            scale = base[None, :] ** power[:, None]
            scale = jnp.concatenate([scale, scale], axis=-1)
            cos, sin = (jnp.cos(freqs), jnp.sin(freqs))
            q = q * cos * scale + rotate_half(q) * sin * scale
            k = k * cos / scale + rotate_half(k) * sin / scale
            return (q, k)

        def local_attention(q, k, v):
            b, h, n, d = q.shape
            w = n // WINDOW
            bq = q.reshape(b, h, w, WINDOW, d) * QK_SCALE
            bk = k.reshape(b, h, w, WINDOW, d)
            bv = v.reshape(b, h, w, WINDOW, d)

            def look_around(t):
                p = jnp.pad(t, ((0, 0), (0, 0), (1, 0), (0, 0), (0, 0)))
                return jnp.concatenate([p[:, :, :w], p[:, :, 1:]], axis=3)
            bk, bv = (look_around(bk), look_around(bv))
            bt = jnp.arange(n).reshape(w, WINDOW)
            btp = jnp.pad(bt, ((1, 0), (0, 0)), constant_values=-1)
            btk = jnp.concatenate([btp[:w], btp[1:]], axis=1)
            sim = jnp.einsum('bhwid,bhwjd->bhwij', bq, bk)
            i = bt[:, :, None]
            j = btk[:, None, :]
            mask = (i < j) | (i > j + WINDOW) | (j == -1)
            sim = jnp.where(mask, -jnp.finfo(sim.dtype).max, sim)
            attn = jax.nn.softmax(sim, axis=-1)
            out = jnp.einsum('bhwij,bhwjd->bhwid', attn, bv)
            return out.reshape(b, h, n, d)

        def _layer(x, wqkv, qs, ksc, wo, lg, lb, w1, b1, w2, b2):
            b, n, _ = x.shape
            h = shift_token(x)
            qkv = h @ wqkv
            q, k, v = jnp.split(qkv, 3, axis=-1)
            to_heads = lambda t: t.reshape(b, n, HEADS, DIM_HEAD).transpose(0, 2, 1, 3)
            q, k, v = (to_heads(q), to_heads(k), to_heads(v))
            q = l2norm(q) * qs
            k = l2norm(k) * ksc
            q, k = rotary_xpos(q, k)
            o = local_attention(q, k, v)
            o = o.transpose(0, 2, 1, 3).reshape(b, n, INNER)
            x = x + o @ wo
            h = shift_token(x)
            mu = h.mean(-1, keepdims=True)
            var = h.var(-1, keepdims=True)
            h = (h - mu) / jnp.sqrt(var + 1e-05) * lg + lb
            h = h @ w1 + b1
            a, g = jnp.split(h, 2, axis=-1)
            h = a * jax.nn.gelu(g, approximate=False)
            x = x + h @ w2 + b2
            return x
        key = jax.random.key(seed)
        ks = jax.random.split(key, 6)
        return {'x': jax.random.normal(ks[0], (B, N, DIM), jnp.float32), 'wqkv': jax.random.normal(ks[1], (DEPTH, DIM, 3 * INNER), jnp.float32) * 0.02, 'q_scale': jnp.ones((DEPTH, DIM_HEAD), jnp.float32), 'k_scale': jnp.ones((DEPTH, DIM_HEAD), jnp.float32), 'wo': jax.random.normal(ks[2], (DEPTH, INNER, DIM), jnp.float32) * 0.02, 'ln_g': jnp.ones((DEPTH, DIM), jnp.float32), 'ln_b': jnp.zeros((DEPTH, DIM), jnp.float32), 'w1': jax.random.normal(ks[3], (DEPTH, DIM, 2 * HID), jnp.float32) * 0.02, 'b1': jnp.zeros((DEPTH, 2 * HID), jnp.float32), 'w2': jax.random.normal(ks[4], (DEPTH, HID, DIM), jnp.float32) * 0.02, 'b2': jnp.zeros((DEPTH, DIM), jnp.float32)}
    _L0_ffn_in = _L0_ffn_setup()

    def _L1_attn_setup():
        import jax, jax.numpy as jnp
        import numpy as np
        RSQRT2 = 2 ** (-0.5)
        B, S, D_IN = (2, 512, 128)
        H, D_HEAD = (8, 64)
        QK_DIM = H * D_HEAD
        V_DIM = H * D_HEAD
        OUT_DIM = D_IN
        LN_EPS = 1e-05

        def _layernorm(y, gamma, beta):
            mu = jnp.mean(y, axis=-1, keepdims=True)
            var = jnp.mean(jnp.square(y - mu), axis=-1, keepdims=True)
            return (y - mu) * jax.lax.rsqrt(var + LN_EPS) * gamma + beta
        key = jax.random.key(seed)
        ks = jax.random.split(key, 8)

        def lecun(k, fan_in, shape):
            return jax.random.normal(k, shape, dtype=jnp.float32) * (1.0 / np.sqrt(fan_in))
        return {'x': jax.random.normal(ks[0], (B, S, D_IN), dtype=jnp.float32), 'W_qk': lecun(ks[1], D_IN, (D_IN, 2 * QK_DIM)), 'b_qk': jnp.zeros((2 * QK_DIM,), jnp.float32), 'W_v': lecun(ks[2], D_IN, (D_IN, V_DIM)), 'b_v': jnp.zeros((V_DIM,), jnp.float32), 'W_out': lecun(ks[3], V_DIM, (V_DIM, OUT_DIM)), 'b_out': jnp.zeros((OUT_DIM,), jnp.float32), 'ln_gamma': jnp.ones((OUT_DIM,), jnp.float32), 'ln_beta': jnp.zeros((OUT_DIM,), jnp.float32)}
    _L1_attn_in = _L1_attn_setup()

    def _L1_ffn_setup():
        import math
        import jax, jax.numpy as jnp
        from jax import lax
        import numpy as np
        E = 16
        K = 2
        CF = 1.25
        key = jax.random.key(seed)
        k0, k1, k2, k3, k4 = jax.random.split(key, 5)
        B, S, D, H = (2, 256, 128, 128)
        scale = 0.02
        return {'x': jax.random.normal(k0, (B, S, D), dtype=jnp.float32), 'router_w': jax.random.normal(k1, (D, E), dtype=jnp.float32) * scale, 'gate_w': jax.random.normal(k2, (E, D, H), dtype=jnp.float32) * scale, 'up_w': jax.random.normal(k3, (E, D, H), dtype=jnp.float32) * scale, 'down_w': jax.random.normal(k4, (E, H, D), dtype=jnp.float32) * scale}
    _L1_ffn_in = _L1_ffn_setup()
    _d = {'L0_attn_x': _L0_attn_in['x'], 'L0_attn_Wq': _L0_attn_in['Wq'], 'L0_attn_bq': _L0_attn_in['bq'], 'L0_attn_Wdown': _L0_attn_in['Wdown'], 'L0_attn_bdown': _L0_attn_in['bdown'], 'L0_attn_Wup': _L0_attn_in['Wup'], 'L0_attn_bup': _L0_attn_in['bup'], 'L0_attn_Wout': _L0_attn_in['Wout'], 'L0_attn_bout': _L0_attn_in['bout'], 'L0_ffn_wqkv': _L0_ffn_in['wqkv'], 'L0_ffn_q_scale': _L0_ffn_in['q_scale'], 'L0_ffn_k_scale': _L0_ffn_in['k_scale'], 'L0_ffn_wo': _L0_ffn_in['wo'], 'L0_ffn_ln_g': _L0_ffn_in['ln_g'], 'L0_ffn_ln_b': _L0_ffn_in['ln_b'], 'L0_ffn_w1': _L0_ffn_in['w1'], 'L0_ffn_b1': _L0_ffn_in['b1'], 'L0_ffn_w2': _L0_ffn_in['w2'], 'L0_ffn_b2': _L0_ffn_in['b2'], 'L1_attn_W_qk': _L1_attn_in['W_qk'], 'L1_attn_b_qk': _L1_attn_in['b_qk'], 'L1_attn_W_v': _L1_attn_in['W_v'], 'L1_attn_b_v': _L1_attn_in['b_v'], 'L1_attn_W_out': _L1_attn_in['W_out'], 'L1_attn_b_out': _L1_attn_in['b_out'], 'L1_attn_ln_gamma': _L1_attn_in['ln_gamma'], 'L1_attn_ln_beta': _L1_attn_in['ln_beta'], 'L1_ffn_router_w': _L1_ffn_in['router_w'], 'L1_ffn_gate_w': _L1_ffn_in['gate_w'], 'L1_ffn_up_w': _L1_ffn_in['up_w'], 'L1_ffn_down_w': _L1_ffn_in['down_w']}
    _x0 = _d['L0_attn_x']
    _d['L0_attn_x'] = jax.random.normal(jax.random.fold_in(jax.random.key(seed), 1), (4, 1024, 128), dtype=_x0.dtype)
    del _x0
    return _d

def reference(L0_attn_x, L0_attn_Wq, L0_attn_bq, L0_attn_Wdown, L0_attn_bdown, L0_attn_Wup, L0_attn_bup, L0_attn_Wout, L0_attn_bout, L0_ffn_wqkv, L0_ffn_q_scale, L0_ffn_k_scale, L0_ffn_wo, L0_ffn_ln_g, L0_ffn_ln_b, L0_ffn_w1, L0_ffn_b1, L0_ffn_w2, L0_ffn_b2, L1_attn_W_qk, L1_attn_b_qk, L1_attn_W_v, L1_attn_b_v, L1_attn_W_out, L1_attn_b_out, L1_attn_ln_gamma, L1_attn_ln_beta, L1_ffn_router_w, L1_ffn_gate_w, L1_ffn_up_w, L1_ffn_down_w):

    def _L0_attn_ref(x, Wq, bq, Wdown, bdown, Wup, bup, Wout, bout):
        import jax, jax.numpy as jnp
        import numpy as np
        D_MODEL = 128
        N_HEADS = 16
        D_LATENT = 32
        HEAD_DIM = D_MODEL // N_HEADS

        def apply_rope(x):
            B, T, H, D = x.shape
            inv_freq = 1.0 / 10000.0 ** (jnp.arange(0, D, 2, dtype=jnp.float32) / D)
            t = jnp.arange(T, dtype=jnp.float32)
            freqs = t[:, None] * inv_freq[None, :]
            sin_f = jnp.sin(freqs)[None, :, None, :]
            cos_f = jnp.cos(freqs)[None, :, None, :]
            x1, x2 = jnp.split(x, 2, axis=-1)
            return jnp.concatenate([x1 * cos_f - x2 * sin_f, x1 * sin_f + x2 * cos_f], axis=-1)
        B, T, D = x.shape
        H, Dh = (N_HEADS, HEAD_DIM)
        q = x @ Wq + bq
        kv_latent = x @ Wdown + bdown
        kv = kv_latent @ Wup + bup
        q = q.reshape(B, T, H, Dh)
        kv = kv.reshape(B, T, H, 2 * Dh)
        k, v = jnp.split(kv, 2, axis=-1)
        q = apply_rope(q)
        k = apply_rope(k)
        att = jnp.einsum('bthd,btgd->bthg', q, k) / jnp.sqrt(jnp.float32(Dh))
        att = jax.nn.softmax(att, axis=-1)
        out = jnp.einsum('bthg,btgd->bthd', att, v)
        out = out.reshape(B, T, D)
        return out @ Wout + bout

    def _L0_ffn_ref(x, wqkv, q_scale, k_scale, wo, ln_g, ln_b, w1, b1, w2, b2):
        import jax, jax.numpy as jnp
        import numpy as np
        DIM = 128
        DEPTH = 2
        HEADS = 8
        DIM_HEAD = 64
        WINDOW = 64
        INNER = HEADS * DIM_HEAD
        HID = int(DIM * 4 * 2 / 3)
        B, N = (2, 1024)
        QK_SCALE = 8.0

        def shift_token(t):
            t1, t2 = jnp.split(t, 2, axis=-1)
            t2 = jnp.pad(t2, ((0, 0), (1, 0), (0, 0)))[:, :-1]
            return jnp.concatenate([t1, t2], axis=-1)

        def l2norm(t):
            return t / jnp.clip(jnp.linalg.norm(t, axis=-1, keepdims=True), 1e-12)

        def rotate_half(x):
            x1, x2 = jnp.split(x, 2, axis=-1)
            return jnp.concatenate([-x2, x1], axis=-1)

        def rotary_xpos(q, k):
            n = q.shape[-2]
            half_idx = jnp.arange(0, DIM_HEAD, 2, dtype=jnp.float32)
            inv_freq = 1.0 / 10000.0 ** (half_idx / DIM_HEAD)
            t = jnp.arange(n, dtype=jnp.float32)
            freqs = t[:, None] * inv_freq[None, :]
            freqs = jnp.concatenate([freqs, freqs], axis=-1)
            base = (half_idx + 0.4 * DIM_HEAD) / (1.4 * DIM_HEAD)
            power = (t - n // 2) / float(WINDOW // 2)
            scale = base[None, :] ** power[:, None]
            scale = jnp.concatenate([scale, scale], axis=-1)
            cos, sin = (jnp.cos(freqs), jnp.sin(freqs))
            q = q * cos * scale + rotate_half(q) * sin * scale
            k = k * cos / scale + rotate_half(k) * sin / scale
            return (q, k)

        def local_attention(q, k, v):
            b, h, n, d = q.shape
            w = n // WINDOW
            bq = q.reshape(b, h, w, WINDOW, d) * QK_SCALE
            bk = k.reshape(b, h, w, WINDOW, d)
            bv = v.reshape(b, h, w, WINDOW, d)

            def look_around(t):
                p = jnp.pad(t, ((0, 0), (0, 0), (1, 0), (0, 0), (0, 0)))
                return jnp.concatenate([p[:, :, :w], p[:, :, 1:]], axis=3)
            bk, bv = (look_around(bk), look_around(bv))
            bt = jnp.arange(n).reshape(w, WINDOW)
            btp = jnp.pad(bt, ((1, 0), (0, 0)), constant_values=-1)
            btk = jnp.concatenate([btp[:w], btp[1:]], axis=1)
            sim = jnp.einsum('bhwid,bhwjd->bhwij', bq, bk)
            i = bt[:, :, None]
            j = btk[:, None, :]
            mask = (i < j) | (i > j + WINDOW) | (j == -1)
            sim = jnp.where(mask, -jnp.finfo(sim.dtype).max, sim)
            attn = jax.nn.softmax(sim, axis=-1)
            out = jnp.einsum('bhwij,bhwjd->bhwid', attn, bv)
            return out.reshape(b, h, n, d)

        def _layer(x, wqkv, qs, ksc, wo, lg, lb, w1, b1, w2, b2):
            b, n, _ = x.shape
            h = shift_token(x)
            qkv = h @ wqkv
            q, k, v = jnp.split(qkv, 3, axis=-1)
            to_heads = lambda t: t.reshape(b, n, HEADS, DIM_HEAD).transpose(0, 2, 1, 3)
            q, k, v = (to_heads(q), to_heads(k), to_heads(v))
            q = l2norm(q) * qs
            k = l2norm(k) * ksc
            q, k = rotary_xpos(q, k)
            o = local_attention(q, k, v)
            o = o.transpose(0, 2, 1, 3).reshape(b, n, INNER)
            x = x + o @ wo
            h = shift_token(x)
            mu = h.mean(-1, keepdims=True)
            var = h.var(-1, keepdims=True)
            h = (h - mu) / jnp.sqrt(var + 1e-05) * lg + lb
            h = h @ w1 + b1
            a, g = jnp.split(h, 2, axis=-1)
            h = a * jax.nn.gelu(g, approximate=False)
            x = x + h @ w2 + b2
            return x
        for l in range(DEPTH):
            x = _layer(x, wqkv[l], q_scale[l], k_scale[l], wo[l], ln_g[l], ln_b[l], w1[l], b1[l], w2[l], b2[l])
        return x

    def _L1_attn_ref(x, W_qk, b_qk, W_v, b_v, W_out, b_out, ln_gamma, ln_beta):
        import jax, jax.numpy as jnp
        import numpy as np
        RSQRT2 = 2 ** (-0.5)
        B, S, D_IN = (2, 512, 128)
        H, D_HEAD = (8, 64)
        QK_DIM = H * D_HEAD
        V_DIM = H * D_HEAD
        OUT_DIM = D_IN
        LN_EPS = 1e-05

        def _layernorm(y, gamma, beta):
            mu = jnp.mean(y, axis=-1, keepdims=True)
            var = jnp.mean(jnp.square(y - mu), axis=-1, keepdims=True)
            return (y - mu) * jax.lax.rsqrt(var + LN_EPS) * gamma + beta
        b, s, _ = x.shape
        scale = D_HEAD ** (-0.5)
        qk = x @ W_qk + b_qk
        qk = qk.reshape(b, s, H, D_HEAD, 2)
        q, k = (qk[..., 0], qk[..., 1])
        v = (x @ W_v + b_v).reshape(b, s, H, D_HEAD)
        sim = jnp.einsum('bihd,bjhd->bhij', q, k) * scale
        attn = jax.nn.softmax(sim, axis=-1)
        o = jnp.einsum('bhij,bjhd->bihd', attn, v)
        o = o.reshape(b, s, V_DIM)
        y = _layernorm(o @ W_out + b_out, ln_gamma, ln_beta)
        return (y + x) * RSQRT2

    def _L1_ffn_ref(x, router_w, gate_w, up_w, down_w):
        import math
        import jax, jax.numpy as jnp
        from jax import lax
        import numpy as np
        E = 16
        K = 2
        CF = 1.25
        B, S, D = x.shape
        xf = x.reshape(-1, D)
        T = B * S
        capacity = max(1, math.ceil(T * K / E * CF))
        Cbuf = K * capacity
        logits = xf @ router_w
        probs = jax.nn.softmax(logits, axis=-1)
        w, idx = lax.top_k(probs, K)
        oh = jax.nn.one_hot(idx, E, dtype=w.dtype)
        rank = jnp.cumsum(oh, axis=0) - oh
        myrank = jnp.sum(rank * oh, axis=-1)
        keep = myrank < capacity
        w = jnp.where(keep, w, 0.0)
        flat_e = idx.reshape(-1)
        flat_w = w.reshape(-1)
        keep_f = keep.reshape(-1)
        tok = jnp.repeat(jnp.arange(T, dtype=jnp.int32), K)
        ohk = jax.nn.one_hot(flat_e, E, dtype=jnp.int32) * keep_f[:, None].astype(jnp.int32)
        pos = jnp.cumsum(ohk, axis=0) - ohk
        slot = jnp.sum(pos * ohk, axis=-1)
        e_idx = jnp.where(keep_f, flat_e, E)
        dispatch = jnp.full((E + 1, Cbuf), T, dtype=jnp.int32).at[e_idx, slot].set(tok)
        wbuf = jnp.zeros((E + 1, Cbuf), dtype=w.dtype).at[e_idx, slot].set(flat_w)
        dispatch = dispatch[:E]
        wbuf = wbuf[:E]
        x_pad = jnp.concatenate([xf, jnp.zeros((1, D), xf.dtype)], axis=0)
        xe = x_pad[dispatch]
        gate = jnp.einsum('ecd,edh->ech', xe, gate_w)
        up = jnp.einsum('ecd,edh->ech', xe, up_w)
        hidden = jax.nn.silu(gate) * up
        out = jnp.einsum('ech,ehd->ecd', hidden, down_w)
        out = out * wbuf[:, :, None]
        combined = jnp.zeros((T + 1, D), dtype=xf.dtype).at[dispatch.reshape(-1)].add(out.reshape(-1, D))
        return combined[:T].reshape(B, S, D)
    x = L0_attn_x
    x = x + _layernorm(_L0_attn_ref(_layernorm(x, axis=-1), L0_attn_Wq, L0_attn_bq, L0_attn_Wdown, L0_attn_bdown, L0_attn_Wup, L0_attn_bup, L0_attn_Wout, L0_attn_bout), axis=-1)
    x = x + _layernorm(_L0_ffn_ref(_layernorm(x, axis=-1), L0_ffn_wqkv, L0_ffn_q_scale, L0_ffn_k_scale, L0_ffn_wo, L0_ffn_ln_g, L0_ffn_ln_b, L0_ffn_w1, L0_ffn_b1, L0_ffn_w2, L0_ffn_b2), axis=-1)
    x = x + _layernorm(_L1_attn_ref(_layernorm(x, axis=-1), L1_attn_W_qk, L1_attn_b_qk, L1_attn_W_v, L1_attn_b_v, L1_attn_W_out, L1_attn_b_out, L1_attn_ln_gamma, L1_attn_ln_beta), axis=-1)
    x = x + _layernorm(_L1_ffn_ref(_layernorm(x, axis=-1), L1_ffn_router_w, L1_ffn_gate_w, L1_ffn_up_w, L1_ffn_down_w), axis=-1)
    return x

_drawn_inputs = setup_inputs


def setup_inputs(seed=0):
    import zlib

    import numpy as np

    out = dict(_drawn_inputs(seed))
    spreads = {'L0_attn_bq': (0.0, 0.1),
     'L0_attn_bdown': (0.0, 0.1),
     'L0_attn_bup': (0.0, 0.1),
     'L0_attn_bout': (0.0, 0.1),
     'L0_ffn_q_scale': (1.0, 0.6),
     'L0_ffn_k_scale': (1.0, 0.6),
     'L0_ffn_ln_g': (1.0, 0.6),
     'L0_ffn_ln_b': (0.0, 0.8),
     'L0_ffn_b1': (0.0, 0.8),
     'L0_ffn_b2': (0.0, 0.506),
     'L1_attn_b_qk': (0.0, 0.73),
     'L1_attn_b_v': (0.0, 0.1),
     'L1_attn_b_out': (0.0, 0.1),
     'L1_attn_ln_gamma': (1.0, 0.2),
     'L1_attn_ln_beta': (0.0, 0.31)}
    factors = {'L0_ffn_wqkv': 2.801, 'L0_ffn_w1': 5.81, 'L0_ffn_w2': 5.594}
    for name, (base, spread) in spreads.items():
        noise = np.random.default_rng([zlib.crc32(name.encode()), seed]).standard_normal(out[name].shape)
        drawn = base * np.exp(spread * noise) if base else spread * noise
        out[name] = jnp.asarray(drawn.astype(out[name].dtype))
    for name, factor in factors.items():
        out[name] = (out[name] * factor).astype(out[name].dtype)
    return out
```

```python
from collections import namedtuple
from contextlib import ExitStack

import concourse.bass as bass
from concourse import mybir

F32 = mybir.dt.float32
BF16 = mybir.dt.bfloat16
ALU = mybir.AluOpType
ACT = mybir.ActivationFunctionType
AX_X = mybir.AxisListType.X

P = 128
TOKENS = 4096
SEQ = 1024
TILES = TOKENS // P
SEQ_TILES = SEQ // P
BATCHES = TOKENS // SEQ
EPS = 1e-5

HEADS_A = 16
DIM_A = P // HEADS_A
LATENT = 32

LAYERS = 2
HEADS_B = 8
DIM_B = 64
INNER = HEADS_B * DIM_B
WINDOW = 64
KEYS_B = P + WINDOW
CHUNKS = INNER // P
HID_B = int(P * 4 * 2 / 3)

HEADS_C = 8
DIM_C = 64

EXPERTS = 16
CAPACITY = -(-TOKENS * 2 * 5 // (EXPERTS * 4))


class Group:
    pass


def sems(ctx, nc, prefix, names):
    found = [nc.alloc_semaphore(name=prefix + n) for n in names.split()]

    def clear():
        nc.clear_and_free_semaphores(found)
        nc.all_engine_barrier()

    ctx.callback(clear)
    return namedtuple("Semaphores", names)(*found)


def done(eng, sem, t):
    eng.wait_ge(sem, t + 1)


def freed(eng, sem, t, depth=2):
    if isinstance(t, int) and t < depth:
        return
    eng.wait_ge(sem, t - depth + 1)


def pipeline(eng, tiles, steps, unroll=2, depth=4):
    first = -(-(max(lag for lag, _ in steps) + depth) // unroll) * unroll
    whole = (tiles - first) // unroll
    end = first + unroll * whole

    def one_round(i, k):
        for lag, step in steps:
            if not isinstance(i, int) or 0 <= i + k - lag < tiles:
                step(i + k - lag, (first + k - lag) % unroll)

    for r in range(first):
        one_round(r - r % unroll, r % unroll)
    if whole == 1:
        for k in range(unroll):
            one_round(first, k)
    elif whole > 1:
        with eng.Fori(first, end - unroll + 1, unroll) as i:
            for k in range(unroll):
                one_round(i, k)
    for r in range(end, tiles + max(lag for lag, _ in steps)):
        one_round(r - r % unroll, r % unroll)


def over(ap, axis, count):
    shape = list(ap.shape)
    shape.insert(axis, count)
    return ap.unsqueeze(axis).to_broadcast(shape)


def l0_attention(nc, g, w, tab):
    with ExitStack() as ctx:
        def sb(name, shape, dt=F32):
            return ctx.enter_context(nc.sbuf_tensor("a_" + name, shape, dt))

        def pb(name, shape, dt=F32):
            return ctx.enter_context(nc.psum_tensor("a_" + name, shape, dt))

        down_up = sb("down_up", [P, 3 * P])
        bias = sb("bias", [1, 3 * P])
        wdown_t = sb("wdown_t", [LATENT, P])
        stats = sb("stats", [P, 2, 6])
        mean_var = sb("mean_var", [P, 4, 2])
        rstd = sb("rstd", [P, 2, 1])
        veps = sb("veps", [P, 2, 1])
        h = sb("h", [P, 2, P])
        h_t = sb("h_t", [P, 2, P])
        qk_raw = sb("qk_raw", [P, 2, 2 * P])
        v = sb("v", [P, 4, P])
        turned_c = sb("turned_c", [P, 2, 2 * P])
        turned_s = sb("turned_s", [P, 2, 2 * P])
        qk = sb("qk", [P, 2, 2 * P])
        prod_qk = sb("prod_qk", [P, 2, HEADS_A * HEADS_A * DIM_A])
        score = sb("score", [P, 2, HEADS_A * HEADS_A])
        top = sb("top", [P, 2, HEADS_A])
        shifted = sb("shifted", [P, 2, HEADS_A * HEADS_A])
        prob = sb("prob", [P, 2, HEADS_A * HEADS_A])
        total = sb("total", [P, 2, HEADS_A])
        inv = sb("inv", [P, 2, HEADS_A])
        prod_pv = sb("prod_pv", [P, 2, HEADS_A * HEADS_A * DIM_A])
        mixed = sb("mixed", [P, 2, P])
        o = sb("o", [P, 2, P])
        o_t = sb("o_t", [P, 2, P])
        stats2 = sb("stats2", [P, 2, 6])
        mean_var2 = sb("mean_var2", [P, 4, 2])
        rstd2 = sb("rstd2", [P, 2, 1])
        veps2 = sb("veps2", [P, 2, 1])
        y = sb("y", [P, 2, P])
        ps_h = pb("ps_h", [P, 512])
        ps_qkv = [pb(f"ps_qkv{u}", [P, 512]) for u in range(2)]
        ps_o = pb("ps_o", [P, 512])
        ps_out = [pb(f"ps_out{u}", [P, 512]) for u in range(4)]
        s = sems(ctx, nc, "a_", "wd_t wd_copy fold fold_w fold_b stats mean_var veps rstd h ps_h h_t ps_qkv qk_raw v "
                 "turn1 turn2 turn3 qk prod_qk score top shifted prob total inv prod_pv mixed o ps_o o_t "
                 "ps_out stats2 mean_var2 veps2 rstd2 y x")
        block = ctx.enter_context(nc.Block())

        def heads(ap):
            return ap.rearrange("p (h d) -> p h d", d=DIM_A)

        @block.tensor
        def _(pe):
            pe.wait_ge(g.ident_ready, 1)
            pe.wait_ge(w.small_loaded, w.small_count)
            pe.transpose(ps_h[0:LATENT, 0:P], w.wdown[:], g.ident[:]).then_inc(s.wd_t, 1)
            done(pe, s.wd_copy, 0)
            pe.matmul(ps_qkv[0][:, 0:2 * P], wdown_t[:], w.wup[:], start=True, stop=True)
            pe.matmul(ps_o[0:1, 0:2 * P], w.bdown[:], w.wup[:], start=True, stop=True).then_inc(s.fold, 1)

            def transpose_h(t, u4):
                u = u4 % 2
                done(pe, s.h, t)
                freed(pe, s.h_t, t, 1)
                if isinstance(t, int) and t == 0:
                    done(pe, s.wd_copy, 0)
                pe.transpose(ps_h[:, 0:P], h[:, u, :], g.ident[:]).then_inc(s.ps_h, 1)

            def project(t, u4):
                u = u4 % 2
                if isinstance(t, int) and t == 0:
                    pe.wait_ge(s.fold_w, 2)
                    pe.wait_ge(s.fold_b, 2)
                done(pe, s.h_t, t)
                freed(pe, s.v, t)
                pe.matmul(ps_qkv[u][:, 0:3 * P], h_t[:, u, :], down_up[:], start=True, stop=False)
                pe.matmul(ps_qkv[u][:, 0:3 * P], g.ones_row[:], bias[:], start=False, stop=True).then_inc(s.ps_qkv, 1)

            def transpose_o(t, u4):
                u = u4 % 2
                done(pe, s.o, t)
                freed(pe, s.o_t, t, 1)
                pe.transpose(ps_o[:, 0:P], o[:, u, :], g.ident[:]).then_inc(s.ps_o, 1)

            def project_out(t, u4):
                u = u4 % 2
                done(pe, s.o_t, t)
                freed(pe, s.y, t, 4)
                pe.matmul(ps_out[u4][:, 0:P], o_t[:, u, :], w.wout_a[:], start=True, stop=False)
                pe.matmul(ps_out[u4][:, 0:P], g.ones_row[:], w.bout_a[:], start=False, stop=True).then_inc(s.ps_out, 1)

            pipeline(pe, TILES, [(2, transpose_h), (2, project), (7, transpose_o), (7, project_out)], unroll=4)

        @block.scalar
        def _(act):
            done(act, s.wd_t, 0)
            act.activation(wdown_t[:], ps_h[0:LATENT, 0:P], ACT.Copy).then_inc(s.wd_copy, 1)
            act.wait_ge(w.small_loaded, w.small_count)
            act.activation(down_up[:, 0:P], w.wq_a[:], ACT.Copy).then_inc(s.fold_w, 1)
            act.activation(bias[:, 0:P], w.bq_a[:], ACT.Copy).then_inc(s.fold_b, 1)
            done(act, s.fold, 0)
            kv = "p (h a d) -> p a h d"
            act.activation(down_up[:, P:].rearrange("p (a h d) -> p a h d", a=2, d=DIM_A),
                           ps_qkv[0][:, 0:2 * P].rearrange(kv, a=2, d=DIM_A), ACT.Copy).then_inc(s.fold_w, 1)

            def copy_h(t, u4):
                u = u4 % 2
                done(act, s.ps_h, t)
                freed(act, s.ps_qkv, t)
                act.activation(h_t[:, u, :], ps_h[:, 0:P], ACT.Copy).then_inc(s.h_t, 1)

            def copy_qkv(t, u4):
                u = u4 % 2
                done(act, s.ps_qkv, t)
                freed(act, s.qk, t)
                act.activation(qk_raw[:, u, :], ps_qkv[u][:, 0:2 * P], ACT.Copy).then_inc(s.qk_raw, 1)
                freed(act, s.prod_pv, t, 4)
                act.activation(v[:, u4, :].rearrange("p (d h) -> p h d", d=DIM_A),
                               heads(ps_qkv[u][:, 2 * P:3 * P]), ACT.Copy).then_inc(s.v, 1)

            def exp(t, u4):
                u = u4 % 2
                done(act, s.shifted, t)
                freed(act, s.prod_pv, t)
                freed(act, s.total, t)
                act.activation(prob[:, u, :], shifted[:, u, :], ACT.Exp, scale=float(DIM_A) ** -0.5).then_inc(s.prob, 1)

            def copy_o(t, u4):
                u = u4 % 2
                done(act, s.ps_o, t)
                freed(act, s.ps_out, t)
                act.activation(o_t[:, u, :], ps_o[:, 0:P], ACT.Copy).then_inc(s.o_t, 1)

            pipeline(act, TILES, [(2, copy_h), (2, copy_qkv), (7, copy_o), (5, exp)], unroll=4)

        @block.gpsimd
        def _(pool):
            def rstd_in(t, u4):
                u = u4 % 2
                done(pool, s.veps, t)
                freed(pool, s.h, t)
                pool.tensor_tensor(rstd[:, u, :], veps[:, u, :], g.minus_half[:], ALU.pow).then_inc(s.rstd, 1)

            def rotate(t, u4):
                u = u4 % 2
                n = t % SEQ_TILES
                done(pool, s.qk_raw, t)
                freed(pool, s.qk, t)
                src = qk_raw[:, u, :].rearrange("p (g a d) -> p g a d", a=2, d=DIM_A // 2)
                cos = tab.rope_a[:, n, 0:DIM_A]
                sin = tab.rope_a[:, n, DIM_A:2 * DIM_A].rearrange("p (a d) -> p a d", a=2)
                pool.tensor_tensor(heads(turned_c[:, u, :]), heads(qk_raw[:, u, :]),
                                   over(cos, 1, 2 * HEADS_A), ALU.mult).then_inc(s.turn1, 1)
                dst = turned_s[:, u, :].rearrange("p (g a d) -> p g a d", a=2, d=DIM_A // 2)
                for a, sem in ((0, s.turn2), (1, s.turn3)):
                    pool.tensor_tensor(dst[:, :, a, :], src[:, :, 1 - a, :], over(sin[:, a, :], 1, 2 * HEADS_A),
                                       ALU.mult).then_inc(sem, 1)
                done(pool, s.turn1, t)
                done(pool, s.turn2, t)
                done(pool, s.turn3, t)
                freed(pool, s.prod_qk, t)
                pool.tensor_tensor(qk[:, u, :], turned_c[:, u, :], turned_s[:, u, :], ALU.add).then_inc(s.qk, 1)

            def shift(t, u4):
                u = u4 % 2
                done(pool, s.top, t)
                freed(pool, s.prob, t)
                by_head = "p (h g) -> p h g"
                pool.tensor_tensor(shifted[:, u, :].rearrange(by_head, h=HEADS_A),
                                   score[:, u, :].rearrange(by_head, h=HEADS_A),
                                   over(top[:, u, :], 2, HEADS_A), ALU.subtract).then_inc(s.shifted, 1)

            def mix(t, u4):
                u = u4 % 2
                done(pool, s.prob, t)
                done(pool, s.v, t)
                freed(pool, s.mixed, t)
                out = prod_pv[:, u, :].rearrange("p (h d g) -> p h d g", h=HEADS_A, g=HEADS_A)
                p = over(prob[:, u, :].rearrange("p (h g) -> p h g", h=HEADS_A), 2, DIM_A)
                vs = over(v[:, u4, :].rearrange("p (d g) -> p d g", d=DIM_A), 1, HEADS_A)
                pool.tensor_tensor(out, p, vs, ALU.mult).then_inc(s.prod_pv, 1)

            def rstd_out(t, u4):
                u = u4 % 2
                done(pool, s.veps2, t)
                freed(pool, s.y, t)
                pool.tensor_tensor(rstd2[:, u, :], veps2[:, u, :], g.minus_half[:], ALU.pow).then_inc(s.rstd2, 1)

            def residual(t, u4):
                u = u4 % 2
                done(pool, s.y, t)
                pool.tensor_tensor(g.x[:, t, :], g.x[:, t, :], y[:, u, :], ALU.add).then_inc(s.x, 1)

            pool.wait_ge(g.consts_ready, 1)
            pool.wait_ge(tab.loaded, 16)
            pipeline(pool, TILES, [(1, rstd_in), (9, rstd_out), (10, residual), (5, shift), (3, rotate), (5, mix)], unroll=4)

        @block.vector
        def _(dve):
            done(dve, s.fold, 0)
            dve.tensor_tensor(bias[:, P:].rearrange("p (a h d) -> p a h d", a=2, d=DIM_A),
                              ps_o[0:1, 0:2 * P].rearrange("p (h a d) -> p a h d", a=2, d=DIM_A),
                              w.bup[:].rearrange("p (h a d) -> p a h d", a=2, d=DIM_A), ALU.add).then_inc(s.fold_b, 1)

            def stats_in(t, u4):
                u = u4 % 2
                dve.bn_stats(stats[:, u, :], g.x[:, t, :]).then_inc(s.stats, 1)
                freed(dve, s.h, t, 4)
                done(dve, s.stats, t)

            def variance_in(t, u4):
                u = u4 % 2
                done(dve, s.mean_var, t)
                freed(dve, s.rstd, t)
                dve.tensor_scalar(veps[:, u, :], mean_var[:, u4, 1:2], EPS, None, ALU.add).then_inc(s.veps, 1)

            def aggregate_in(t, u4):
                u = u4 % 2
                dve.bn_aggr(mean_var[:, u4, :], stats[:, u, :]).then_inc(s.mean_var, 1)

            def normalize(t, u4):
                u = u4 % 2
                done(dve, s.rstd, t)
                freed(dve, s.ps_h, t)
                dve.tensor_scalar(h[:, u, :], g.x[:, t, :], mean_var[:, u4, 0:1], rstd[:, u, :],
                                  ALU.subtract, ALU.mult).then_inc(s.h, 1)

            def scores(t, u4):
                u = u4 % 2
                done(dve, s.qk, t)
                freed(dve, s.score, t)
                out = prod_qk[:, u, :].rearrange("p (h g d) -> p h g d", h=HEADS_A, d=DIM_A)
                q = over(heads(qk[:, u, 0:P]), 2, HEADS_A)
                k = over(heads(qk[:, u, P:]), 1, HEADS_A)
                dve.tensor_tensor(out, q, k, ALU.mult).then_inc(s.prod_qk, 1)
                done(dve, s.prod_qk, t)
                freed(dve, s.shifted, t)
                dve.tensor_reduce(score[:, u, :], prod_qk[:, u, :].rearrange("p (s d) -> p s d", d=DIM_A),
                                  AX_X, ALU.add).then_inc(s.score, 1)
                done(dve, s.score, t)
                dve.tensor_reduce(top[:, u, :], score[:, u, :].rearrange("p (h g) -> p h g", h=HEADS_A),
                                  AX_X, ALU.max).then_inc(s.top, 1)

            def totals(t, u4):
                u = u4 % 2
                done(dve, s.prob, t)
                dve.tensor_reduce(total[:, u, :], prob[:, u, :].rearrange("p (h g) -> p h g", h=HEADS_A),
                                  AX_X, ALU.add).then_inc(s.total, 1)
                done(dve, s.total, t)
                freed(dve, s.o, t)
                dve.reciprocal(inv[:, u, :], total[:, u, :]).then_inc(s.inv, 1)

            def gather(t, u4):
                u = u4 % 2
                done(dve, s.prod_pv, t)
                freed(dve, s.o, t)
                dve.tensor_reduce(mixed[:, u, :], prod_pv[:, u, :].rearrange("p (s g) -> p s g", g=HEADS_A),
                                  AX_X, ALU.add).then_inc(s.mixed, 1)
                done(dve, s.mixed, t)
                done(dve, s.inv, t)
                freed(dve, s.ps_o, t)
                dve.tensor_tensor(heads(o[:, u, :]), heads(mixed[:, u, :]), over(inv[:, u, :], 2, DIM_A),
                                  ALU.mult).then_inc(s.o, 1)

            def stats_out(t, u4):
                u = u4 % 2
                done(dve, s.ps_out, t)
                dve.bn_stats(stats2[:, u, :], ps_out[u4][:, 0:P]).then_inc(s.stats2, 1)
                freed(dve, s.y, t, 4)
                done(dve, s.stats2, t)

            def variance_out(t, u4):
                u = u4 % 2
                done(dve, s.mean_var2, t)
                freed(dve, s.rstd2, t)
                dve.tensor_scalar(veps2[:, u, :], mean_var2[:, u4, 1:2], EPS, None, ALU.add).then_inc(s.veps2, 1)

            def aggregate_out(t, u4):
                u = u4 % 2
                dve.bn_aggr(mean_var2[:, u4, :], stats2[:, u, :]).then_inc(s.mean_var2, 1)

            def normalize_out(t, u4):
                u = u4 % 2
                done(dve, s.rstd2, t)
                freed(dve, s.x, t)
                dve.tensor_scalar(y[:, u, :], ps_out[u4][:, 0:P], mean_var2[:, u4, 0:1], rstd2[:, u, :],
                                  ALU.subtract, ALU.mult).then_inc(s.y, 1)

            dve.wait_ge(g.x_loaded, 16 * BATCHES)
            pipeline(dve, TILES, [(0, stats_in), (1, variance_in), (0, aggregate_in), (2, normalize),
                                  (8, stats_out), (9, variance_out), (8, aggregate_out), (10, normalize_out),
                                  (6, totals), (6, gather), (4, scores)], unroll=4)


def normalize_all(nc, g, name, src, dst, add):
    with ExitStack() as ctx:
        def sb(n, shape):
            return ctx.enter_context(nc.sbuf_tensor(name + n, shape, F32))

        stats = sb("stats", [P, 4, 6])
        mean_var = sb("mean_var", [P, 4, 2])
        veps = sb("veps", [P, 4, 1])
        rstd = sb("rstd", [P, 4, 1])
        y = sb("y", [P, 4, P])
        s = sems(ctx, nc, name, "stats mean_var veps rstd y dst")
        block = ctx.enter_context(nc.Block())

        @block.gpsimd
        def _(pool):
            def inverse(t, u):
                done(pool, s.veps, t)
                freed(pool, s.y, t, 4)
                pool.tensor_tensor(rstd[:, u, :], veps[:, u, :], g.minus_half[:], ALU.pow).then_inc(s.rstd, 1)

            def residual(t, u):
                done(pool, s.y, t)
                pool.tensor_tensor(dst[:, t, :], dst[:, t, :], y[:, u, :], ALU.add).then_inc(s.dst, 1)

            pipeline(pool, TILES, [(1, inverse)] + [(3, residual)] * add, unroll=4)

        @block.vector
        def _(dve):
            def stats_of(t, u):
                dve.bn_stats(stats[:, u, :], src[:, t, :]).then_inc(s.stats, 1)
                freed(dve, s.y, t, 4)
                done(dve, s.stats, t)

            def variance(t, u):
                done(dve, s.mean_var, t)
                freed(dve, s.rstd, t, 4)
                dve.tensor_scalar(veps[:, u, :], mean_var[:, u, 1:2], EPS, None, ALU.add).then_inc(s.veps, 1)

            def aggregate(t, u):
                dve.bn_aggr(mean_var[:, u, :], stats[:, u, :]).then_inc(s.mean_var, 1)

            def normalize(t, u):
                done(dve, s.rstd, t)
                if add:
                    freed(dve, s.dst, t, 4)
                out = y[:, u, :] if add else dst[:, t, :]
                dve.tensor_scalar(out, src[:, t, :], mean_var[:, u, 0:1], rstd[:, u, :],
                                  ALU.subtract, ALU.mult).then_inc(s.y, 1)

            pipeline(dve, TILES, [(0, stats_of), (1, variance), (0, aggregate), (3, normalize)], unroll=4)


def l0_ffn(nc, g, w, tab):
    with ExitStack() as ctx:
        y = ctx.enter_context(nc.sbuf_tensor("b_y", [P, TILES, P], F32))
        normalize_all(nc, g, "b_in_", g.x, y, False)
        for layer in range(LAYERS):
            local_attention(nc, g, w, tab, layer, y)
            gated_ffn(nc, g, w, layer, y)
        normalize_all(nc, g, "b_out_", y, g.x, True)


def shifted_transpose(act, g, s, t, u, n, ps_y, h_t):
    act.activation(h_t[0:64, u, :], ps_y[0:64, 0:P], ACT.Copy)
    act.activation(h_t[64:P, u, 1:P], ps_y[64:P, 0:P - 1], ACT.Copy)
    act.activation(h_t[64:P, 1 - u, 0:1], ps_y[64:P, P - 1:P], ACT.Copy, scale=g.carry[64:P, bass.ds(n, 1)]) \
        .then_inc(s.h_t, 1)


def local_attention(nc, g, w, tab, layer, y):
    pre = f"l{layer}_"
    with ExitStack() as ctx:
        def sb(name, shape, dt=F32):
            return ctx.enter_context(nc.sbuf_tensor(pre + name, shape, dt))

        def pb(name, shape=(P, 512)):
            return ctx.enter_context(nc.psum_tensor(pre + name, list(shape), F32))

        w_qkv = w.wqkv_b[layer]
        w_rot = sb("w_rot", [P, 2 * INNER])
        rot = sb("rot", [P, 4, SEQ])
        y_now = sb("y_now", [P, 2, P])
        h_t = sb("h_t", [P, 2, P])
        by_cos = sb("by_cos", [P, 2, INNER])
        by_sin = sb("by_sin", [P, 2, INNER])
        square = sb("square", [P, 2, 2, INNER])
        q_t = sb("q_t", [P, 4, INNER])
        k_sum = sb("k_sum", [P, 4, INNER])
        k_t = sb("k_t", [P, 4, CHUNKS, KEYS_B])
        v = sb("v", [P, 4, INNER])
        v_before = sb("v_before", [WINDOW, 4, INNER])
        norm = sb("norm", [P, 2, 2 * HEADS_B])
        r_norm = sb("r_norm", [P, 4, 2 * HEADS_B])
        q_scale8 = sb("q_scale8", [P, 4, HEADS_B])
        rk_t = sb("rk_t", [HEADS_B, 2, P])
        top = sb("top", [P, 4, 2])
        neg_top = sb("neg_top", [P, 4, 2])
        prob = sb("prob", [P, 4, 2 * KEYS_B])
        total = sb("total", [P, 2, HEADS_B])
        inv = sb("inv", [P, 2, HEADS_B])
        prob_t = sb("prob_t", [P, 2, 512])
        o = sb("o", [P, 2, INNER])
        o_t = sb("o_t", [P, 2, INNER])
        ps_qk = pb("ps_qk", (P, 2 * INNER))
        ps_v = pb("ps_v")
        ps_s = [pb(f"ps_s{u}") for u in range(2)]
        ps_t = pb("ps_t")
        ps_o = pb("ps_o")
        ps_m = pb("ps_m")
        s = sems(ctx, nc, pre, "w_rot rot first y_now ps_y h_t ps_q ps_k square_q square_k cos_q sin_q cos_k sin_k q_t "
                 "k_sum k_t k_next ps_v v v_before ps_n norm r_norm q_scale8 ps_r rk_t ps_b ps_s top neg_top prob ps_t "
                 "prob_t ps_o inv o ps_ot o_t ps_w y")
        block = ctx.enter_context(nc.Block())
        GROUPS = HEADS_B // 2

        def head_of_group(c, hh):
            return 4 * (c // 2) + 2 * hh + c % 2

        def group(t, c):
            return t * GROUPS + c

        @block.tensor
        def _(pe):
            pe.wait_ge(s.w_rot, 4)
            pe.wait_ge(s.first, 3)

            def transpose_y(t, u4):
                done(pe, s.y_now, t)
                if isinstance(t, int) and t == 1:
                    done(pe, s.h_t, 0)
                elif isinstance(t, int) and 2 <= t < 5:
                    pe.wait_ge(s.rk_t, t - 1)
                freed(pe, s.y, t, 5)
                pe.transpose(ps_m[:, 0:P], y_now[:, u4 % 2, :], g.ident[:]).then_inc(s.ps_y, 1)

            def project_q(t, u4):
                done(pe, s.h_t, t)
                freed(pe, s.cos_k, t, 1)
                freed(pe, s.sin_k, t, 1)
                freed(pe, s.square_k, t, 1)
                project_pair(t, u4, 0, s.ps_q)

            def project_pair(t, u4, k, sem):
                for c in range(CHUNKS):
                    cols = slice(k * INNER + c * P, k * INNER + c * P + P)
                    pe.matmul(ps_qk[:, c * P:c * P + P], w_qkv[:, cols], h_t[:, u4 % 2, :], start=True, stop=True)
                    mm = pe.matmul(ps_qk[:, INNER + c * P:INNER + c * P + P], w_rot[:, cols], h_t[:, u4 % 2, :],
                                   start=True, stop=True)
                mm.then_inc(sem, 1)

            def project_k(t, u4):
                done(pe, s.cos_q, t)
                done(pe, s.sin_q, t)
                done(pe, s.square_q, t)
                project_pair(t, u4, 1, s.ps_k)

            def project_v(t, u4):
                freed(pe, s.k_t, t, 2)
                pe.matmul(ps_v[:], h_t[:, u4 % 2, :], w_qkv[:, 2 * INNER:3 * INNER], start=True, stop=True) \
                    .then_inc(s.ps_v, 1)

            def norms(t, u4):
                done(pe, s.square_k, t)
                if isinstance(t, int) and t + 1 == TILES:
                    freed(pe, s.y, t, 4)
                else:
                    done(pe, s.h_t, t + 1)
                for k in range(2):
                    for c in range(CHUNKS):
                        at = k * HEADS_B + 2 * c
                        mm = pe.matmul(ps_m[:, at:at + 2], square[:, u4 % 2, k, c * P:c * P + P], g.head_of[:],
                                       start=True, stop=True)
                mm.then_inc(s.ps_n, 1)

            def transpose_rk(t, u4):
                done(pe, s.r_norm, t)
                pe.transpose(ps_m[0:HEADS_B, 0:P], r_norm[:, u4, HEADS_B:], g.ident[:]).then_inc(s.ps_r, 1)

            def spread_rk(t, u4):
                done(pe, s.rk_t, t)
                if isinstance(t, int) and t + 1 == TILES:
                    freed(pe, s.k_t, t, 1)
                else:
                    done(pe, s.v_before, t + 1)
                for c in range(CHUNKS):
                    mm = pe.matmul(ps_v[:, c * P:c * P + P], g.spread[:, c, :], rk_t[:, u4 % 2, :], start=True, stop=True)
                mm.then_inc(s.ps_b, 1)

            def scores(t, u4, c):
                if c == 0:
                    done(pe, s.k_t, t)
                    freed(pe, s.k_next, t, 1)
                    done(pe, s.q_t, t)
                freed(pe, s.prob, group(t, c))
                out = ps_s[c % 2]
                mask = tab.mask_b[:, bass.ds((t % SEQ_TILES) * KEYS_B, KEYS_B)]
                for hh in range(2):
                    rows = slice((c % 2) * DIM_B, (c % 2 + 1) * DIM_B)
                    chunk = head_of_group(c, hh) // 2
                    pe.matmul(out[:, hh * KEYS_B:(hh + 1) * KEYS_B], g.ident_bf[:], mask, start=True, stop=False)
                    mm = pe.matmul(out[:, hh * KEYS_B:(hh + 1) * KEYS_B], q_t[rows, u4, chunk * P:chunk * P + P],
                                   k_t[rows, u4, chunk, :], start=False, stop=True)
                mm.then_inc(s.ps_s, 1)

            def transpose_p(t, u4, c):
                done(pe, s.prob, group(t, c))
                if c == 0:
                    freed(pe, s.o_t, t, 2)
                else:
                    done(pe, s.prob_t, group(t, c - 1))
                for hh in range(2):
                    p = prob[:, c, hh * KEYS_B:(hh + 1) * KEYS_B]
                    pe.transpose(ps_t[:, hh * 256:hh * 256 + P], p[:, WINDOW:], g.ident[:])
                    mm = pe.transpose(ps_t[:, hh * 256 + P:hh * 256 + 2 * P], p[:, 0:P], g.ident[:])
                mm.then_inc(s.ps_t, 1)

            def mix(t, u4, c):
                done(pe, s.prob_t, group(t, c))
                if c == 0:
                    freed(pe, s.o, t, 1)
                for hh in range(2):
                    cols = slice(head_of_group(c, hh) * DIM_B, (head_of_group(c, hh) + 1) * DIM_B)
                    p_t = prob_t[:, c % 2, hh * 256:hh * 256 + 256]
                    pe.matmul(ps_o[:, cols], p_t[:, 0:P], v[:, u4, cols], start=True, stop=False)
                    mm = pe.matmul(ps_o[:, cols], p_t[0:WINDOW, P:2 * P], v_before[:, u4, cols], start=False, stop=True)
                mm.then_inc(s.ps_o, 1)

            def transpose_o(t, u4):
                done(pe, s.o, t)
                if isinstance(t, int) and t + 1 == TILES:
                    freed(pe, s.o_t, t, 1)
                else:
                    done(pe, s.prob_t, group(t + 1, GROUPS - 1))
                for c in range(CHUNKS):
                    mm = pe.transpose(ps_t[:, c * P:c * P + P], o[:, u4 % 2, c * P:c * P + P], g.ident[:])
                mm.then_inc(s.ps_ot, 1)

            def project_out(t, u4):
                done(pe, s.o_t, t)
                if isinstance(t, int) and t + 3 >= TILES:
                    freed(pe, s.y, t, 1)
                if not isinstance(t, int) or t + 3 < TILES:
                    done(pe, s.rk_t, t + 3)
                for c in range(CHUNKS):
                    mm = pe.matmul(ps_m[:, 0:P], o_t[:, u4 % 2, c * P:c * P + P], w.wo_b[layer][:, c, :],
                                   start=(c == 0), stop=(c == CHUNKS - 1))
                mm.then_inc(s.ps_w, 1)

            def part(step, c):
                return lambda t, u4: step(t, u4, c)

            pipeline(pe, TILES, [
                (1, transpose_y), (4, part(scores, 0)), (1, project_q), (4, part(scores, 1)), (2, norms),
                (4, part(transpose_p, 0)), (4, part(scores, 2)), (1, project_k), (4, part(mix, 0)),
                (4, part(transpose_p, 1)), (4, part(scores, 3)), (2, transpose_rk), (3, spread_rk),
                (4, part(mix, 1)), (4, part(transpose_p, 2)), (1, project_v), (4, part(mix, 2)),
                (4, part(transpose_p, 3)), (4, part(mix, 3)), (5, transpose_o), (5, project_out)], unroll=4)

        @block.scalar
        def _(act):
            src = w_qkv[:, 0:2 * INNER].rearrange("p (g a d) -> p g a d", a=2, d=DIM_B // 2)
            dst = w_rot[:].rearrange("p (g a d) -> p g a d", a=2, d=DIM_B // 2)
            for half in range(2):
                for k in range(2):
                    heads = slice(k * HEADS_B, (k + 1) * HEADS_B)
                    act.activation(dst[:, heads, half, :], src[:, heads, 1 - half, :], ACT.Copy).then_inc(s.w_rot, 1)

            def copy_h(t, u4):
                done(act, s.ps_y, t)
                freed(act, s.ps_v, t, 1)
                shifted_transpose(act, g, s, t, u4 % 2, t % SEQ_TILES, ps_m, h_t)

            def square_q(t, u4):
                done(act, s.ps_q, t)
                freed(act, s.ps_n, t)
                act.activation(square[:, u4 % 2, 0, :], ps_qk[:, 0:INNER], ACT.Square).then_inc(s.square_q, 1)

            def square_k(t, u4):
                done(act, s.ps_k, t)
                act.activation(square[:, u4 % 2, 1, :], ps_qk[:, 0:INNER], ACT.Square).then_inc(s.square_k, 1)

            def copy_v(t, u4):
                done(act, s.ps_v, t)
                if not isinstance(t, int) or t >= 4:
                    act.wait_ge(s.ps_o, group(t, 0) - 12)
                act.activation(v[:, u4, :], ps_v[:], ACT.Copy).then_inc(s.v, 1)

            def copy_before(t, u4):
                if not isinstance(t, int) or t >= 3:
                    act.wait_ge(s.ps_o, group(t, 0) - 8)
                act.activation(v_before[:, (u4 + 1) % 4, :], ps_v[WINDOW:P, :], ACT.Copy).then_inc(s.v_before, 1)

            def copy_rk(t, u4):
                done(act, s.ps_r, t)
                freed(act, s.ps_b, t)
                act.activation(rk_t[:, u4 % 2, :], ps_m[0:HEADS_B, 0:P], ACT.Copy).then_inc(s.rk_t, 1)

            def exp(t, u4, c):
                done(act, s.neg_top, group(t, c))
                if c == 0:
                    freed(act, s.o, t)
                if not isinstance(t, int) or t >= 1:
                    act.wait_ge(s.ps_t, group(t, c) - 3)
                for hh in range(2):
                    head = head_of_group(c, hh)
                    e = act.activation(prob[:, c, hh * KEYS_B:(hh + 1) * KEYS_B],
                                       ps_s[c % 2][:, hh * KEYS_B:(hh + 1) * KEYS_B], ACT.Exp,
                                       bias=neg_top[:, c, hh:hh + 1], scale=q_scale8[:, u4, head:head + 1],
                                       accum_out=total[:, u4 % 2, head:head + 1])
                e.then_inc(s.prob, 1)

            def copy_p(t, u4, c):
                done(act, s.ps_t, group(t, c))
                if not isinstance(t, int) or t > 0 or c >= 2:
                    act.wait_ge(s.ps_o, group(t, c) - 1)
                act.activation(prob_t[:, c % 2, :], ps_t[:], ACT.Copy).then_inc(s.prob_t, 1)

            def copy_o(t, u4):
                done(act, s.ps_ot, t)
                freed(act, s.ps_w, t)
                act.activation(o_t[:, u4 % 2, :], ps_t[:], ACT.Copy).then_inc(s.o_t, 1)

            def part(step, c):
                return lambda t, u4: step(t, u4, c)

            pipeline(act, TILES, [
                (1, copy_h), (4, part(exp, 0)), (2, copy_before), (1, square_q), (4, part(exp, 1)), (4, part(copy_p, 0)),
                (4, part(exp, 2)), (1, square_k), (4, part(copy_p, 1)), (4, part(exp, 3)), (2, copy_rk),
                (4, part(copy_p, 2)), (1, copy_v), (4, part(copy_p, 3)), (5, copy_o)], unroll=4)

        @block.gpsimd
        def _(pool):
            pool.memset(h_t[64:P, 0, 0:1], 0.0).then_inc(s.first, 1)
            pool.wait_ge(s.first, 1)
            pool.memset(k_t[:, 0, :, 0:WINDOW], 0.0).then_inc(s.first, 1)
            pool.wait_ge(s.first, 2)
            pool.memset(v_before[:, 0, :], 0.0).then_inc(s.first, 1)

            def stage_y(t, u4):
                freed(pool, s.ps_y, t)
                pool.tensor_copy(y_now[:, u4 % 2, :], y[:, t, :]).then_inc(s.y_now, 1)

            def sum_q(t, u4):
                done(pool, s.cos_q, t)
                done(pool, s.sin_q, t)
                if not isinstance(t, int) or t >= 4:
                    pool.wait_ge(s.ps_s, group(t, 0) - 12)
                pool.tensor_tensor(q_t[:, u4, :], by_cos[:, 0, :], by_sin[:, 0, :], ALU.add).then_inc(s.q_t, 1)

            def sum_k(t, u4):
                done(pool, s.cos_k, t)
                done(pool, s.sin_k, t)
                freed(pool, s.k_t, t, 4)
                pool.tensor_tensor(k_sum[:, u4, :], by_cos[:, 1, :], by_sin[:, 1, :], ALU.add).then_inc(s.k_sum, 1)

            def inverse_norm(t, u4):
                done(pool, s.norm, t)
                freed(pool, s.q_scale8, t, 4)
                freed(pool, s.ps_r, t, 4)
                pool.tensor_tensor(r_norm[:, u4, :], norm[:, u4 % 2, :],
                                   g.minus_half[:].to_broadcast([P, 2 * HEADS_B]), ALU.pow).then_inc(s.r_norm, 1)

            pipeline(pool, TILES, [(0, stage_y), (1, sum_q), (2, inverse_norm), (1, sum_k)], unroll=4)

        @block.vector
        def _(dve):
            dve.wait_ge(w.b_loaded, w.b_count)
            for n in range(4):
                dve.tensor_scalar(rot[:, n, :], tab.rope_b[:, n, :], w.scales_b[:, layer, n:n + 1], None,
                                  ALU.mult).then_inc(s.rot, 1)
            dve.wait_ge(s.rot, 4)

            def rotate(t, u4, k, ps_sem, square_sem, cos_sem, sin_sem, read_sem):
                done(dve, ps_sem, t)
                freed(dve, read_sem, t, 1)
                for half, dst, sem in ((1, by_sin, sin_sem), (0, by_cos, cos_sem)):
                    if half == 0:
                        done(dve, square_sem, t)
                    table = rot[:, 2 * k + half, bass.ds((t % SEQ_TILES) * P, P)]
                    dve.tensor_tensor(dst[:, k, :].rearrange("p (c n) -> p c n", c=CHUNKS),
                                      ps_qk[:, half * INNER:(half + 1) * INNER].rearrange("p (c n) -> p c n", c=CHUNKS),
                                      over(table, 1, CHUNKS), ALU.mult).then_inc(sem, 1)

            def rotate_q(t, u4):
                rotate(t, u4, 0, s.ps_q, s.square_q, s.cos_q, s.sin_q, s.q_t)

            def rotate_k(t, u4):
                rotate(t, u4, 1, s.ps_k, s.square_k, s.cos_k, s.sin_k, s.k_sum)

            def clip_norm(t, u4):
                done(dve, s.ps_n, t)
                freed(dve, s.r_norm, t)
                dve.tensor_scalar(norm[:, u4 % 2, :], ps_m[:, 0:2 * HEADS_B], 1e-24, None, ALU.max).then_inc(s.norm, 1)

            def scale_q8(t, u4):
                done(dve, s.r_norm, t)
                if not isinstance(t, int) or t >= 4:
                    dve.wait_ge(s.prob, group(t, 0) - 12)
                dve.tensor_scalar(q_scale8[:, u4, :], r_norm[:, u4, 0:HEADS_B], 8.0, None, ALU.mult).then_inc(s.q_scale8, 1)

            def scale_k(t, u4):
                done(dve, s.ps_b, t)
                done(dve, s.k_sum, t)
                if not isinstance(t, int) or t >= 4:
                    dve.wait_ge(s.ps_s, group(t, 0) - 12)
                dve.tensor_tensor(k_t[:, u4, :, WINDOW:], k_sum[:, u4, :].rearrange("p (c n) -> p c n", c=CHUNKS),
                                  ps_v[:].rearrange("p (c n) -> p c n", c=CHUNKS), ALU.mult).then_inc(s.k_t, 1)

            def keys_before(t, u4):
                if not isinstance(t, int) or t >= 3:
                    dve.wait_ge(s.ps_s, group(t, 0) - 8)
                done(dve, s.k_t, t)
                dve.tensor_copy(k_t[:, (u4 + 1) % 4, :, 0:WINDOW], k_t[:, u4, :, P:P + WINDOW]).then_inc(s.k_next, 1)

            def tops(t, u4, c):
                done(dve, s.ps_s, group(t, c))
                if not isinstance(t, int) or t > 0:
                    dve.wait_ge(s.prob, group(t, c) - 3)
                dve.tensor_reduce(top[:, c, :], ps_s[c % 2][:, 0:2 * KEYS_B].rearrange("p (h n) -> p h n", h=2), AX_X,
                                  ALU.max).then_inc(s.top, 1)
                done(dve, s.top, group(t, c))
                dve.scalar_tensor_tensor(out=neg_top[:, c, :], in0=top[:, c, :], scalar=-1.0,
                                         in1=q_scale8[:, u4, head_of_group(c, 0):head_of_group(c, 1) + 1:2], op0=ALU.mult,
                                         op1=ALU.mult).then_inc(s.neg_top, 1)

            def scale_out(t, u4):
                done(dve, s.prob, group(t, GROUPS - 1))
                dve.reciprocal(inv[:, u4 % 2, :], total[:, u4 % 2, :]).then_inc(s.inv, 1)
                done(dve, s.ps_o, group(t, GROUPS - 1))
                done(dve, s.inv, t)
                freed(dve, s.ps_ot, t)
                dve.tensor_tensor(o[:, u4 % 2, :].rearrange("p (h d) -> p h d", d=DIM_B),
                                  ps_o[:].rearrange("p (h d) -> p h d", d=DIM_B),
                                  over(inv[:, u4 % 2, :], 2, DIM_B), ALU.mult).then_inc(s.o, 1)

            def residual(t, u4):
                done(dve, s.ps_w, t)
                dve.tensor_tensor(y[:, t, :], y[:, t, :], ps_m[:, 0:P], ALU.add).then_inc(s.y, 1)

            def part(step, c):
                return lambda t, u4: step(t, u4, c)

            pipeline(dve, TILES, [
                (4, part(tops, 0)), (1, rotate_q), (4, part(tops, 1)), (2, clip_norm), (4, part(tops, 2)),
                (2, scale_q8), (1, rotate_k), (4, part(tops, 3)), (3, scale_k), (3, keys_before), (4, scale_out), (5, residual)], unroll=4)


def gated_ffn(nc, g, w, layer, y):
    pre = f"f{layer}_"
    PAD = 3 * P
    with ExitStack() as ctx:
        def sb(name, shape, dt=F32):
            return ctx.enter_context(nc.sbuf_tensor(pre + name, shape, dt))

        def pb(name, shape=(P, 512)):
            return ctx.enter_context(nc.psum_tensor(pre + name, list(shape), F32))

        w1 = w.w1_b[layer]
        w1_g = sb("w1_g", [P, 2 * HID_B])
        beta = sb("beta", [P, P])
        offset = sb("offset", [P, 2 * HID_B])
        y_now = sb("y_now", [P, 2, P])
        h_t = sb("h_t", [P, 2, P])
        centred = sb("centred", [P, 4, P])
        square = sb("square", [P, 2, P])
        veps = sb("veps", [P, 2, 1])
        rstd = sb("rstd", [P, 2, 1])
        gate = sb("gate", [P, 2, HID_B])
        gelu = sb("gelu", [P, 2, HID_B])
        linear = sb("linear", [P, 2, HID_B])
        hidden = sb("hidden", [P, 2, PAD])
        hidden_t = sb("hidden_t", [P, 2, PAD])
        ps_y = pb("ps_y")
        ps_c = pb("ps_c")
        ps_n = pb("ps_n")
        ps_a = pb("ps_a")
        ps_g = pb("ps_g")
        ps_t = pb("ps_t")
        ps_o = [pb(f"ps_o{u}") for u in range(2)]
        s = sems(ctx, nc, pre, "w1_g beta offset ps_off first y_now ps_y h_t ps_c centred square ps_n veps rstd ps_a ps_g "
                 "gate linear gelu hidden ps_t hidden_t ps_o y")
        block = ctx.enter_context(nc.Block())

        @block.tensor
        def _(pe):
            pe.wait_ge(s.beta, 1)
            for ps, cols in ((ps_a, slice(0, HID_B)), (ps_g, slice(HID_B, 2 * HID_B))):
                pe.matmul(ps[:, 0:HID_B], beta[:], w1[:, cols], start=True, stop=False)
                mm = pe.matmul(ps[:, 0:HID_B], g.ones_row[:], w.b1_b[:, layer, cols], start=False, stop=True)
            mm.then_inc(s.ps_off, 1)
            pe.wait_ge(s.offset, 2)
            pe.wait_ge(s.first, 2)

            def transpose_y(t, u4):
                done(pe, s.y_now, t)
                freed(pe, s.h_t, t, 1)
                pe.transpose(ps_y[:, 0:P], y_now[:, u4 % 2, :], g.ident[:]).then_inc(s.ps_y, 1)

            def centre(t, u4):
                done(pe, s.h_t, t)
                freed(pe, s.square, t, 1)
                pe.matmul(ps_c[:, 0:P], g.centre[:], h_t[:, u4 % 2, :], start=True, stop=True).then_inc(s.ps_c, 1)

            def variance(t, u4):
                done(pe, s.square, t)
                freed(pe, s.veps, t, 1)
                pe.matmul(ps_n[:, 0:1], square[:, u4 % 2, :], g.mean_col[:], start=True, stop=True).then_inc(s.ps_n, 1)

            def expand(t, u4):
                done(pe, s.centred, t)
                freed(pe, s.gate, t, 1)
                pe.matmul(ps_g[:, 0:HID_B], centred[:, u4, :], w1_g[:, HID_B:], start=True, stop=True).then_inc(s.ps_g, 1)
                freed(pe, s.linear, t, 1)
                pe.matmul(ps_a[:, 0:HID_B], centred[:, u4, :], w1_g[:, 0:HID_B], start=True, stop=True).then_inc(s.ps_a, 1)

            def transpose_hidden(t, u4):
                done(pe, s.hidden, t)
                freed(pe, s.hidden_t, t, 1)
                for c in range(3):
                    mm = pe.transpose(ps_t[:, c * P:c * P + P], hidden[:, u4 % 2, c * P:c * P + P], g.ident[:])
                mm.then_inc(s.ps_t, 1)

            def contract(t, u4):
                done(pe, s.hidden_t, t)
                freed(pe, s.y, t)
                for c in range(3):
                    pe.matmul(ps_o[u4 % 2][:, 0:P], hidden_t[:, u4 % 2, c * P:c * P + P], w.w2_b[layer][:, c, :],
                              start=(c == 0), stop=False)
                pe.matmul(ps_o[u4 % 2][:, 0:P], g.ones_row[:], w.b2_b[:, layer, :], start=False, stop=True) \
                    .then_inc(s.ps_o, 1)

            pipeline(pe, TILES, [(1, transpose_y), (5, transpose_hidden), (2, variance), (3, expand), (1, centre),
                                 (5, contract)], unroll=4)

        @block.scalar
        def _(act):
            done(act, s.ps_off, 0)
            act.activation(offset[:, 0:HID_B], ps_a[:, 0:HID_B], ACT.Copy).then_inc(s.offset, 1)
            act.activation(offset[:, HID_B:], ps_g[:, 0:HID_B], ACT.Copy).then_inc(s.offset, 1)

            def copy_h(t, u4):
                done(act, s.ps_y, t)
                freed(act, s.ps_c, t, 1)
                shifted_transpose(act, g, s, t, u4 % 2, t % SEQ_TILES, ps_y, h_t)

            def copy_centred(t, u4):
                done(act, s.ps_c, t)
                freed(act, s.ps_a, t, 4)
                act.activation(centred[:, u4, :], ps_c[:, 0:P], ACT.Copy).then_inc(s.centred, 1)
                freed(act, s.ps_n, t)
                act.activation(square[:, u4 % 2, :], ps_c[:, 0:P], ACT.Square).then_inc(s.square, 1)

            def gelu_of(t, u4):
                done(act, s.gate, t)
                freed(act, s.hidden, t)
                act.activation(gelu[:, u4 % 2, :], gate[:, u4 % 2, :], ACT.Gelu).then_inc(s.gelu, 1)

            def copy_hidden(t, u4):
                done(act, s.ps_t, t)
                freed(act, s.ps_o, t)
                act.activation(hidden_t[:, u4 % 2, :], ps_t[:, 0:PAD], ACT.Copy).then_inc(s.hidden_t, 1)

            pipeline(act, TILES, [(1, copy_h), (5, copy_hidden), (4, gelu_of), (1, copy_centred)], unroll=4)

        @block.gpsimd
        def _(pool):
            pool.memset(h_t[64:P, 0, 0:1], 0.0).then_inc(s.first, 1)
            pool.wait_ge(s.first, 1)
            pool.memset(hidden[:], 0.0).then_inc(s.first, 1)
            pool.wait_ge(s.first, 2)

            def stage_y(t, u4):
                freed(pool, s.ps_y, t)
                pool.tensor_copy(y_now[:, u4 % 2, :], y[:, t, :]).then_inc(s.y_now, 1)

            def inverse(t, u4):
                done(pool, s.veps, t)
                freed(pool, s.linear, t)
                pool.tensor_tensor(rstd[:, u4 % 2, :], veps[:, u4 % 2, :], g.minus_half[:], ALU.pow).then_inc(s.rstd, 1)

            def gated(t, u4):
                done(pool, s.gelu, t)
                done(pool, s.linear, t)
                freed(pool, s.ps_t, t)
                pool.tensor_tensor(hidden[:, u4 % 2, 0:HID_B], linear[:, u4 % 2, :], gelu[:, u4 % 2, :], ALU.mult) \
                    .then_inc(s.hidden, 1)

            pipeline(pool, TILES, [(0, stage_y), (2, inverse), (4, gated)], unroll=4)

        @block.vector
        def _(dve):
            dve.wait_ge(w.b_loaded, w.b_count)
            dve.tensor_scalar(w1_g[:], w1[:], w.ln_b[:, layer, 0:1], None, ALU.mult).then_inc(s.w1_g, 1)
            dve.tensor_scalar(beta[:], g.zeros[:], w.ln_b[:, layer, 1:2], None, ALU.add).then_inc(s.beta, 1)
            dve.wait_ge(s.w1_g, 1)
            dve.wait_ge(s.offset, 2)

            def add_eps(t, u4):
                done(dve, s.ps_n, t)
                freed(dve, s.rstd, t)
                dve.tensor_scalar(veps[:, u4 % 2, :], ps_n[:, 0:1], EPS, None, ALU.add).then_inc(s.veps, 1)

            def scale_hidden(t, u4):
                done(dve, s.rstd, t)
                done(dve, s.ps_g, t)
                freed(dve, s.gelu, t)
                dve.scalar_tensor_tensor(out=gate[:, u4 % 2, :], in0=ps_g[:, 0:HID_B], scalar=rstd[:, u4 % 2, :],
                                         in1=offset[:, HID_B:], op0=ALU.mult, op1=ALU.add).then_inc(s.gate, 1)
                done(dve, s.ps_a, t)
                freed(dve, s.hidden, t)
                dve.scalar_tensor_tensor(out=linear[:, u4 % 2, :], in0=ps_a[:, 0:HID_B], scalar=rstd[:, u4 % 2, :],
                                         in1=offset[:, 0:HID_B], op0=ALU.mult, op1=ALU.add).then_inc(s.linear, 1)

            def residual(t, u4):
                done(dve, s.ps_o, t)
                dve.tensor_tensor(y[:, t, :], y[:, t, :], ps_o[u4 % 2][:, 0:P], ALU.add).then_inc(s.y, 1)

            pipeline(dve, TILES, [(6, residual), (2, add_eps), (3, scale_hidden)], unroll=4)


def l1_attention(nc, g, w):
    with ExitStack() as outer:
        def keep(name, shape, dt=F32):
            return outer.enter_context(nc.sbuf_tensor("c_" + name, shape, dt))

        xn = keep("xn", [P, TILES, P])
        vo = keep("vo", [P, BATCHES * CHUNKS + 1, SEQ_TILES, P])
        with ExitStack() as mid:
            h_all = mid.enter_context(nc.sbuf_tensor("c_h_all", [P, TOKENS], F32))
            l1_attention_values(nc, g, w, xn, h_all, vo)
            l1_attention_heads(nc, g, w, h_all, vo)
        l1_attention_out(nc, g, w, xn, vo)


def l1_attention_values(nc, g, w, xn, h_all, vo):
    with ExitStack() as ctx:
        def sb(name, shape, dt=F32):
            return ctx.enter_context(nc.sbuf_tensor("cv_" + name, shape, dt))

        stats = sb("stats", [P, 2, 6])
        mean_var = sb("mean_var", [P, 4, 2])
        veps = sb("veps", [P, 2, 1])
        rstd = sb("rstd", [P, 2, 1])
        stage = sb("stage", [P, 2, P])
        h_t = sb("h_t", [P, 2, P])
        ps_h = [ctx.enter_context(nc.psum_tensor(f"cv_ps_h{u}", [P, 512], F32)) for u in range(2)]
        ps_v = [ctx.enter_context(nc.psum_tensor(f"cv_ps_v{u}", [P, 512], F32)) for u in range(2)]
        s = sems(ctx, nc, "cv_", "stats mean_var veps rstd xn kept ps_h h_t h_all ps_v v")
        block = ctx.enter_context(nc.Block())

        @block.tensor
        def _(pe):
            pe.wait_ge(w.c_loaded, w.c_count)

            def project(t, u4):
                u = u4 % 2
                done(pe, s.h_t, t)
                freed(pe, s.v, t)
                pe.matmul(ps_v[u][:], h_t[:, u, :], w.wv_c[:], start=True, stop=False)
                pe.matmul(ps_v[u][:], g.ones_row[:], w.bv_c[:], start=False, stop=True).then_inc(s.ps_v, 1)

            def transpose_in(t, u4):
                u = u4 % 2
                done(pe, s.xn, t)
                freed(pe, s.h_t, t)
                pe.transpose(ps_h[u][:, 0:P], stage[:, u, :], g.ident[:]).then_inc(s.ps_h, 1)

            pipeline(pe, TILES, [(2, transpose_in), (2, project)], unroll=4)

        @block.scalar
        def _(act):
            def copy_h(t, u4):
                u = u4 % 2
                done(act, s.ps_h, t)
                freed(act, s.ps_v, t)
                freed(act, s.h_all, t)
                act.activation(h_t[:, u, :], ps_h[u][:, 0:P], ACT.Copy).then_inc(s.h_t, 1)

            def copy_v(t, u4):
                u = u4 % 2
                done(act, s.ps_v, t)
                slot = (t // SEQ_TILES) * CHUNKS + 1
                act.activation(vo[:, bass.ds(slot, CHUNKS), bass.ds(t % SEQ_TILES, 1), :].rearrange("p c a n -> p c (a n)"),
                               ps_v[u][:].rearrange("p (c n) -> p c n", c=CHUNKS), ACT.Copy).then_inc(s.v, 1)

            pipeline(act, TILES, [(2, copy_h), (3, copy_v)], unroll=4)

        @block.gpsimd
        def _(pool):
            def rstd_in(t, u4):
                u = u4 % 2
                done(pool, s.veps, t)
                freed(pool, s.xn, t)
                pool.tensor_tensor(rstd[:, u, :], veps[:, u, :], g.minus_half[:], ALU.pow).then_inc(s.rstd, 1)

            def keep_xn(t, u4):
                done(pool, s.xn, t)
                pool.tensor_copy(xn[:, t, :], stage[:, u4 % 2, :]).then_inc(s.kept, 1)

            def keep_h(t, u4):
                done(pool, s.h_t, t)
                pool.tensor_copy(h_all[:, bass.ts(t, P)], h_t[:, u4 % 2, :]).then_inc(s.h_all, 1)

            pipeline(pool, TILES, [(1, rstd_in), (3, keep_h), (2, keep_xn)], unroll=4)

        @block.vector
        def _(dve):
            def stats_in(t, u4):
                u = u4 % 2
                dve.bn_stats(stats[:, u, :], g.x[:, t, :]).then_inc(s.stats, 1)
                freed(dve, s.xn, t, 4)
                done(dve, s.stats, t)

            def variance_in(t, u4):
                u = u4 % 2
                done(dve, s.mean_var, t)
                freed(dve, s.rstd, t)
                dve.tensor_scalar(veps[:, u, :], mean_var[:, u4, 1:2], EPS, None, ALU.add).then_inc(s.veps, 1)

            def aggregate_in(t, u4):
                dve.bn_aggr(mean_var[:, u4, :], stats[:, u4 % 2, :]).then_inc(s.mean_var, 1)

            def normalize(t, u4):
                u = u4 % 2
                done(dve, s.rstd, t)
                freed(dve, s.ps_h, t)
                freed(dve, s.kept, t)
                dve.tensor_scalar(stage[:, u, :], g.x[:, t, :], mean_var[:, u4, 0:1], rstd[:, u, :],
                                  ALU.subtract, ALU.mult).then_inc(s.xn, 1)

            pipeline(dve, TILES, [(0, stats_in), (1, variance_in), (0, aggregate_in), (2, normalize)],
                     unroll=4)


PAIR_STEPS = 2 * SEQ_TILES
STEPS_C = BATCHES * (HEADS_C // 2) * PAIR_STEPS


def l1_attention_heads(nc, g, w, h_all, vo):
    F32R = mybir.dt.float32r
    with ExitStack() as ctx:
        def sb(name, shape, dt=F32):
            return ctx.enter_context(nc.sbuf_tensor("ch_" + name, shape, dt))

        def pb(name, shape):
            return ctx.enter_context(nc.psum_tensor("ch_" + name, shape, F32))

        w_sorted = sb("w_sorted", [P, 2, INNER])
        w_now = sb("w_now", [P, 2, P])
        q_hl = sb("q_hl", [P, 2, 2, SEQ], F32R)
        k_h = sb("k_h", [P, 2, 2, SEQ], F32R)
        k_l = sb("k_l", [P, 2, 2, SEQ], F32R)
        low = sb("low", [P, 512])
        q_now = sb("q_now", [P, 2, P], F32R)
        neg_top = sb("neg_top", [P, 4, 1])
        prob = sb("prob", [P, 2, SEQ])
        total = sb("total", [P, 4, 1])
        inv = sb("inv", [P, 4, 1])
        prob_t = sb("prob_t", [P, 2, SEQ_TILES, P])
        ps_s = [pb(f"ps_s{u}", [P, SEQ]) for u in range(2)]
        ps_t = [pb(f"ps_t{u}", [P, 512]) for u in range(2)]
        ps_o = pb("ps_o", [P, 512])
        ps_p = pb("ps_p", [P, 512])
        s = sems(ctx, nc, "ch_", "w_sorted w_now ps_p hi lo whole q_now ps_s neg_top prob total ps_ta ps_tb pt_a pt_b ps_o inv o")
        block = ctx.enter_context(nc.Block())

        def job(t):
            return t // 2

        def job_place(t):
            return t // PAIR_STEPS, (t % 8) // 4, (t % PAIR_STEPS) // 8

        def scaled_bias(t, k):
            pair = (t // PAIR_STEPS) % (HEADS_C // 2)
            head = pair * 2 + (t % 8) // 4
            return w.bias_c[:, k, bass.ds(head, 1)]

        @block.tensor
        def _(pe):
            def project(t, u):
                if u % 2:
                    return
                done(pe, s.w_now, job(t))
                freed(pe, s.lo, job(t), 1)
                pair, _, half = job_place(t)
                cols = (pair // (HEADS_C // 2)) * SEQ + half * 512
                pe.matmul(ps_p[:], w_now[:, u // 2, :], h_all[:, bass.ds(cols, 512)], start=True, stop=True) \
                    .then_inc(s.ps_p, 1)

            def scores(t, u):
                hh = u % 2
                pair = t // PAIR_STEPS
                if hh == 0:
                    pe.wait_ge(s.lo, (pair + 1) * 8)
                done(pe, s.q_now, t)
                freed(pe, s.prob, t)
                for half in range(2):
                    out = ps_s[hh][:, half * 512:half * 512 + 512]
                    cols = (pair % 2) * 2 * SEQ + hh * SEQ + half * 512
                    for part, (k, start) in enumerate(((k_h, True), (k_l, False))):
                        flat = k[:].rearrange("p a b n -> p (a b n)")
                        mm = pe.matmul(out, q_now[:, hh, :], flat[:, bass.ds(cols, 512)], start=start, stop=not start)
                mm.then_inc(s.ps_s, 1)

            def transposes(t, u):
                done(pe, s.prob, t)
                for half, free, sem in ((0, s.pt_a, s.ps_ta), (1, s.pt_b, s.ps_tb)):
                    freed(pe, free, t, 1)
                    for j in range(4):
                        c = half * 4 + j
                        mm = pe.transpose(ps_t[half][:, j * P:(j + 1) * P], prob[:, u % 2, c * P:(c + 1) * P], g.ident[:])
                    mm.then_inc(sem, 1)

            def mix(t, u):
                freed(pe, s.o, t, 1)
                done(pe, s.pt_a, t)
                pair = t // PAIR_STEPS
                flat = vo[:].rearrange("p c t n -> p (c t n)")
                base = (pair + 1) * (SEQ_TILES * P) + (u % 2) * DIM_C
                for j in range(SEQ_TILES):
                    if j == 4:
                        done(pe, s.pt_b, t)
                    mm = pe.matmul(ps_o[:, 0:DIM_C], prob_t[:, u % 2, j, :], flat[:, bass.ds(base + j * P, DIM_C)],
                                   start=(j == 0), stop=(j == SEQ_TILES - 1))
                mm.then_inc(s.ps_o, 1)

            pipeline(pe, STEPS_C, [(1, project), (17, scores), (20, mix), (19, transposes)], unroll=4)

        @block.scalar
        def _(act):
            def split_high(t, u):
                if u % 2:
                    return
                done(act, s.ps_p, job(t))
                pair, head, half = job_place(t)
                if not isinstance(t, int) or pair >= 1:
                    act.wait_ge(s.ps_s, (t - PAIR_STEPS) // PAIR_STEPS * PAIR_STEPS + 1)
                dst = (q_hl, k_h)[u // 2][:].rearrange("p a b n -> p (a b n)")
                cols = (pair % 2) * 2 * SEQ + head * SEQ + half * 512
                scale = (float(DIM_C) ** -0.5, 1.0)[u // 2]
                act.activation(dst[:, bass.ds(cols, 512)], ps_p[:], ACT.Identity, bias=scaled_bias(t, u // 2),
                               scale=scale).then_inc(s.hi, 1)

            def exp(t, u):
                done(act, s.neg_top, t)
                if not isinstance(t, int) or t >= 2:
                    act.wait_ge(s.ps_tb, t - 1)
                freed(act, s.inv, t, 4)
                act.activation(prob[:, u % 2, :], ps_s[u % 2][:], ACT.Exp, bias=neg_top[:, u, :],
                               accum_out=total[:, u, :]).then_inc(s.prob, 1)

            def copy_a(t, u):
                done(act, s.ps_ta, t)
                freed(act, s.ps_o, t)
                act.activation(prob_t[:, u % 2, 0:4, :].rearrange("p j n -> p (j n)"), ps_t[0][:], ACT.Copy) \
                    .then_inc(s.pt_a, 1)

            pipeline(act, STEPS_C, [(2, split_high), (19, copy_a), (17, exp)], unroll=4)

        @block.gpsimd
        def _(pool):
            pool.wait_ge(s.w_sorted, 2)

            def stage_weights(t, u):
                if u % 2:
                    return
                if not isinstance(t, int) or t >= 4:
                    pool.wait_ge(s.ps_p, job(t - 2))
                pair = (t // PAIR_STEPS) % (HEADS_C // 2)
                cols = (pair * 2 + (t % 8) // 4) * DIM_C
                pool.tensor_copy(w_now[:, u // 2, :].rearrange("p (a d) -> p a d", a=2),
                                 over(w_sorted[:, u // 2, bass.ds(cols, DIM_C)], 1, 2)).then_inc(s.w_now, 1)

            def stage_q(t, u):
                hh = u % 2
                pair = t // PAIR_STEPS
                if hh == 0:
                    pool.wait_ge(s.lo, (pair + 1) * 8)
                freed(pool, s.ps_s, t)
                flat = q_hl[:].rearrange("p a b n -> p (a b n)")
                cols = (pair % 2) * 2 * SEQ + hh * SEQ + ((t % PAIR_STEPS) // 2) * P
                pool.tensor_copy(q_now[:, hh, :], flat[:, bass.ds(cols, P)]).then_inc(s.q_now, 1)

            pipeline(pool, STEPS_C, [(0, stage_weights), (17, stage_q)], unroll=4)

        @block.vector
        def _(dve):
            dve.wait_ge(w.c_loaded, w.c_count)
            src = w.wqk_c[:].rearrange("p (n k) -> p k n", k=2)
            for k in range(2):
                dve.tensor_copy(w_sorted[:, k, :], src[:, k, :]).then_inc(s.w_sorted, 1)

            def split_low(t, u):
                if u % 2:
                    return
                done(dve, s.hi, job(t))
                pair, head, half = job_place(t)
                cols = (pair % 2) * 2 * SEQ + head * SEQ + half * 512
                if u // 2 == 0:
                    here = q_hl[64:P].rearrange("p a b n -> p (a b n)")[:, bass.ds(cols, 512)]
                    dve.tensor_scalar(low[64:P, :], ps_p[64:P, :], float(DIM_C) ** -0.5, scaled_bias(t, 0)[64:P],
                                      ALU.mult, ALU.add).then_inc(s.whole, 1)
                    done(dve, s.whole, job(t) // 2)
                    dve.tensor_tensor(here, low[64:P, :], here.bitcast(F32), ALU.subtract).then_inc(s.lo, 1)
                else:
                    high = k_h[:].rearrange("p a b n -> p (a b n)")[:, bass.ds(cols, 512)]
                    dst = k_l[:].rearrange("p a b n -> p (a b n)")[:, bass.ds(cols, 512)]
                    dve.scalar_tensor_tensor(out=dst, in0=ps_p[:], scalar=scaled_bias(t, 1), in1=high.bitcast(F32),
                                             op0=ALU.add, op1=ALU.subtract).then_inc(s.lo, 1)

            def top(t, u):
                done(dve, s.ps_s, t)
                freed(dve, s.prob, t, 4)
                dve.tensor_reduce(neg_top[:, u, :], ps_s[u % 2][:], AX_X, ALU.max, negate=True).then_inc(s.neg_top, 1)

            def copy_b(t, u):
                done(dve, s.ps_tb, t)
                freed(dve, s.ps_o, t)
                dve.tensor_copy(prob_t[:, u % 2, 4:8, :].rearrange("p j n -> p (j n)"), ps_t[1][:]).then_inc(s.pt_b, 1)

            def inverse(t, u):
                done(dve, s.prob, t)
                freed(dve, s.o, t, 4)
                dve.reciprocal(inv[:, u, :], total[:, u, :]).then_inc(s.inv, 1)

            def scale_out(t, u):
                done(dve, s.ps_o, t)
                done(dve, s.inv, t)
                pair = t // PAIR_STEPS
                flat = vo[:].rearrange("p c t n -> p (c t n)")
                base = pair * (SEQ_TILES * P) + ((t % PAIR_STEPS) // 2) * P + (u % 2) * DIM_C
                dve.tensor_scalar(flat[:, bass.ds(base, DIM_C)], ps_o[:, 0:DIM_C], inv[:, u, :], None,
                                  ALU.mult).then_inc(s.o, 1)

            pipeline(dve, STEPS_C, [(17, top), (2, split_low), (20, scale_out), (19, copy_b), (18, inverse)],
                     unroll=4)

RSQRT2 = 2 ** -0.5


def l1_attention_out(nc, g, w, xn, vo):
    with ExitStack() as ctx:
        def sb(name, shape, dt=F32):
            return ctx.enter_context(nc.sbuf_tensor("co_" + name, shape, dt))

        def pb(name):
            return ctx.enter_context(nc.psum_tensor("co_" + name, [P, 512], F32))

        o_now = sb("o_now", [P, 2, INNER])
        o_t = sb("o_t", [P, 2, INNER])
        gamma = sb("gamma", [P, P])
        beta = sb("beta", [P, P])
        stats = sb("stats", [P, 2, 6])
        mean_var = sb("mean_var", [P, 4, 2])
        veps = sb("veps", [P, 2, 1])
        rstd = sb("rstd", [P, 2, 1])
        y = sb("y", [P, 2, P])
        scaled = sb("scaled", [P, 2, P])
        base = sb("base", [P, 2, P])
        z = sb("z", [P, 4, P])
        stats2 = sb("stats2", [P, 2, 6])
        mean_var2 = sb("mean_var2", [P, 4, 2])
        veps2 = sb("veps2", [P, 2, 1])
        rstd2 = sb("rstd2", [P, 2, 1])
        r = sb("r", [P, 2, P])
        ps_t = [pb(f"ps_t{u}") for u in range(2)]
        ps_y = [pb(f"ps_y{u}") for u in range(4)]
        s = sems(ctx, nc, "co_", "gamma beta o_now ps_t o_t ps_y stats mean_var veps rstd y scaled base z stats2 "
                 "mean_var2 veps2 rstd2 r x")
        block = ctx.enter_context(nc.Block())

        @block.tensor
        def _(pe):
            def transpose_o(t, u4):
                u = u4 % 2
                done(pe, s.o_now, t)
                freed(pe, s.o_t, t)
                for c in range(CHUNKS):
                    mm = pe.transpose(ps_t[u][:, c * P:(c + 1) * P], o_now[:, u, c * P:(c + 1) * P], g.ident[:])
                mm.then_inc(s.ps_t, 1)

            def project(t, u4):
                u = u4 % 2
                done(pe, s.o_t, t)
                freed(pe, s.y, t, 4)
                for c in range(CHUNKS):
                    pe.matmul(ps_y[u4][:, 0:P], o_t[:, u, c * P:(c + 1) * P], w.wout_c[:, c, :], start=(c == 0), stop=False)
                pe.matmul(ps_y[u4][:, 0:P], g.ones_row[:], w.bout_c[:], start=False, stop=True).then_inc(s.ps_y, 1)

            pipeline(pe, TILES, [(1, transpose_o), (2, project)], unroll=4)

        @block.scalar
        def _(act):
            def stage_o(t, u4):
                u = u4 % 2
                freed(act, s.ps_t, t)
                slot = (t // SEQ_TILES) * CHUNKS
                src = vo[:, bass.ds(slot, CHUNKS), bass.ds(t % SEQ_TILES, 1), :]
                act.activation(o_now[:, u, :].rearrange("p (c n) -> p c n", c=CHUNKS),
                               src.rearrange("p c a n -> p c (a n)"), ACT.Copy).then_inc(s.o_now, 1)

            def copy_o(t, u4):
                u = u4 % 2
                done(act, s.ps_t, t)
                freed(act, s.ps_y, t)
                act.activation(o_t[:, u, :], ps_t[u][:], ACT.Copy).then_inc(s.o_t, 1)

            pipeline(act, TILES, [(0, stage_o), (1, copy_o)], unroll=4)

        @block.gpsimd
        def _(pool):
            def rstd_y(t, u4):
                u = u4 % 2
                done(pool, s.veps, t)
                freed(pool, s.y, t)
                pool.tensor_tensor(rstd[:, u, :], veps[:, u, :], g.minus_half[:], ALU.pow).then_inc(s.rstd, 1)

            def affine(t, u4):
                u = u4 % 2
                done(pool, s.y, t)
                pool.tensor_tensor(scaled[:, u, :], y[:, u, :], gamma[:], ALU.mult).then_inc(s.scaled, 1)
                done(pool, s.scaled, t)
                done(pool, s.base, t)
                freed(pool, s.r, t, 4)
                pool.tensor_tensor(z[:, u4, :], scaled[:, u, :], base[:, u, :], ALU.add).then_inc(s.z, 1)

            def rstd_z(t, u4):
                u = u4 % 2
                done(pool, s.veps2, t)
                freed(pool, s.r, t)
                pool.tensor_tensor(rstd2[:, u, :], veps2[:, u, :], g.minus_half[:], ALU.pow).then_inc(s.rstd2, 1)

            def residual(t, u4):
                done(pool, s.r, t)
                pool.tensor_tensor(g.x[:, t, :], g.x[:, t, :], r[:, u4 % 2, :], ALU.add).then_inc(s.x, 1)

            pipeline(pool, TILES, [(4, rstd_y), (7, rstd_z), (5, affine), (8, residual)], unroll=4)

        @block.vector
        def _(dve):
            dve.tensor_scalar(gamma[:], w.gamma_c[:], RSQRT2, None, ALU.mult).then_inc(s.gamma, 1)
            dve.tensor_scalar(beta[:], w.beta_c[:], RSQRT2, None, ALU.mult).then_inc(s.beta, 1)
            dve.wait_ge(s.gamma, 1)
            dve.wait_ge(s.beta, 1)

            def stats_y(t, u4):
                done(dve, s.ps_y, t)
                dve.bn_stats(stats[:, u4 % 2, :], ps_y[u4][:, 0:P]).then_inc(s.stats, 1)
                freed(dve, s.y, t, 4)
                done(dve, s.stats, t)

            def variance_y(t, u4):
                u = u4 % 2
                done(dve, s.mean_var, t)
                freed(dve, s.rstd, t)
                dve.tensor_scalar(veps[:, u, :], mean_var[:, u4, 1:2], EPS, None, ALU.add).then_inc(s.veps, 1)

            def aggregate_y(t, u4):
                dve.bn_aggr(mean_var[:, u4, :], stats[:, u4 % 2, :]).then_inc(s.mean_var, 1)

            def normalize_y(t, u4):
                u = u4 % 2
                done(dve, s.rstd, t)
                freed(dve, s.scaled, t)
                dve.tensor_scalar(y[:, u, :], ps_y[u4][:, 0:P], mean_var[:, u4, 0:1], rstd[:, u, :],
                                  ALU.subtract, ALU.mult).then_inc(s.y, 1)
                freed(dve, s.z, t)
                dve.scalar_tensor_tensor(out=base[:, u, :], in0=xn[:, t, :], scalar=RSQRT2, in1=beta[:],
                                         op0=ALU.mult, op1=ALU.add).then_inc(s.base, 1)

            def stats_z(t, u4):
                done(dve, s.z, t)
                dve.bn_stats(stats2[:, u4 % 2, :], z[:, u4, :]).then_inc(s.stats2, 1)
                freed(dve, s.r, t, 4)
                done(dve, s.stats2, t)

            def variance_z(t, u4):
                u = u4 % 2
                done(dve, s.mean_var2, t)
                freed(dve, s.rstd2, t)
                dve.tensor_scalar(veps2[:, u, :], mean_var2[:, u4, 1:2], EPS, None, ALU.add).then_inc(s.veps2, 1)

            def aggregate_z(t, u4):
                dve.bn_aggr(mean_var2[:, u4, :], stats2[:, u4 % 2, :]).then_inc(s.mean_var2, 1)

            def normalize_z(t, u4):
                u = u4 % 2
                done(dve, s.rstd2, t)
                freed(dve, s.x, t)
                dve.tensor_scalar(r[:, u, :], z[:, u4, :], mean_var2[:, u4, 0:1], rstd2[:, u, :],
                                  ALU.subtract, ALU.mult).then_inc(s.r, 1)

            pipeline(dve, TILES, [(3, stats_y), (4, variance_y), (3, aggregate_y), (6, stats_z), (7, variance_z),
                                  (6, aggregate_z), (5, normalize_y), (8, normalize_z)], unroll=4)


def l1_ffn(nc, g, w):
    with ExitStack() as ctx:
        h_all = ctx.enter_context(nc.sbuf_tensor("d_h_all", [P, TOKENS], F32))
        weight = ctx.enter_context(nc.sbuf_tensor("d_weight", [P, TILES, EXPERTS], F32))
        mixed = ctx.enter_context(nc.sbuf_tensor("d_mixed", [P, TILES, P], F32))
        with ExitStack() as mid:
            logits = mid.enter_context(nc.sbuf_tensor("d_logits", [P, TILES, EXPERTS], F32))
            router_logits(nc, g, w, h_all, logits)
            route(nc, g, w, logits, weight)
        experts(nc, g, w, h_all, weight, mixed)
        normalize_all(nc, g, "d_out_", mixed, g.x, True)


def router_logits(nc, g, w, h_all, logits):
    with ExitStack() as ctx:
        def sb(name, shape, dt=F32):
            return ctx.enter_context(nc.sbuf_tensor("dr_" + name, shape, dt))

        stats = sb("stats", [P, 2, 6])
        mean_var = sb("mean_var", [P, 4, 2])
        veps = sb("veps", [P, 2, 1])
        rstd = sb("rstd", [P, 2, 1])
        h = sb("h", [P, 2, P])
        h_t = sb("h_t", [P, 2, P])
        ps_h = [ctx.enter_context(nc.psum_tensor(f"dr_ps_h{u}", [P, 512], F32)) for u in range(2)]
        ps_l = [ctx.enter_context(nc.psum_tensor(f"dr_ps_l{u}", [P, 512], F32)) for u in range(2)]
        s = sems(ctx, nc, "dr_", "stats mean_var veps rstd h ps_h h_t h_all ps_l logits")
        block = ctx.enter_context(nc.Block())

        @block.tensor
        def _(pe):
            pe.wait_ge(w.d_loaded, w.d_count)

            def transpose_h(t, u4):
                u = u4 % 2
                done(pe, s.h, t)
                freed(pe, s.h_t, t)
                pe.transpose(ps_h[u][:, 0:P], h[:, u, :], g.ident[:]).then_inc(s.ps_h, 1)

            def project(t, u4):
                u = u4 % 2
                done(pe, s.h_t, t)
                freed(pe, s.logits, t)
                pe.matmul(ps_l[u][:, 0:EXPERTS], h_t[:, u, :], w.router_d[:], start=True, stop=True).then_inc(s.ps_l, 1)

            pipeline(pe, TILES, [(2, transpose_h), (2, project)], unroll=4)

        @block.scalar
        def _(act):
            def copy_h(t, u4):
                u = u4 % 2
                done(act, s.ps_h, t)
                freed(act, s.ps_l, t)
                freed(act, s.h_all, t)
                act.activation(h_t[:, u, :], ps_h[u][:, 0:P], ACT.Copy).then_inc(s.h_t, 1)

            def copy_logits(t, u4):
                done(act, s.ps_l, t)
                act.activation(logits[:, t, :], ps_l[u4 % 2][:, 0:EXPERTS], ACT.Copy).then_inc(s.logits, 1)

            pipeline(act, TILES, [(2, copy_h), (3, copy_logits)], unroll=4)

        @block.gpsimd
        def _(pool):
            def inverse(t, u4):
                u = u4 % 2
                done(pool, s.veps, t)
                freed(pool, s.h, t)
                pool.tensor_tensor(rstd[:, u, :], veps[:, u, :], g.minus_half[:], ALU.pow).then_inc(s.rstd, 1)

            def keep_h(t, u4):
                done(pool, s.h_t, t)
                pool.tensor_copy(h_all[:, bass.ts(t, P)], h_t[:, u4 % 2, :]).then_inc(s.h_all, 1)

            pipeline(pool, TILES, [(1, inverse), (3, keep_h)], unroll=4)

        @block.vector
        def _(dve):
            def stats_of(t, u4):
                dve.bn_stats(stats[:, u4 % 2, :], g.x[:, t, :]).then_inc(s.stats, 1)
                freed(dve, s.h, t, 4)
                done(dve, s.stats, t)

            def variance(t, u4):
                u = u4 % 2
                done(dve, s.mean_var, t)
                freed(dve, s.rstd, t)
                dve.tensor_scalar(veps[:, u, :], mean_var[:, u4, 1:2], EPS, None, ALU.add).then_inc(s.veps, 1)

            def aggregate(t, u4):
                dve.bn_aggr(mean_var[:, u4, :], stats[:, u4 % 2, :]).then_inc(s.mean_var, 1)

            def normalize(t, u4):
                u = u4 % 2
                done(dve, s.rstd, t)
                freed(dve, s.ps_h, t)
                dve.tensor_scalar(h[:, u, :], g.x[:, t, :], mean_var[:, u4, 0:1], rstd[:, u, :],
                                  ALU.subtract, ALU.mult).then_inc(s.h, 1)

            pipeline(dve, TILES, [(0, stats_of), (1, variance), (0, aggregate), (2, normalize)], unroll=4)


def route(nc, g, w, logits, weight):
    with ExitStack() as ctx:
        def sb(name, shape, dt=F32):
            return ctx.enter_context(nc.sbuf_tensor("dw_" + name, shape, dt))

        COLS = TILES * EXPERTS
        best = sb("best", [P, TILES])
        shifted = sb("shifted", [P, TILES, EXPERTS])
        e = sb("e", [P, TILES, EXPERTS])
        total = sb("total", [P, TILES])
        inv = sb("inv", [P, TILES])
        left = sb("left", [P, 2, TILES, EXPERTS])
        top = sb("top", [P, 2, TILES])
        tie = sb("tie", [P, 2, TILES, EXPERTS])
        place = sb("place", [P, 2, TILES, EXPERTS])
        first = sb("first", [P, 2, TILES])
        chosen = sb("chosen", [P, 2, TILES, EXPERTS])
        chosen_bf = sb("chosen_bf", [P, 2, TILES, EXPERTS], BF16)
        counts = sb("counts", [P, 2, 2, TILES, EXPERTS])
        rank = sb("rank", [P, 2, TILES, EXPERTS])
        kept = sb("kept", [P, 2, TILES, EXPERTS])
        valued = sb("valued", [P, 2, TILES, EXPERTS])
        ps_before = [ctx.enter_context(nc.psum_tensor(f"dw_before{k}", [P, COLS], F32)) for k in range(2)]
        ps_count = [ctx.enter_context(nc.psum_tensor(f"dw_count{k}", [P, COLS], F32)) for k in range(2)]
        s = sems(ctx, nc, "dw_", "shifted exp chosen ps_before ps_count step")
        block = ctx.enter_context(nc.Block())

        @block.scalar
        def _(act):
            act.wait_ge(s.shifted, 1)
            act.activation(e[:], shifted[:], ACT.Exp).then_inc(s.exp, 1)

        @block.tensor
        def _(pe):
            pe.wait_ge(w.d_loaded, w.d_count)
            for k in range(2):
                pe.wait_ge(s.chosen, k + 1)
                cols = chosen_bf[:, k, :, :].rearrange("p t e -> p (t e)")
                pe.matmul(ps_before[k][:], w.earlier_d[:], cols, start=True, stop=True).then_inc(s.ps_before, 1)
                pe.matmul(ps_count[k][:], w.ones_d[:], cols, start=True, stop=True).then_inc(s.ps_count, 1)

        @block.vector
        def _(dve):
            steps = [0]

            def then(instruction):
                steps[0] += 1
                instruction.then_inc(s.step, 1)
                dve.wait_ge(s.step, steps[0])

            def by_tile(ap):
                return over(ap, 2, EXPERTS)

            iota = over(w.iota_d[:], 1, TILES)
            then(dve.tensor_reduce(best[:], logits[:], AX_X, ALU.max))
            dve.tensor_tensor(shifted[:], logits[:], by_tile(best[:]), ALU.subtract).then_inc(s.shifted, 1)
            dve.wait_ge(s.exp, 1)
            then(dve.tensor_reduce(total[:], e[:], AX_X, ALU.add))
            then(dve.reciprocal(inv[:], total[:]))
            then(dve.tensor_tensor(left[:, 0], e[:], by_tile(inv[:]), ALU.mult))
            for k in range(2):
                then(dve.tensor_reduce(top[:, k], left[:, k], AX_X, ALU.max))
                then(dve.tensor_tensor(tie[:, k], left[:, k], by_tile(top[:, k]), ALU.is_equal))
                then(dve.tensor_tensor(place[:, k], tie[:, k], iota, ALU.mult))
                then(dve.tensor_reduce(first[:, k], place[:, k], AX_X, ALU.min))
                then(dve.tensor_tensor(chosen[:, k], iota, by_tile(first[:, k]), ALU.is_equal))
                dve.tensor_copy(chosen_bf[:, k], chosen[:, k]).then_inc(s.chosen, 1)
                if k == 0:
                    then(dve.scalar_tensor_tensor(out=left[:, 1].rearrange("p t e -> p (t e)"),
                                                  in0=chosen[:, 0].rearrange("p t e -> p (t e)"), scalar=-2.0,
                                                  in1=left[:, 0].rearrange("p t e -> p (t e)"),
                                                  op0=ALU.mult, op1=ALU.add))
            for k in range(2):
                dve.wait_ge(s.ps_count, k + 1)
                then(dve.tensor_copy(counts[:, 0, k].rearrange("p t e -> p (t e)"), ps_count[k][:]))
            reach, at = 1, 0
            while reach < TILES:
                src, dst = counts[:, at], counts[:, 1 - at]
                dve.tensor_copy(dst[:, :, 0:reach, :], src[:, :, 0:reach, :]).then_inc(s.step, 1)
                steps[0] += 1
                then(dve.tensor_tensor(dst[:, :, reach:, :], src[:, :, reach:, :], src[:, :, :TILES - reach, :], ALU.add))
                reach, at = 2 * reach, 1 - at
            for k in range(2):
                dve.wait_ge(s.ps_before, k + 1)
                before = ps_before[k][:].rearrange("p (t e) -> p t e", e=EXPERTS)
                dve.tensor_copy(rank[:, k, 0:1, :], before[:, 0:1, :]).then_inc(s.step, 1)
                steps[0] += 1
                then(dve.tensor_tensor(rank[:, k, 1:, :], counts[:, at, k, 0:TILES - 1, :], before[:, 1:, :], ALU.add))
            then(dve.tensor_scalar(kept[:], rank[:], float(CAPACITY), None, ALU.is_lt))
            then(dve.tensor_tensor(kept[:], kept[:], chosen[:], ALU.mult))
            for k in range(2):
                then(dve.tensor_tensor(valued[:, k], kept[:, k], by_tile(top[:, k]), ALU.mult))
            then(dve.tensor_tensor(weight[:], valued[:, 0], valued[:, 1], ALU.add))


BLOCK = 512
BLOCKS = TOKENS // BLOCK
UNITS = EXPERTS * BLOCKS


def experts(nc, g, w, h_all, weight, mixed):
    with ExitStack() as ctx:
        def sb(name, shape, dt=F32):
            return ctx.enter_context(nc.sbuf_tensor("de_" + name, shape, dt))

        mats = sb("mats", [P, 2, 3, P])
        silu = sb("silu", [P, 2, BLOCK])
        hidden = sb("hidden", [P, 2, BLOCK])
        ps_gate = [ctx.enter_context(nc.psum_tensor(f"de_ps_gate{u}", [P, BLOCK], F32)) for u in range(2)]
        ps_up = [ctx.enter_context(nc.psum_tensor(f"de_ps_up{u}", [P, BLOCK], F32)) for u in range(2)]
        ps_out = [ctx.enter_context(nc.psum_tensor(f"de_ps_out{u}", [P, BLOCK], F32)) for u in range(2)]
        s = sems(ctx, nc, "de_", "zeroed ps_gate ps_up silu hidden ps_out mixed")
        loaded = [ctx.enter_context(nc.semaphore(f"de_loaded{u}")) for u in range(2)]
        block = ctx.enter_context(nc.Block())

        @block.sync
        def _(sp):
            def load(e, parity):
                for n, m in enumerate((w.gate, w.up, w.down)):
                    sp.dma_start(mats[:, parity, n, :], m[bass.ds(e, 1)].rearrange("a p n -> p (a n)")) \
                        .then_inc(loaded[parity], 16)

            load(0, 0)
            load(1, 1)
            with sp.Fori(2, EXPERTS - 1, 2) as e:
                for parity in range(2):
                    sp.wait_ge(s.ps_out, (e + parity - 1) * BLOCKS)
                    load(e + parity, parity)

        @block.tensor
        def _(pe):
            def hidden_of(t, u16):
                u, parity, blk = u16 % 2, u16 // BLOCKS, u16 % BLOCKS
                if blk == 0:
                    pe.wait_ge(loaded[parity], 48 * (t // (2 * BLOCKS) + 1))
                rhs = h_all[:, blk * BLOCK:(blk + 1) * BLOCK]
                freed(pe, s.silu, t)
                pe.matmul(ps_gate[u][:], mats[:, parity, 0, :], rhs, start=True, stop=True).then_inc(s.ps_gate, 1)
                freed(pe, s.hidden, t)
                pe.matmul(ps_up[u][:], mats[:, parity, 1, :], rhs, start=True, stop=True).then_inc(s.ps_up, 1)

            def out_of(t, u16):
                u, parity = u16 % 2, u16 // BLOCKS
                done(pe, s.hidden, t)
                freed(pe, s.mixed, t)
                for c in range(BLOCK // P):
                    mm = pe.matmul(ps_out[u][:, c * P:(c + 1) * P], hidden[:, u, c * P:(c + 1) * P], mats[:, parity, 2, :],
                                   start=True, stop=True)
                mm.then_inc(s.ps_out, 1)

            pipeline(pe, UNITS, [(0, hidden_of), (1, out_of)], unroll=2 * BLOCKS)

        @block.scalar
        def _(act):
            def silu_of(t, u):
                done(act, s.ps_gate, t)
                freed(act, s.hidden, t)
                act.activation(silu[:, u, :], ps_gate[u][:], ACT.Silu).then_inc(s.silu, 1)

            pipeline(act, UNITS, [(0, silu_of)])

        @block.vector
        def _(dve):
            dve.memset(mixed[:], 0.0).then_inc(s.zeroed, 1)
            dve.wait_ge(s.zeroed, 1)

            def gated(t, u8):
                u = u8 % 2
                done(dve, s.silu, t)
                done(dve, s.ps_up, t)
                freed(dve, s.ps_out, t)
                dve.tensor_tensor(hidden[:, u, :], silu[:, u, :], ps_up[u][:], ALU.mult).then_inc(s.hidden, 1)

            def accumulate(t, u8):
                u = u8 % 2
                done(dve, s.ps_out, t)
                tile = (t % BLOCKS) * (BLOCK // P)
                expert = t // BLOCKS
                w_flat = weight[:].rearrange("p t e -> p (t e)")
                m_flat = mixed[:].rearrange("p t n -> p (t n)")
                if not isinstance(t, int) or t >= BLOCKS:
                    dve.wait_ge(s.mixed, t - BLOCKS + 1)
                for c in range(BLOCK // P):
                    at = m_flat[:, bass.ds((tile + c) * P, P)]
                    m = dve.scalar_tensor_tensor(out=at, in0=ps_out[u][:, c * P:(c + 1) * P],
                                                 scalar=w_flat[:, bass.ds((tile + c) * EXPERTS + expert, 1)],
                                                 in1=at, op0=ALU.mult, op1=ALU.add)
                m.then_inc(s.mixed, 1)

            pipeline(dve, UNITS, [(0, gated), (1, accumulate)], unroll=BLOCKS, depth=BLOCKS)


def build(nc, a, out):
    with ExitStack() as ctx:
        def sb(name, shape, dt=F32):
            return ctx.enter_context(nc.sbuf_tensor(name, shape, dt))

        def row(ap):
            return ap.rearrange("(a n) -> a n", a=1)

        x = sb("x", [P, TILES, P])
        ident = sb("ident", [P, P])
        ones_row = sb("ones_row", [1, P])
        minus_half = sb("minus_half", [P, 1])
        s = sems(ctx, nc, "g_", "ident0 ident_ready consts_ready ones_ready x_loaded small_loaded tab_loaded stored c_loaded b_loaded d_loaded")
        g = Group()
        g.x, g.ident, g.ones_row, g.minus_half = x, ident, ones_row, minus_half
        g.ident_ready, g.consts_ready, g.x_loaded = s.ident_ready, s.consts_ready, s.x_loaded
        small = [("wq_a", a["L0_attn_Wq"], [P, P]), ("wdown", a["L0_attn_Wdown"], [P, LATENT]),
                 ("wup", a["L0_attn_Wup"], [LATENT, 2 * P]), ("wout_a", a["L0_attn_Wout"], [P, P]),
                 ("bq_a", row(a["L0_attn_bq"]), [1, P]), ("bup", row(a["L0_attn_bup"]), [1, 2 * P]),
                 ("bout_a", row(a["L0_attn_bout"]), [1, P]),
                 ("bdown", a["L0_attn_bdown"].rearrange("(n a) -> n a", a=1), [LATENT, 1])]
        for_c = [("wqk_c", a["L1_attn_W_qk"], [P, 2 * INNER]), ("wv_c", a["L1_attn_W_v"], [P, INNER]),
                 ("bv_c", row(a["L1_attn_b_v"]), [1, INNER]), ("bout_c", row(a["L1_attn_b_out"]), [1, P]),
                 ("wout_c", a["L1_attn_W_out"].rearrange("(c p) n -> p c n", p=P), [P, CHUNKS, P]),
                 ("gamma_c", row(a["L1_attn_ln_gamma"]).to_broadcast([P, P]), [P, P]),
                 ("beta_c", row(a["L1_attn_ln_beta"]).to_broadcast([P, P]), [P, P])]
        bqk_c = sb("bqk_c", [P, HEADS_C, 2])
        bias_c = sb("bias_c", [P, 2, HEADS_C])
        w = Group()
        w.bias_c, w.c_loaded, w.c_count = bias_c, s.c_loaded, 16 * (len(for_c) + 2)
        w.small_loaded, w.small_count = s.small_loaded, 16 * len(small)
        dst = {n: sb(n, shape) for n, _, shape in small}
        w.wq_a, w.wdown, w.wup, w.wout_a, w.bq_a, w.bup, w.bout_a, w.bdown = (dst[n] for n, _, _ in small)
        dst_c = {n: sb(n, shape) for n, _, shape in for_c}
        w.wqk_c, w.wv_c, w.bv_c, w.bout_c, w.wout_c, w.gamma_c, w.beta_c = (dst_c[n] for n, _, _ in for_c)
        tab = Group()
        tab.rope_a, tab.loaded = sb("rope_a", [P, SEQ_TILES, 2 * DIM_A]), s.tab_loaded
        x_dram = a["L0_attn_x"].rearrange("b (n p) d -> b p n d", p=P)
        out_dram = out.rearrange("b (n p) d -> b p n d", p=P)
        shapes_b = [("rope_b", [P, 4, SEQ], F32), ("mask_b", [P, SEQ_TILES * KEYS_B], BF16), ("carry", [P, SEQ_TILES], F32),
                    ("head_of", [P, 2], F32), ("spread", [HEADS_B, CHUNKS, P], F32), ("centre", [P, P], F32),
                    ("mean_col", [P, 1], F32), ("zeros", [P, P], F32), ("ident_bf", [P, P], BF16)]
        for_d = [("router_d", a["L1_ffn_router_w"], [P, EXPERTS], F32), ("earlier_d", a["tab_earlier"], [P, P], BF16),
                 ("ones_d", a["tab_ones"], [P, P], BF16), ("iota_d", a["tab_iota"], [P, EXPERTS], F32)]
        d = {n: sb(n, shape, dt) for n, _, shape, dt in for_d}
        w.router_d, w.earlier_d, w.ones_d, w.iota_d = (d[n] for n, _, _, _ in for_d)
        w.d_loaded, w.d_count = s.d_loaded, 16 * len(for_d)
        w.gate, w.up, w.down = a["L1_ffn_gate_w"], a["L1_ffn_up_w"], a["L1_ffn_down_w"]

        with nc.Block() as block:
            @block.sync
            def _(sp):
                sp.dma_start(x[:, 0:SEQ_TILES, :], x_dram[0]).then_inc(s.x_loaded, 16)
                for n, src, _ in small:
                    sp.dma_start(dst[n][:], src).then_inc(s.small_loaded, 16)
                sp.dma_start(tab.rope_a[:], a["tab_rope_a"]).then_inc(s.tab_loaded, 16)
                for b in range(1, BATCHES):
                    sp.dma_start(x[:, b * SEQ_TILES:(b + 1) * SEQ_TILES, :], x_dram[b]).then_inc(s.x_loaded, 16)
                for n, src, _ in for_c:
                    sp.dma_start(dst_c[n][:], src).then_inc(s.c_loaded, 16)
                for n, src, _, _ in for_d:
                    sp.dma_start(d[n][:], src).then_inc(s.d_loaded, 16)
                for twice in range(2):
                    sp.dma_start(bqk_c[twice * DIM_C:(twice + 1) * DIM_C],
                                 a["L1_attn_b_qk"].rearrange("(h d k) -> d h k", k=2, d=DIM_C)).then_inc(s.c_loaded, 16)

            @block.gpsimd
            def _(pool):
                pool.memset(ident[:], 0.0).then_inc(s.ident0, 1)
                pool.memset(minus_half[:], -0.5)
                pool.memset(ones_row[:], 1.0).then_inc(s.consts_ready, 1)
                pool.wait_ge(s.ident0, 1)
                pool.affine_select(out=ident[:], in_=ident[:], compare_op=ALU.not_equal, fill=1.0, base=0,
                                   pattern=[[-1, P]], channel_multiplier=1).then_inc(s.ident_ready, 1)

        with ExitStack() as first_two:
            def sb2(name, shape, dt=F32):
                return first_two.enter_context(nc.sbuf_tensor(name, shape, dt))

            b = {n: sb2(n, shape, dt) for n, shape, dt in shapes_b}
            w.wqkv_b = [sb2(f"wqkv_b{n}", [P, 3 * INNER]) for n in range(LAYERS)]
            w.wo_b = [sb2(f"wo_b{n}", [P, CHUNKS, P]) for n in range(LAYERS)]
            w.w1_b = [sb2(f"w1_b{n}", [P, 2 * HID_B]) for n in range(LAYERS)]
            w.w2_b = [sb2(f"w2_b{n}", [P, 3, P]) for n in range(LAYERS)]
            w.b1_b = sb2("b1_b", [1, LAYERS, 2 * HID_B])
            w.b2_b = sb2("b2_b", [1, LAYERS, P])
            w.ln_b = sb2("ln_b", [P, LAYERS, 2])
            w.scales_b = sb2("scales_b", [P, LAYERS, 4])
            tab.rope_b, tab.mask_b = b["rope_b"], b["mask_b"]
            g.carry, g.head_of, g.spread, g.centre = b["carry"], b["head_of"], b["spread"], b["centre"]
            g.mean_col, g.zeros, g.ident_bf = b["mean_col"], b["zeros"], b["ident_bf"]
            loads = [(b[n][:], a["tab_" + n]) for n, _, _ in shapes_b]
            last = HID_B - 2 * P
            half = DIM_B // 2
            for n in range(LAYERS):
                loads += [(w.wqkv_b[n][:], a["L0_ffn_wqkv"][n]),
                          (w.wo_b[n][:], a["L0_ffn_wo"][n].rearrange("(c p) n -> p c n", p=P)),
                          (w.w1_b[n][:], a["L0_ffn_w1"][n]),
                          (w.w2_b[n][:, 0:2, :], a["L0_ffn_w2"][n, 0:2 * P].rearrange("(c p) n -> p c n", p=P)),
                          (w.w2_b[n][0:last, 2, :], a["L0_ffn_w2"][n, 2 * P:HID_B])]
            loads += [(w.b1_b[:], a["L0_ffn_b1"].rearrange("(a l) n -> a l n", a=1)),
                      (w.b2_b[:], a["L0_ffn_b2"].rearrange("(a l) n -> a l n", a=1))]
            for k, name in ((0, "L0_ffn_ln_g"), (1, "L0_ffn_ln_b")):
                loads.append((w.ln_b[:, :, k], a[name].rearrange("l n -> n l")))
            for k, name in ((0, "L0_ffn_q_scale"), (1, "L0_ffn_k_scale")):
                src = a[name].rearrange("l d -> d l")
                for head in range(2):
                    at = head * DIM_B
                    loads += [(w.scales_b[at:at + DIM_B, :, 2 * k], src),
                              (w.scales_b[at:at + half, :, 2 * k + 1], src[half:DIM_B]),
                              (w.scales_b[at + half:at + DIM_B, :, 2 * k + 1], src[0:half])]
            w.b_loaded, w.b_count = s.b_loaded, 16 * len(loads)

            with nc.Block() as block:
                @block.gpsimd
                def _(pool):
                    for n in range(LAYERS):
                        pool.memset(w.w2_b[n][:, 2, :], 0.0)

            with nc.Block() as block:
                @block.sync
                def _(sp):
                    for to, src in loads:
                        sp.dma_start(to, src, allow_slow_non_contiguous=True).then_inc(s.b_loaded, 16)

            l0_attention(nc, g, w, tab)
            with nc.Block() as block:
                @block.sync
                def _(sp):
                    sp.wait_ge(w.b_loaded, w.b_count)
            l0_ffn(nc, g, w, tab)

        with nc.Block() as block:
            @block.vector
            def _(dve):
                dve.wait_ge(w.c_loaded, w.c_count)
                dve.tensor_scalar(bias_c[:, 0, :], bqk_c[:, :, 0], float(DIM_C) ** -0.5, None, ALU.mult)
                dve.tensor_copy(bias_c[:, 1, :], bqk_c[:, :, 1])
        l1_attention(nc, g, w)
        l1_ffn(nc, g, w)

        with nc.Block() as block:
            @block.sync
            def _(sp):
                sp.wait_ge(s.x_loaded, 16 * BATCHES)
                sp.wait_ge(s.small_loaded, w.small_count)
                sp.wait_ge(s.tab_loaded, 16)
                sp.wait_ge(s.c_loaded, w.c_count)
                sp.wait_ge(s.d_loaded, w.d_count)
                for b in range(BATCHES):
                    sp.dma_start(out_dram[b], x[:, b * SEQ_TILES:(b + 1) * SEQ_TILES, :]).then_inc(s.stored, 16)
                sp.wait_ge(s.stored, 16 * BATCHES)


def tables():
    import numpy as np

    def by_tile(t):
        return np.ascontiguousarray(t.reshape(SEQ_TILES, P, -1).transpose(1, 0, 2))

    f = np.float32
    pos = np.arange(SEQ, dtype=f)
    inv = (f(1.0) / f(10000.0) ** (np.arange(0, DIM_A, 2, dtype=f) / f(DIM_A))).astype(f)
    angle = pos[:, None] * inv[None, :]
    cos, sin = np.cos(angle), np.sin(angle)
    rope_a = by_tile(np.concatenate([cos, cos, -sin, sin], axis=-1).astype(f))

    half = np.arange(0, DIM_B, 2, dtype=f)
    inv = f(1.0) / f(10000.0) ** (half / f(DIM_B))
    angle = (pos[:, None] * inv[None, :]).astype(f)
    base = ((half + f(0.4 * DIM_B)) / f(1.4 * DIM_B)).astype(f)
    power = ((pos - SEQ // 2) / f(WINDOW // 2)).astype(f)
    scale = (base[None, :] ** power[:, None]).astype(f)
    sign = np.concatenate([-np.ones(DIM_B // 2, f), np.ones(DIM_B // 2, f)])
    cos, sin, scale = (np.concatenate([m, m], axis=-1) for m in (np.cos(angle), np.sin(angle), scale))
    rope_b = np.stack([cos * scale, sign * sin * scale, cos / scale, sign * sin / scale]).astype(f)
    rope_b = np.ascontiguousarray(np.tile(rope_b.transpose(2, 0, 1), (2, 1, 1)))

    bf16 = np.dtype("bfloat16")
    i, j = np.arange(P)[:, None], np.arange(-WINDOW, P)[None, :]
    seen = (i >= j) & (i <= j + WINDOW)
    mask = np.stack([seen & (j >= 0)] + [seen] * (SEQ_TILES - 1), axis=1)
    mask_b = np.where(mask, f(0.0), f(-1e30)).astype(bf16).reshape(P, -1)

    carry = np.ones((P, SEQ_TILES), f)
    carry[:, SEQ_TILES - 1] = 0.0
    feature = np.arange(P)
    head_of = (feature[:, None] // DIM_B == np.arange(2)[None, :]).astype(f)
    spread = (np.arange(HEADS_B)[:, None, None] == 2 * np.arange(CHUNKS)[None, :, None]
              + feature[None, None, :] // DIM_B).astype(f)
    centre = (np.eye(P) - 1.0 / P).astype(f)
    iota = np.tile(np.arange(EXPERTS, dtype=f) - EXPERTS, (P, 1))
    earlier = (feature[:, None] < feature[None, :]).astype(bf16)
    return {"tab_iota": iota, "tab_earlier": earlier, "tab_ones": np.ones((P, P), bf16), "tab_rope_a": rope_a, "tab_rope_b": rope_b, "tab_mask_b": mask_b, "tab_carry": carry, "tab_head_of": head_of,
            "tab_spread": spread, "tab_centre": centre, "tab_mean_col": np.full((P, 1), 1.0 / P, f),
            "tab_zeros": np.zeros((P, P), f), "tab_ident_bf": np.eye(P).astype(bf16)}


def kernel(**inputs):
    import numpy as np
    import concourse.bacc as bacc
    from concourse.bass_utils import run_bass_kernel_spmd

    nc = bacc.Bacc("TRN2", target_bir_lowering=False, num_devices=1)
    arrays, aps = {}, {}
    for name, value in [*inputs.items(), *tables().items()]:
        v = np.ascontiguousarray(value)
        arrays[name + "_dram"] = v
        aps[name] = nc.dram_tensor(name + "_dram", v.shape, mybir.dt.from_np(v.dtype), kind="ExternalInput").ap()
    out = nc.dram_tensor("out_dram", (BATCHES, SEQ, P), F32, kind="ExternalOutput").ap()
    build(nc, aps, out)
    r = run_bass_kernel_spmd(nc, [arrays], core_ids=[0])
    return r.results[0]["out_dram"]
```

```python
from collections import namedtuple
from contextlib import ExitStack

import concourse.bass as bass
from concourse import mybir

F32 = mybir.dt.float32
BF16 = mybir.dt.bfloat16
ALU = mybir.AluOpType
ACT = mybir.ActivationFunctionType
AX_X = mybir.AxisListType.X

P = 128
TOKENS = 4096
SEQ = 1024
TILES = TOKENS // P
SEQ_TILES = SEQ // P
BATCHES = TOKENS // SEQ
EPS = 1e-5

HEADS_A = 16
DIM_A = P // HEADS_A
LATENT = 32

LAYERS = 2
HEADS_B = 8
DIM_B = 64
INNER = HEADS_B * DIM_B
WINDOW = 64
KEYS_B = P + WINDOW
CHUNKS = INNER // P
HID_B = int(P * 4 * 2 / 3)

HEADS_C = 8
DIM_C = 64

EXPERTS = 16
CAPACITY = -(-TOKENS * 2 * 5 // (EXPERTS * 4))


class Group:
    pass


def sems(ctx, nc, prefix, names):
    found = [nc.alloc_semaphore(name=prefix + n) for n in names.split()]

    def clear():
        nc.clear_and_free_semaphores(found)
        nc.all_engine_barrier()

    ctx.callback(clear)
    return namedtuple("Semaphores", names)(*found)


def done(eng, sem, t):
    eng.wait_ge(sem, t + 1)


def freed(eng, sem, t, depth=2):
    if isinstance(t, int) and t < depth:
        return
    eng.wait_ge(sem, t - depth + 1)


def pipeline(eng, tiles, steps, unroll=2, depth=4):
    first = -(-(max(lag for lag, _ in steps) + depth) // unroll) * unroll
    whole = (tiles - first) // unroll
    end = first + unroll * whole

    def one_round(i, k):
        for lag, step in steps:
            if not isinstance(i, int) or 0 <= i + k - lag < tiles:
                step(i + k - lag, (first + k - lag) % unroll)

    for r in range(first):
        one_round(r - r % unroll, r % unroll)
    if whole == 1:
        for k in range(unroll):
            one_round(first, k)
    elif whole > 1:
        with eng.Fori(first, end - unroll + 1, unroll) as i:
            for k in range(unroll):
                one_round(i, k)
    for r in range(end, tiles + max(lag for lag, _ in steps)):
        one_round(r - r % unroll, r % unroll)


def over(ap, axis, count):
    shape = list(ap.shape)
    shape.insert(axis, count)
    return ap.unsqueeze(axis).to_broadcast(shape)


def l0_attention(nc, g, w, tab):
    with ExitStack() as ctx:
        def sb(name, shape, dt=F32):
            return ctx.enter_context(nc.sbuf_tensor("a_" + name, shape, dt))

        def pb(name, shape, dt=F32):
            return ctx.enter_context(nc.psum_tensor("a_" + name, shape, dt))

        down_up = sb("down_up", [P, 3 * P])
        bias = sb("bias", [1, 3 * P])
        wdown_t = sb("wdown_t", [LATENT, P])
        stats = sb("stats", [P, 2, 6])
        mean_var = sb("mean_var", [P, 4, 2])
        rstd = sb("rstd", [P, 2, 1])
        veps = sb("veps", [P, 2, 1])
        h = sb("h", [P, 2, P])
        h_t = sb("h_t", [P, 2, P])
        qk_raw = sb("qk_raw", [P, 2, 2 * P])
        v = sb("v", [P, 4, P])
        turned_c = sb("turned_c", [P, 2, 2 * P])
        turned_s = sb("turned_s", [P, 2, 2 * P])
        qk = sb("qk", [P, 2, 2 * P])
        prod_qk = sb("prod_qk", [P, 2, HEADS_A * HEADS_A * DIM_A])
        score = sb("score", [P, 2, HEADS_A * HEADS_A])
        top = sb("top", [P, 2, HEADS_A])
        shifted = sb("shifted", [P, 2, HEADS_A * HEADS_A])
        prob = sb("prob", [P, 2, HEADS_A * HEADS_A])
        total = sb("total", [P, 2, HEADS_A])
        inv = sb("inv", [P, 2, HEADS_A])
        prod_pv = sb("prod_pv", [P, 2, HEADS_A * HEADS_A * DIM_A])
        mixed = sb("mixed", [P, 2, P])
        o = sb("o", [P, 2, P])
        o_t = sb("o_t", [P, 2, P])
        stats2 = sb("stats2", [P, 2, 6])
        mean_var2 = sb("mean_var2", [P, 4, 2])
        rstd2 = sb("rstd2", [P, 2, 1])
        veps2 = sb("veps2", [P, 2, 1])
        y = sb("y", [P, 2, P])
        ps_h = pb("ps_h", [P, 512])
        ps_qkv = [pb(f"ps_qkv{u}", [P, 512]) for u in range(2)]
        ps_o = pb("ps_o", [P, 512])
        ps_out = [pb(f"ps_out{u}", [P, 512]) for u in range(4)]
        s = sems(ctx, nc, "a_", "wd_t wd_copy fold fold_w fold_b stats mean_var veps rstd h ps_h h_t ps_qkv qk_raw v "
                 "turn1 turn2 turn3 qk prod_qk score top shifted prob total inv prod_pv mixed o ps_o o_t "
                 "ps_out stats2 mean_var2 veps2 rstd2 y x")
        block = ctx.enter_context(nc.Block())

        def heads(ap):
            return ap.rearrange("p (h d) -> p h d", d=DIM_A)

        @block.tensor
        def _(pe):
            pe.wait_ge(g.ident_ready, 1)
            pe.wait_ge(w.small_loaded, w.small_count)
            pe.transpose(ps_h[0:LATENT, 0:P], w.wdown[:], g.ident[:]).then_inc(s.wd_t, 1)
            done(pe, s.wd_copy, 0)
            pe.matmul(ps_qkv[0][:, 0:2 * P], wdown_t[:], w.wup[:], start=True, stop=True)
            pe.matmul(ps_o[0:1, 0:2 * P], w.bdown[:], w.wup[:], start=True, stop=True).then_inc(s.fold, 1)

            def transpose_h(t, u4):
                u = u4 % 2
                done(pe, s.h, t)
                freed(pe, s.h_t, t, 1)
                if isinstance(t, int) and t == 0:
                    done(pe, s.wd_copy, 0)
                pe.transpose(ps_h[:, 0:P], h[:, u, :], g.ident[:]).then_inc(s.ps_h, 1)

            def project(t, u4):
                u = u4 % 2
                if isinstance(t, int) and t == 0:
                    pe.wait_ge(s.fold_w, 2)
                    pe.wait_ge(s.fold_b, 2)
                done(pe, s.h_t, t)
                freed(pe, s.v, t)
                pe.matmul(ps_qkv[u][:, 0:3 * P], h_t[:, u, :], down_up[:], start=True, stop=False)
                pe.matmul(ps_qkv[u][:, 0:3 * P], g.ones_row[:], bias[:], start=False, stop=True).then_inc(s.ps_qkv, 1)

            def transpose_o(t, u4):
                u = u4 % 2
                done(pe, s.o, t)
                freed(pe, s.o_t, t, 1)
                pe.transpose(ps_o[:, 0:P], o[:, u, :], g.ident[:]).then_inc(s.ps_o, 1)

            def project_out(t, u4):
                u = u4 % 2
                done(pe, s.o_t, t)
                freed(pe, s.y, t, 4)
                pe.matmul(ps_out[u4][:, 0:P], o_t[:, u, :], w.wout_a[:], start=True, stop=False)
                pe.matmul(ps_out[u4][:, 0:P], g.ones_row[:], w.bout_a[:], start=False, stop=True).then_inc(s.ps_out, 1)

            pipeline(pe, TILES, [(2, transpose_h), (2, project), (7, transpose_o), (7, project_out)], unroll=4)

        @block.scalar
        def _(act):
            done(act, s.wd_t, 0)
            act.activation(wdown_t[:], ps_h[0:LATENT, 0:P], ACT.Copy).then_inc(s.wd_copy, 1)
            act.wait_ge(w.small_loaded, w.small_count)
            act.activation(down_up[:, 0:P], w.wq_a[:], ACT.Copy).then_inc(s.fold_w, 1)
            act.activation(bias[:, 0:P], w.bq_a[:], ACT.Copy).then_inc(s.fold_b, 1)
            done(act, s.fold, 0)
            kv = "p (h a d) -> p a h d"
            act.activation(down_up[:, P:].rearrange("p (a h d) -> p a h d", a=2, d=DIM_A),
                           ps_qkv[0][:, 0:2 * P].rearrange(kv, a=2, d=DIM_A), ACT.Copy).then_inc(s.fold_w, 1)

            def copy_h(t, u4):
                u = u4 % 2
                done(act, s.ps_h, t)
                freed(act, s.ps_qkv, t)
                act.activation(h_t[:, u, :], ps_h[:, 0:P], ACT.Copy).then_inc(s.h_t, 1)

            def copy_qkv(t, u4):
                u = u4 % 2
                done(act, s.ps_qkv, t)
                freed(act, s.qk, t)
                act.activation(qk_raw[:, u, :], ps_qkv[u][:, 0:2 * P], ACT.Copy).then_inc(s.qk_raw, 1)
                freed(act, s.prod_pv, t, 4)
                act.activation(v[:, u4, :].rearrange("p (d h) -> p h d", d=DIM_A),
                               heads(ps_qkv[u][:, 2 * P:3 * P]), ACT.Copy).then_inc(s.v, 1)

            def exp(t, u4):
                u = u4 % 2
                done(act, s.shifted, t)
                freed(act, s.prod_pv, t)
                freed(act, s.total, t)
                act.activation(prob[:, u, :], shifted[:, u, :], ACT.Exp, scale=float(DIM_A) ** -0.5).then_inc(s.prob, 1)

            def copy_o(t, u4):
                u = u4 % 2
                done(act, s.ps_o, t)
                freed(act, s.ps_out, t)
                act.activation(o_t[:, u, :], ps_o[:, 0:P], ACT.Copy).then_inc(s.o_t, 1)

            pipeline(act, TILES, [(2, copy_h), (2, copy_qkv), (7, copy_o), (5, exp)], unroll=4)

        @block.gpsimd
        def _(pool):
            def rstd_in(t, u4):
                u = u4 % 2
                done(pool, s.veps, t)
                freed(pool, s.h, t)
                pool.tensor_tensor(rstd[:, u, :], veps[:, u, :], g.minus_half[:], ALU.pow).then_inc(s.rstd, 1)

            def rotate(t, u4):
                u = u4 % 2
                n = t % SEQ_TILES
                done(pool, s.qk_raw, t)
                freed(pool, s.qk, t)
                src = qk_raw[:, u, :].rearrange("p (g a d) -> p g a d", a=2, d=DIM_A // 2)
                cos = tab.rope_a[:, n, 0:DIM_A]
                sin = tab.rope_a[:, n, DIM_A:2 * DIM_A].rearrange("p (a d) -> p a d", a=2)
                pool.tensor_tensor(heads(turned_c[:, u, :]), heads(qk_raw[:, u, :]),
                                   over(cos, 1, 2 * HEADS_A), ALU.mult).then_inc(s.turn1, 1)
                dst = turned_s[:, u, :].rearrange("p (g a d) -> p g a d", a=2, d=DIM_A // 2)
                for a, sem in ((0, s.turn2), (1, s.turn3)):
                    pool.tensor_tensor(dst[:, :, a, :], src[:, :, 1 - a, :], over(sin[:, a, :], 1, 2 * HEADS_A),
                                       ALU.mult).then_inc(sem, 1)
                done(pool, s.turn1, t)
                done(pool, s.turn2, t)
                done(pool, s.turn3, t)
                freed(pool, s.prod_qk, t)
                pool.tensor_tensor(qk[:, u, :], turned_c[:, u, :], turned_s[:, u, :], ALU.add).then_inc(s.qk, 1)

            def shift(t, u4):
                u = u4 % 2
                done(pool, s.top, t)
                freed(pool, s.prob, t)
                by_head = "p (h g) -> p h g"
                pool.tensor_tensor(shifted[:, u, :].rearrange(by_head, h=HEADS_A),
                                   score[:, u, :].rearrange(by_head, h=HEADS_A),
                                   over(top[:, u, :], 2, HEADS_A), ALU.subtract).then_inc(s.shifted, 1)

            def mix(t, u4):
                u = u4 % 2
                done(pool, s.prob, t)
                done(pool, s.v, t)
                freed(pool, s.mixed, t)
                out = prod_pv[:, u, :].rearrange("p (h d g) -> p h d g", h=HEADS_A, g=HEADS_A)
                p = over(prob[:, u, :].rearrange("p (h g) -> p h g", h=HEADS_A), 2, DIM_A)
                vs = over(v[:, u4, :].rearrange("p (d g) -> p d g", d=DIM_A), 1, HEADS_A)
                pool.tensor_tensor(out, p, vs, ALU.mult).then_inc(s.prod_pv, 1)

            def rstd_out(t, u4):
                u = u4 % 2
                done(pool, s.veps2, t)
                freed(pool, s.y, t)
                pool.tensor_tensor(rstd2[:, u, :], veps2[:, u, :], g.minus_half[:], ALU.pow).then_inc(s.rstd2, 1)

            def residual(t, u4):
                u = u4 % 2
                done(pool, s.y, t)
                pool.tensor_tensor(g.x[:, t, :], g.x[:, t, :], y[:, u, :], ALU.add).then_inc(s.x, 1)

            pool.wait_ge(g.consts_ready, 1)
            pool.wait_ge(tab.loaded, 16)
            pipeline(pool, TILES, [(1, rstd_in), (9, rstd_out), (10, residual), (5, shift), (3, rotate), (5, mix)], unroll=4)

        @block.vector
        def _(dve):
            done(dve, s.fold, 0)
            dve.tensor_tensor(bias[:, P:].rearrange("p (a h d) -> p a h d", a=2, d=DIM_A),
                              ps_o[0:1, 0:2 * P].rearrange("p (h a d) -> p a h d", a=2, d=DIM_A),
                              w.bup[:].rearrange("p (h a d) -> p a h d", a=2, d=DIM_A), ALU.add).then_inc(s.fold_b, 1)

            def stats_in(t, u4):
                u = u4 % 2
                dve.bn_stats(stats[:, u, :], g.x[:, t, :]).then_inc(s.stats, 1)
                freed(dve, s.h, t, 4)
                done(dve, s.stats, t)

            def variance_in(t, u4):
                u = u4 % 2
                done(dve, s.mean_var, t)
                freed(dve, s.rstd, t)
                dve.tensor_scalar(veps[:, u, :], mean_var[:, u4, 1:2], EPS, None, ALU.add).then_inc(s.veps, 1)

            def aggregate_in(t, u4):
                u = u4 % 2
                dve.bn_aggr(mean_var[:, u4, :], stats[:, u, :]).then_inc(s.mean_var, 1)

            def normalize(t, u4):
                u = u4 % 2
                done(dve, s.rstd, t)
                freed(dve, s.ps_h, t)
                dve.tensor_scalar(h[:, u, :], g.x[:, t, :], mean_var[:, u4, 0:1], rstd[:, u, :],
                                  ALU.subtract, ALU.mult).then_inc(s.h, 1)

            def scores(t, u4):
                u = u4 % 2
                done(dve, s.qk, t)
                freed(dve, s.score, t)
                out = prod_qk[:, u, :].rearrange("p (h g d) -> p h g d", h=HEADS_A, d=DIM_A)
                q = over(heads(qk[:, u, 0:P]), 2, HEADS_A)
                k = over(heads(qk[:, u, P:]), 1, HEADS_A)
                dve.tensor_tensor(out, q, k, ALU.mult).then_inc(s.prod_qk, 1)
                done(dve, s.prod_qk, t)
                freed(dve, s.shifted, t)
                dve.tensor_reduce(score[:, u, :], prod_qk[:, u, :].rearrange("p (s d) -> p s d", d=DIM_A),
                                  AX_X, ALU.add).then_inc(s.score, 1)
                done(dve, s.score, t)
                dve.tensor_reduce(top[:, u, :], score[:, u, :].rearrange("p (h g) -> p h g", h=HEADS_A),
                                  AX_X, ALU.max).then_inc(s.top, 1)

            def totals(t, u4):
                u = u4 % 2
                done(dve, s.prob, t)
                dve.tensor_reduce(total[:, u, :], prob[:, u, :].rearrange("p (h g) -> p h g", h=HEADS_A),
                                  AX_X, ALU.add).then_inc(s.total, 1)
                done(dve, s.total, t)
                freed(dve, s.o, t)
                dve.reciprocal(inv[:, u, :], total[:, u, :]).then_inc(s.inv, 1)

            def gather(t, u4):
                u = u4 % 2
                done(dve, s.prod_pv, t)
                freed(dve, s.o, t)
                dve.tensor_reduce(mixed[:, u, :], prod_pv[:, u, :].rearrange("p (s g) -> p s g", g=HEADS_A),
                                  AX_X, ALU.add).then_inc(s.mixed, 1)
                done(dve, s.mixed, t)
                done(dve, s.inv, t)
                freed(dve, s.ps_o, t)
                dve.tensor_tensor(heads(o[:, u, :]), heads(mixed[:, u, :]), over(inv[:, u, :], 2, DIM_A),
                                  ALU.mult).then_inc(s.o, 1)

            def stats_out(t, u4):
                u = u4 % 2
                done(dve, s.ps_out, t)
                dve.bn_stats(stats2[:, u, :], ps_out[u4][:, 0:P]).then_inc(s.stats2, 1)
                freed(dve, s.y, t, 4)
                done(dve, s.stats2, t)

            def variance_out(t, u4):
                u = u4 % 2
                done(dve, s.mean_var2, t)
                freed(dve, s.rstd2, t)
                dve.tensor_scalar(veps2[:, u, :], mean_var2[:, u4, 1:2], EPS, None, ALU.add).then_inc(s.veps2, 1)

            def aggregate_out(t, u4):
                u = u4 % 2
                dve.bn_aggr(mean_var2[:, u4, :], stats2[:, u, :]).then_inc(s.mean_var2, 1)

            def normalize_out(t, u4):
                u = u4 % 2
                done(dve, s.rstd2, t)
                freed(dve, s.x, t)
                dve.tensor_scalar(y[:, u, :], ps_out[u4][:, 0:P], mean_var2[:, u4, 0:1], rstd2[:, u, :],
                                  ALU.subtract, ALU.mult).then_inc(s.y, 1)

            dve.wait_ge(g.x_loaded, 16 * BATCHES)
            pipeline(dve, TILES, [(0, stats_in), (1, variance_in), (0, aggregate_in), (2, normalize),
                                  (8, stats_out), (9, variance_out), (8, aggregate_out), (10, normalize_out),
                                  (6, totals), (6, gather), (4, scores)], unroll=4)


def normalize_all(nc, g, name, src, dst, add):
    with ExitStack() as ctx:
        def sb(n, shape):
            return ctx.enter_context(nc.sbuf_tensor(name + n, shape, F32))

        stats = sb("stats", [P, 4, 6])
        mean_var = sb("mean_var", [P, 4, 2])
        veps = sb("veps", [P, 4, 1])
        rstd = sb("rstd", [P, 4, 1])
        y = sb("y", [P, 4, P])
        s = sems(ctx, nc, name, "stats mean_var veps rstd y dst")
        block = ctx.enter_context(nc.Block())

        @block.gpsimd
        def _(pool):
            def inverse(t, u):
                done(pool, s.veps, t)
                freed(pool, s.y, t, 4)
                pool.tensor_tensor(rstd[:, u, :], veps[:, u, :], g.minus_half[:], ALU.pow).then_inc(s.rstd, 1)

            def residual(t, u):
                done(pool, s.y, t)
                pool.tensor_tensor(dst[:, t, :], dst[:, t, :], y[:, u, :], ALU.add).then_inc(s.dst, 1)

            pipeline(pool, TILES, [(1, inverse)] + [(3, residual)] * add, unroll=4)

        @block.vector
        def _(dve):
            def stats_of(t, u):
                dve.bn_stats(stats[:, u, :], src[:, t, :]).then_inc(s.stats, 1)
                freed(dve, s.y, t, 4)
                done(dve, s.stats, t)

            def variance(t, u):
                done(dve, s.mean_var, t)
                freed(dve, s.rstd, t, 4)
                dve.tensor_scalar(veps[:, u, :], mean_var[:, u, 1:2], EPS, None, ALU.add).then_inc(s.veps, 1)

            def aggregate(t, u):
                dve.bn_aggr(mean_var[:, u, :], stats[:, u, :]).then_inc(s.mean_var, 1)

            def normalize(t, u):
                done(dve, s.rstd, t)
                if add:
                    freed(dve, s.dst, t, 4)
                out = y[:, u, :] if add else dst[:, t, :]
                dve.tensor_scalar(out, src[:, t, :], mean_var[:, u, 0:1], rstd[:, u, :],
                                  ALU.subtract, ALU.mult).then_inc(s.y, 1)

            pipeline(dve, TILES, [(0, stats_of), (1, variance), (0, aggregate), (3, normalize)], unroll=4)


def l0_ffn(nc, g, w, tab):
    with ExitStack() as ctx:
        y = ctx.enter_context(nc.sbuf_tensor("b_y", [P, TILES, P], F32))
        normalize_all(nc, g, "b_in_", g.x, y, False)
        for layer in range(LAYERS):
            local_attention(nc, g, w, tab, layer, y)
            gated_ffn(nc, g, w, layer, y)
        normalize_all(nc, g, "b_out_", y, g.x, True)


def shifted_transpose(act, g, s, t, u, n, ps_y, h_t):
    act.activation(h_t[0:64, u, :], ps_y[0:64, 0:P], ACT.Copy)
    act.activation(h_t[64:P, u, 1:P], ps_y[64:P, 0:P - 1], ACT.Copy)
    act.activation(h_t[64:P, 1 - u, 0:1], ps_y[64:P, P - 1:P], ACT.Copy, scale=g.carry[64:P, bass.ds(n, 1)]) \
        .then_inc(s.h_t, 1)


def local_attention(nc, g, w, tab, layer, y):
    pre = f"l{layer}_"
    WINDOWS = P // WINDOW
    with ExitStack() as ctx:
        def sb(name, shape, dt=F32):
            return ctx.enter_context(nc.sbuf_tensor(pre + name, shape, dt))

        def pb(name, shape=(P, 512)):
            return ctx.enter_context(nc.psum_tensor(pre + name, list(shape), F32))

        w_qkv = w.wqkv_b[layer]
        rot = sb("rot", [P, 4, SEQ_TILES, DIM_B])
        y_now = sb("y_now", [P, 2, P])
        h_t = sb("h_t", [P, 2, P])
        by_cos = sb("by_cos", [P, 2, INNER])
        by_sin = sb("by_sin", [P, 2, INNER])
        square = sb("square", [P, 2, INNER])
        norm = sb("norm", [P, 2, 2 * HEADS_B])
        clipped = sb("clipped", [P, 2, 2 * HEADS_B])
        r_norm = sb("r_norm", [P, 2, 2 * HEADS_B])
        q_sum = sb("q_sum", [P, 2, INNER])
        k_sum = sb("k_sum", [P, 2, INNER])
        q_unit = sb("q_unit", [P, 2, INNER])
        k_unit = sb("k_unit", [P, 2, INNER])
        q_t = sb("q_t", [P, 2, WINDOWS, CHUNKS, P])
        k_t = sb("k_t", [P, 4, CHUNKS, KEYS_B])
        v = sb("v", [P, 4, INNER])
        v_shift = sb("v_shift", [P, 4, INNER])
        top = sb("top", [P, WINDOWS, CHUNKS])
        neg_top = sb("neg_top", [P, WINDOWS, CHUNKS])
        total = sb("total", [P, WINDOWS, CHUNKS])
        inv = sb("inv", [P, WINDOWS, CHUNKS])
        term = sb("term", [P, WINDOWS, 512])
        prob = sb("prob", [P, WINDOWS, 512])
        prob_t = sb("prob_t", [P, 512])
        o_t = sb("o_t", [P, 2, CHUNKS, P])
        ps_qk = [pb(f"ps_qk{k}") for k in range(2)]
        ps_v = pb("ps_v")
        ps_s = [pb(f"ps_s{w}") for w in range(WINDOWS)]
        ps_t = pb("ps_t")
        ps_o = pb("ps_o")
        ps_m = pb("ps_m")
        s = sems(ctx, nc, pre, "rot first y_now ps_y h_t ps_q ps_k square_q square_k cos_q sin_q cos_k sin_k q_sum k_sum "
                 "norm_q norm_k clipped r_norm q_unit k_unit ps_qt ps_kt q_t k_t k_next ps_v v v_before ps_s masked top "
                 "neg_top term inv prob ps_t prob_t ps_o o_t ps_w y")
        block = ctx.enter_context(nc.Block())

        def group(t, win):
            return t * WINDOWS + win

        def blocks(ap):
            return ap.rearrange("p (c n) -> p c n", c=CHUNKS)

        def heads(ap):
            return ap.rearrange("p (h d) -> p h d", d=DIM_B)

        def window(step, win):
            return lambda t, u4: step(t, u4, win)

        @block.tensor
        def _(pe):
            pe.wait_ge(s.first, 3)

            def transpose_y(t, u4):
                done(pe, s.y_now, t)
                if isinstance(t, int) and 1 <= t < 6:
                    done(pe, s.h_t, t - 1)
                freed(pe, s.y, t, 6)
                pe.transpose(ps_m[:, 0:P], y_now[:, u4 % 2, :], g.ident[:]).then_inc(s.ps_y, 1)

            def project_q(t, u4):
                done(pe, s.h_t, t)
                freed(pe, s.cos_q, t, 1)
                freed(pe, s.sin_q, t, 1)
                freed(pe, s.square_q, t, 1)
                pe.matmul(ps_qk[0][:], h_t[:, u4 % 2, :], w_qkv[:, 0:INNER], start=True, stop=True).then_inc(s.ps_q, 1)

            def project_k(t, u4):
                freed(pe, s.cos_k, t, 1)
                freed(pe, s.sin_k, t, 1)
                freed(pe, s.square_k, t, 1)
                pe.matmul(ps_qk[1][:], h_t[:, u4 % 2, :], w_qkv[:, INNER:2 * INNER], start=True, stop=True) \
                    .then_inc(s.ps_k, 1)

            def project_v(t, u4):
                if isinstance(t, int) and t == 1:
                    done(pe, s.v, 0)
                freed(pe, s.k_t, t)
                pe.matmul(ps_v[:], h_t[:, u4 % 2, :], w_qkv[:, 2 * INNER:3 * INNER], start=True, stop=True) \
                    .then_inc(s.ps_v, 1)

            def transpose_q(t, u4):
                done(pe, s.q_unit, t)
                if isinstance(t, int) and t + 1 == TILES:
                    freed(pe, s.k_t, t, 1)
                else:
                    done(pe, s.v, t + 1)
                for c in range(CHUNKS):
                    mm = pe.transpose(ps_v[:, c * P:c * P + P], q_unit[:, u4 % 2, c * P:c * P + P], g.ident[:])
                mm.then_inc(s.ps_qt, 1)

            def transpose_k(t, u4):
                done(pe, s.k_unit, t)
                done(pe, s.q_t, t)
                for c in range(CHUNKS):
                    mm = pe.transpose(ps_v[:, c * P:c * P + P], k_unit[:, u4 % 2, c * P:c * P + P], g.ident[:])
                mm.then_inc(s.ps_kt, 1)

            def scores(t, u4, win):
                if win == 0:
                    done(pe, s.k_t, t)
                    freed(pe, s.k_next, t, 1)
                    done(pe, s.q_t, t)
                freed(pe, s.masked, group(t, win))
                for c in range(CHUNKS):
                    mm = pe.matmul(ps_s[win][:, c * P:c * P + P], q_t[:, u4 % 2, win, c, :],
                                   k_t[:, u4, c, win * WINDOW:win * WINDOW + P], start=True, stop=True)
                mm.then_inc(s.ps_s, 1)

            def transpose_p(t, u4, win):
                done(pe, s.prob, group(t, win))
                freed(pe, s.prob_t, group(t, win), 1)
                for c in range(CHUNKS):
                    mm = pe.transpose(ps_t[:, c * P:c * P + P], prob[:, win, c * P:c * P + P], g.ident[:])
                mm.then_inc(s.ps_t, 1)

            def mix(t, u4, win):
                done(pe, s.prob_t, group(t, win))
                freed(pe, s.o_t, group(t, win), 1)
                if win == 0:
                    done(pe, s.v_before, t)
                values = (v_shift, v)[win]
                for c in range(CHUNKS):
                    cols = slice(c * P, c * P + P)
                    mm = pe.matmul(ps_o[:, cols], values[:, u4, cols], prob_t[:, cols], start=True, stop=True)
                mm.then_inc(s.ps_o, 1)

            def project_out(t, u4):
                done(pe, s.o_t, group(t, 1))
                if isinstance(t, int) and t + 5 >= TILES:
                    freed(pe, s.y, t, 1)
                if not isinstance(t, int) or t + 5 < TILES:
                    done(pe, s.h_t, t + 5)
                for c in range(CHUNKS):
                    mm = pe.matmul(ps_m[:, 0:P], o_t[:, u4 % 2, c, :], w.wo_b[layer][:, c, :],
                                   start=(c == 0), stop=(c == CHUNKS - 1))
                mm.then_inc(s.ps_w, 1)

            pipeline(pe, TILES, [
                (4, window(scores, 0)), (5, window(transpose_p, 0)), (1, project_q), (5, window(mix, 0)), (3, transpose_q),
                (6, project_out), (4, window(scores, 1)), (1, project_k), (5, window(transpose_p, 1)), (3, transpose_k),
                (0, transpose_y), (5, window(mix, 1)), (1, project_v)], unroll=4)

        @block.scalar
        def _(act):
            def copy_h(t, u4):
                done(act, s.ps_y, t)
                freed(act, s.ps_v, t, 1)
                shifted_transpose(act, g, s, t, u4 % 2, t % SEQ_TILES, ps_m, h_t)

            def square_q(t, u4):
                done(act, s.ps_q, t)
                freed(act, s.norm_q, t, 1)
                act.activation(square[:, 0, :], ps_qk[0][:], ACT.Square).then_inc(s.square_q, 1)

            def square_k(t, u4):
                done(act, s.ps_k, t)
                freed(act, s.norm_k, t, 1)
                act.activation(square[:, 1, :], ps_qk[1][:], ACT.Square).then_inc(s.square_k, 1)

            def copy_q(t, u4):
                done(act, s.ps_qt, t)
                if not isinstance(t, int) or t >= 2:
                    act.wait_ge(s.ps_s, group(t, 0) - 2)
                for h in range(2):
                    rows, queries = slice(h * DIM_B, (h + 1) * DIM_B), slice(h * WINDOW, (h + 1) * WINDOW)
                    e = act.activation(q_t[rows, u4 % 2, :, :, queries],
                                       ps_v[rows, :].rearrange("p (c w a) -> p w c a", c=CHUNKS, w=WINDOWS), ACT.Copy)
                e.then_inc(s.q_t, 1)

            def copy_v(t, u4):
                done(act, s.ps_v, t)
                if not isinstance(t, int) or t >= 4:
                    act.wait_ge(s.ps_o, group(t, 0) - 6)
                act.activation(v[:, u4, :], ps_v[:], ACT.Copy)
                act.activation(v_shift[WINDOW:P, u4, :], ps_v[0:WINDOW, :], ACT.Copy).then_inc(s.v, 1)
                if not isinstance(t, int) or t > 0:
                    act.wait_ge(s.v, t)
                before = 0 if isinstance(t, int) and t == 0 else (u4 + 3) % 4
                if isinstance(t, int) and t == 0:
                    act.wait_ge(s.v, 1)
                act.activation(v_shift[0:WINDOW, u4, :], v[WINDOW:P, before, :], ACT.Copy).then_inc(s.v_before, 1)

            def exp(t, u4, win):
                done(act, s.neg_top, group(t, win))
                for c in range(CHUNKS):
                    e = act.activation(term[:, win, c * P:c * P + P], term[:, win, c * P:c * P + P], ACT.Exp,
                                       bias=neg_top[:, win, c:c + 1], scale=8.0,
                                       accum_out=total[:, win, c:c + 1])
                e.then_inc(s.term, 1)

            def copy_p(t, u4, win):
                done(act, s.ps_t, group(t, win))
                freed(act, s.ps_o, group(t, win), 1)
                act.activation(prob_t[:], ps_t[:], ACT.Copy).then_inc(s.prob_t, 1)

            def copy_o(t, u4, win):
                done(act, s.ps_o, group(t, win))
                if win == 0:
                    freed(act, s.ps_w, t)
                for h in range(2):
                    rows, queries = slice(h * DIM_B, (h + 1) * DIM_B), slice(h * WINDOW, (h + 1) * WINDOW)
                    e = act.activation(o_t[rows, u4 % 2, :, win * WINDOW:(win + 1) * WINDOW],
                                       blocks(ps_o[rows, :])[:, :, queries], ACT.Copy)
                e.then_inc(s.o_t, 1)

            pipeline(act, TILES, [
                (5, window(copy_p, 0)), (1, square_q), (4, window(exp, 0)), (3, copy_q), (5, window(copy_o, 0)),
                (1, square_k), (5, window(copy_p, 1)), (4, window(exp, 1)), (0, copy_h), (5, window(copy_o, 1)),
                (1, copy_v)], unroll=4)

        @block.gpsimd
        def _(pool):
            pool.memset(h_t[64:P, 0, 0:1], 0.0).then_inc(s.first, 1)
            pool.wait_ge(s.first, 1)
            pool.memset(k_t[:, 0, :, 0:WINDOW], 0.0).then_inc(s.first, 1)
            pool.wait_ge(s.first, 2)
            pool.memset(q_t[:], 0.0).then_inc(s.first, 1)

            def sum_of(t, u4, k, dst, cos_sem, sin_sem, read_sem, sem):
                done(pool, cos_sem, t)
                done(pool, sin_sem, t)
                freed(pool, read_sem, t)
                pool.tensor_tensor(dst[:, u4 % 2, :], by_cos[:, k, :], by_sin[:, k, :], ALU.add).then_inc(sem, 1)

            def sum_q(t, u4):
                sum_of(t, u4, 0, q_sum, s.cos_q, s.sin_q, s.q_unit, s.q_sum)

            def sum_k(t, u4):
                sum_of(t, u4, 1, k_sum, s.cos_k, s.sin_k, s.k_unit, s.k_sum)

            def inverse_norm(t, u4):
                done(pool, s.clipped, t)
                freed(pool, s.q_unit, t)
                freed(pool, s.k_unit, t)
                pool.tensor_tensor(r_norm[:, u4 % 2, :], clipped[:, u4 % 2, :],
                                   g.minus_half[:].to_broadcast([P, 2 * HEADS_B]), ALU.pow).then_inc(s.r_norm, 1)

            def scale_q(t, u4):
                done(pool, s.r_norm, t)
                done(pool, s.q_sum, t)
                freed(pool, s.ps_qt, t)
                pool.tensor_tensor(heads(q_unit[:, u4 % 2, :]), heads(q_sum[:, u4 % 2, :]),
                                   over(r_norm[:, u4 % 2, 0:HEADS_B], 2, DIM_B), ALU.mult).then_inc(s.q_unit, 1)

            def probabilities(t, u4, win):
                done(pool, s.inv, group(t, win))
                freed(pool, s.ps_t, group(t, win))
                pool.tensor_tensor(blocks(prob[:, win, :]), blocks(term[:, win, :]), over(inv[:, win, :], 2, P),
                                   ALU.mult).then_inc(s.prob, 1)

            pipeline(pool, TILES, [
                (2, inverse_norm), (1, sum_q), (4, window(probabilities, 0)), (2, scale_q), (1, sum_k),
                (4, window(probabilities, 1))], unroll=4)

        @block.vector
        def _(dve):
            dve.wait_ge(w.b_loaded, w.b_count)
            for n in range(4):
                dve.tensor_tensor(rot[:, n], tab.rope_b[:, n], over(w.scales_b[:, layer, n, :], 1, SEQ_TILES),
                                  ALU.mult).then_inc(s.rot, 1)
            dve.wait_ge(s.rot, 4)
            dve.wait_ge(s.first, 3)

            def stage_y(t, u4):
                freed(dve, s.ps_y, t)
                dve.tensor_copy(y_now[:, u4 % 2, :], y[:, t, :]).then_inc(s.y_now, 1)

            def rotate(t, k, ps_sem, square_sem, cos_sem, sin_sem, read_sem):
                done(dve, ps_sem, t)
                done(dve, square_sem, t)
                freed(dve, read_sem, t, 1)
                tables = rot[:].rearrange("p k n d -> p k (n d)")
                at = (t % SEQ_TILES) * DIM_B
                dve.tensor_tensor(heads(by_cos[:, k, :]), heads(ps_qk[k][:]),
                                  over(tables[:, 2 * k, bass.ds(at, DIM_B)], 1, HEADS_B), ALU.mult).then_inc(cos_sem, 1)
                halves = "p (h a d) -> p a h d"
                src, dst = (x.rearrange(halves, a=2, d=DIM_B // 2) for x in (ps_qk[k][:], by_sin[:, k, :]))
                for a in range(2):
                    sin = tables[:, 2 * k + 1, bass.ds(at + a * (DIM_B // 2), DIM_B // 2)]
                    e = dve.tensor_tensor(dst[:, a], src[:, 1 - a], over(sin, 1, HEADS_B), ALU.mult)
                e.then_inc(sin_sem, 1)

            def rotate_q(t, u4):
                rotate(t, 0, s.ps_q, s.square_q, s.cos_q, s.sin_q, s.q_sum)

            def rotate_k(t, u4):
                rotate(t, 1, s.ps_k, s.square_k, s.cos_k, s.sin_k, s.k_sum)

            def norm_q(t, u4):
                freed(dve, s.clipped, t)
                dve.tensor_reduce(norm[:, u4 % 2, 0:HEADS_B], heads(square[:, 0, :]), AX_X, ALU.add).then_inc(s.norm_q, 1)

            def norm_k(t, u4):
                dve.tensor_reduce(norm[:, u4 % 2, HEADS_B:], heads(square[:, 1, :]), AX_X, ALU.add).then_inc(s.norm_k, 1)

            def clip_norm(t, u4):
                done(dve, s.norm_q, t)
                done(dve, s.norm_k, t)
                freed(dve, s.r_norm, t)
                dve.tensor_scalar(clipped[:, u4 % 2, :], norm[:, u4 % 2, :], 1e-24, None, ALU.max).then_inc(s.clipped, 1)

            def scale_k(t, u4):
                done(dve, s.r_norm, t)
                done(dve, s.k_sum, t)
                freed(dve, s.ps_kt, t)
                dve.tensor_tensor(heads(k_unit[:, u4 % 2, :]), heads(k_sum[:, u4 % 2, :]),
                                  over(r_norm[:, u4 % 2, HEADS_B:], 2, DIM_B), ALU.mult).then_inc(s.k_unit, 1)

            def copy_k(t, u4):
                done(dve, s.ps_kt, t)
                if not isinstance(t, int) or t >= 4:
                    dve.wait_ge(s.ps_s, group(t, 0) - 6)
                dve.tensor_copy(k_t[:, u4, :, WINDOW:], blocks(ps_v[:])).then_inc(s.k_t, 1)

            def keys_before(t, u4):
                if not isinstance(t, int) or t >= 3:
                    dve.wait_ge(s.ps_s, group(t, 0) - 4)
                done(dve, s.k_t, t)
                dve.tensor_copy(k_t[:, (u4 + 1) % 4, :, 0:WINDOW], k_t[:, u4, :, P:P + WINDOW]).then_inc(s.k_next, 1)

            def tops(t, u4, win):
                done(dve, s.ps_s, group(t, win))
                freed(dve, s.prob, group(t, win))
                at = (t % SEQ_TILES) * P if win == 0 else SEQ_TILES * P
                mask = over(tab.mask_b[:, bass.ds(at, P)], 1, CHUNKS)
                dve.tensor_tensor(blocks(term[:, win, :]), blocks(ps_s[win][:]), mask, ALU.add).then_inc(s.masked, 1)
                done(dve, s.masked, group(t, win))
                dve.tensor_reduce(top[:, win, :], blocks(term[:, win, :]), AX_X, ALU.max).then_inc(s.top, 1)
                done(dve, s.top, group(t, win))
                dve.tensor_scalar(neg_top[:, win, :], top[:, win, :], -8.0, None, ALU.mult).then_inc(s.neg_top, 1)

            def inverse(t, u4, win):
                done(dve, s.term, group(t, win))
                freed(dve, s.prob, group(t, win))
                dve.reciprocal(inv[:, win, :], total[:, win, :]).then_inc(s.inv, 1)

            def residual(t, u4):
                done(dve, s.ps_w, t)
                dve.tensor_tensor(y[:, t, :], y[:, t, :], ps_m[:, 0:P], ALU.add).then_inc(s.y, 1)

            pipeline(dve, TILES, [
                (4, window(tops, 0)), (2, clip_norm), (1, rotate_q), (4, window(inverse, 0)), (1, norm_q),
                (6, residual), (0, stage_y), (4, window(tops, 1)), (3, copy_k), (3, keys_before), (2, scale_k),
                (1, rotate_k), (1, norm_k), (4, window(inverse, 1))], unroll=4)


def gated_ffn(nc, g, w, layer, y):
    pre = f"f{layer}_"
    PAD = 3 * P
    with ExitStack() as ctx:
        def sb(name, shape, dt=F32):
            return ctx.enter_context(nc.sbuf_tensor(pre + name, shape, dt))

        def pb(name, shape=(P, 512)):
            return ctx.enter_context(nc.psum_tensor(pre + name, list(shape), F32))

        w1 = w.w1_b[layer]
        w1_g = sb("w1_g", [P, 2 * HID_B])
        beta = sb("beta", [P, P])
        offset = sb("offset", [P, 2 * HID_B])
        y_now = sb("y_now", [P, 2, P])
        h_t = sb("h_t", [P, 2, P])
        centred = sb("centred", [P, 4, P])
        square = sb("square", [P, 2, P])
        veps = sb("veps", [P, 2, 1])
        rstd = sb("rstd", [P, 2, 1])
        gate = sb("gate", [P, 2, HID_B])
        gelu = sb("gelu", [P, 2, HID_B])
        linear = sb("linear", [P, 2, HID_B])
        hidden = sb("hidden", [P, 2, PAD])
        hidden_t = sb("hidden_t", [P, 2, PAD])
        ps_y = pb("ps_y")
        ps_c = pb("ps_c")
        ps_n = pb("ps_n")
        ps_a = pb("ps_a")
        ps_g = pb("ps_g")
        ps_t = pb("ps_t")
        ps_o = [pb(f"ps_o{u}") for u in range(2)]
        s = sems(ctx, nc, pre, "w1_g beta offset ps_off first y_now ps_y h_t ps_c centred square ps_n veps rstd ps_a ps_g "
                 "gate linear gelu hidden ps_t hidden_t ps_o y")
        block = ctx.enter_context(nc.Block())

        @block.tensor
        def _(pe):
            pe.wait_ge(s.beta, 1)
            for ps, cols in ((ps_a, slice(0, HID_B)), (ps_g, slice(HID_B, 2 * HID_B))):
                pe.matmul(ps[:, 0:HID_B], beta[:], w1[:, cols], start=True, stop=False)
                mm = pe.matmul(ps[:, 0:HID_B], g.ones_row[:], w.b1_b[:, layer, cols], start=False, stop=True)
            mm.then_inc(s.ps_off, 1)
            pe.wait_ge(s.offset, 2)
            pe.wait_ge(s.first, 2)

            def transpose_y(t, u4):
                done(pe, s.y_now, t)
                freed(pe, s.h_t, t, 1)
                pe.transpose(ps_y[:, 0:P], y_now[:, u4 % 2, :], g.ident[:]).then_inc(s.ps_y, 1)

            def centre(t, u4):
                done(pe, s.h_t, t)
                freed(pe, s.square, t, 1)
                pe.matmul(ps_c[:, 0:P], g.centre[:], h_t[:, u4 % 2, :], start=True, stop=True).then_inc(s.ps_c, 1)

            def variance(t, u4):
                done(pe, s.square, t)
                freed(pe, s.veps, t, 1)
                pe.matmul(ps_n[:, 0:1], square[:, u4 % 2, :], g.mean_col[:], start=True, stop=True).then_inc(s.ps_n, 1)

            def expand(t, u4):
                done(pe, s.centred, t)
                freed(pe, s.gate, t, 1)
                pe.matmul(ps_g[:, 0:HID_B], centred[:, u4, :], w1_g[:, HID_B:], start=True, stop=True).then_inc(s.ps_g, 1)
                freed(pe, s.linear, t, 1)
                pe.matmul(ps_a[:, 0:HID_B], centred[:, u4, :], w1_g[:, 0:HID_B], start=True, stop=True).then_inc(s.ps_a, 1)

            def transpose_hidden(t, u4):
                done(pe, s.hidden, t)
                freed(pe, s.hidden_t, t, 1)
                for c in range(3):
                    mm = pe.transpose(ps_t[:, c * P:c * P + P], hidden[:, u4 % 2, c * P:c * P + P], g.ident[:])
                mm.then_inc(s.ps_t, 1)

            def contract(t, u4):
                done(pe, s.hidden_t, t)
                freed(pe, s.y, t)
                for c in range(3):
                    pe.matmul(ps_o[u4 % 2][:, 0:P], hidden_t[:, u4 % 2, c * P:c * P + P], w.w2_b[layer][:, c, :],
                              start=(c == 0), stop=False)
                pe.matmul(ps_o[u4 % 2][:, 0:P], g.ones_row[:], w.b2_b[:, layer, :], start=False, stop=True) \
                    .then_inc(s.ps_o, 1)

            pipeline(pe, TILES, [(1, transpose_y), (5, transpose_hidden), (2, variance), (3, expand), (1, centre),
                                 (5, contract)], unroll=4)

        @block.scalar
        def _(act):
            done(act, s.ps_off, 0)
            act.activation(offset[:, 0:HID_B], ps_a[:, 0:HID_B], ACT.Copy).then_inc(s.offset, 1)
            act.activation(offset[:, HID_B:], ps_g[:, 0:HID_B], ACT.Copy).then_inc(s.offset, 1)

            def copy_h(t, u4):
                done(act, s.ps_y, t)
                freed(act, s.ps_c, t, 1)
                shifted_transpose(act, g, s, t, u4 % 2, t % SEQ_TILES, ps_y, h_t)

            def copy_centred(t, u4):
                done(act, s.ps_c, t)
                freed(act, s.ps_a, t, 4)
                act.activation(centred[:, u4, :], ps_c[:, 0:P], ACT.Copy).then_inc(s.centred, 1)
                freed(act, s.ps_n, t)
                act.activation(square[:, u4 % 2, :], ps_c[:, 0:P], ACT.Square).then_inc(s.square, 1)

            def gelu_of(t, u4):
                done(act, s.gate, t)
                freed(act, s.hidden, t)
                act.activation(gelu[:, u4 % 2, :], gate[:, u4 % 2, :], ACT.Gelu).then_inc(s.gelu, 1)

            def copy_hidden(t, u4):
                done(act, s.ps_t, t)
                freed(act, s.ps_o, t)
                act.activation(hidden_t[:, u4 % 2, :], ps_t[:, 0:PAD], ACT.Copy).then_inc(s.hidden_t, 1)

            pipeline(act, TILES, [(1, copy_h), (5, copy_hidden), (4, gelu_of), (1, copy_centred)], unroll=4)

        @block.gpsimd
        def _(pool):
            pool.memset(h_t[64:P, 0, 0:1], 0.0).then_inc(s.first, 1)
            pool.wait_ge(s.first, 1)
            pool.memset(hidden[:], 0.0).then_inc(s.first, 1)
            pool.wait_ge(s.first, 2)

            def stage_y(t, u4):
                freed(pool, s.ps_y, t)
                pool.tensor_copy(y_now[:, u4 % 2, :], y[:, t, :]).then_inc(s.y_now, 1)

            def inverse(t, u4):
                done(pool, s.veps, t)
                freed(pool, s.linear, t)
                pool.tensor_tensor(rstd[:, u4 % 2, :], veps[:, u4 % 2, :], g.minus_half[:], ALU.pow).then_inc(s.rstd, 1)

            def gated(t, u4):
                done(pool, s.gelu, t)
                done(pool, s.linear, t)
                freed(pool, s.ps_t, t)
                pool.tensor_tensor(hidden[:, u4 % 2, 0:HID_B], linear[:, u4 % 2, :], gelu[:, u4 % 2, :], ALU.mult) \
                    .then_inc(s.hidden, 1)

            pipeline(pool, TILES, [(0, stage_y), (2, inverse), (4, gated)], unroll=4)

        @block.vector
        def _(dve):
            dve.wait_ge(w.b_loaded, w.b_count)
            dve.tensor_scalar(w1_g[:], w1[:], w.ln_b[:, layer, 0:1], None, ALU.mult).then_inc(s.w1_g, 1)
            dve.tensor_scalar(beta[:], g.zeros[:], w.ln_b[:, layer, 1:2], None, ALU.add).then_inc(s.beta, 1)
            dve.wait_ge(s.w1_g, 1)
            dve.wait_ge(s.offset, 2)

            def add_eps(t, u4):
                done(dve, s.ps_n, t)
                freed(dve, s.rstd, t)
                dve.tensor_scalar(veps[:, u4 % 2, :], ps_n[:, 0:1], EPS, None, ALU.add).then_inc(s.veps, 1)

            def scale_hidden(t, u4):
                done(dve, s.rstd, t)
                done(dve, s.ps_g, t)
                freed(dve, s.gelu, t)
                dve.scalar_tensor_tensor(out=gate[:, u4 % 2, :], in0=ps_g[:, 0:HID_B], scalar=rstd[:, u4 % 2, :],
                                         in1=offset[:, HID_B:], op0=ALU.mult, op1=ALU.add).then_inc(s.gate, 1)
                done(dve, s.ps_a, t)
                freed(dve, s.hidden, t)
                dve.scalar_tensor_tensor(out=linear[:, u4 % 2, :], in0=ps_a[:, 0:HID_B], scalar=rstd[:, u4 % 2, :],
                                         in1=offset[:, 0:HID_B], op0=ALU.mult, op1=ALU.add).then_inc(s.linear, 1)

            def residual(t, u4):
                done(dve, s.ps_o, t)
                dve.tensor_tensor(y[:, t, :], y[:, t, :], ps_o[u4 % 2][:, 0:P], ALU.add).then_inc(s.y, 1)

            pipeline(dve, TILES, [(6, residual), (2, add_eps), (3, scale_hidden)], unroll=4)


def l1_attention(nc, g, w):
    with ExitStack() as outer:
        def keep(name, shape, dt=F32):
            return outer.enter_context(nc.sbuf_tensor("c_" + name, shape, dt))

        xn = keep("xn", [P, TILES, P])
        vo = keep("vo", [P, BATCHES * CHUNKS + 1, SEQ_TILES, P])
        with ExitStack() as mid:
            h_all = mid.enter_context(nc.sbuf_tensor("c_h_all", [P, TOKENS], F32))
            l1_attention_values(nc, g, w, xn, h_all, vo)
            l1_attention_heads(nc, g, w, h_all, vo)
        l1_attention_out(nc, g, w, xn, vo)


def l1_attention_values(nc, g, w, xn, h_all, vo):
    with ExitStack() as ctx:
        def sb(name, shape, dt=F32):
            return ctx.enter_context(nc.sbuf_tensor("cv_" + name, shape, dt))

        stats = sb("stats", [P, 2, 6])
        mean_var = sb("mean_var", [P, 4, 2])
        veps = sb("veps", [P, 2, 1])
        rstd = sb("rstd", [P, 2, 1])
        stage = sb("stage", [P, 2, P])
        h_t = sb("h_t", [P, 2, P])
        ps_h = [ctx.enter_context(nc.psum_tensor(f"cv_ps_h{u}", [P, 512], F32)) for u in range(2)]
        ps_v = [ctx.enter_context(nc.psum_tensor(f"cv_ps_v{u}", [P, 512], F32)) for u in range(2)]
        s = sems(ctx, nc, "cv_", "stats mean_var veps rstd xn kept ps_h h_t h_all ps_v v")
        block = ctx.enter_context(nc.Block())

        @block.tensor
        def _(pe):
            pe.wait_ge(w.c_loaded, w.c_count)

            def project(t, u4):
                u = u4 % 2
                done(pe, s.h_t, t)
                freed(pe, s.v, t)
                pe.matmul(ps_v[u][:], h_t[:, u, :], w.wv_c[:], start=True, stop=True).then_inc(s.ps_v, 1)

            def transpose_in(t, u4):
                u = u4 % 2
                done(pe, s.xn, t)
                freed(pe, s.h_t, t)
                pe.transpose(ps_h[u][:, 0:P], stage[:, u, :], g.ident[:]).then_inc(s.ps_h, 1)

            pipeline(pe, TILES, [(3, transpose_in), (4, project)], unroll=4)

        @block.scalar
        def _(act):
            def copy_h(t, u4):
                u = u4 % 2
                done(act, s.ps_h, t)
                freed(act, s.ps_v, t)
                freed(act, s.h_all, t)
                act.activation(h_t[:, u, :], ps_h[u][:, 0:P], ACT.Copy).then_inc(s.h_t, 1)

            def keep_h(t, u4):
                done(act, s.h_t, t)
                act.activation(h_all[:, bass.ts(t, P)], h_t[:, u4 % 2, :], ACT.Copy).then_inc(s.h_all, 1)

            pipeline(act, TILES, [(3, copy_h), (4, keep_h)], unroll=4)

        @block.gpsimd
        def _(pool):
            def rstd_in(t, u4):
                u = u4 % 2
                done(pool, s.veps, t)
                freed(pool, s.xn, t)
                pool.tensor_tensor(rstd[:, u, :], veps[:, u, :], g.minus_half[:], ALU.pow).then_inc(s.rstd, 1)

            def keep_xn(t, u4):
                done(pool, s.xn, t)
                pool.tensor_copy(xn[:, t, :], stage[:, u4 % 2, :]).then_inc(s.kept, 1)

            pipeline(pool, TILES, [(1, rstd_in), (2, keep_xn)], unroll=4)

        @block.vector
        def _(dve):
            def stats_in(t, u4):
                u = u4 % 2
                dve.bn_stats(stats[:, u, :], g.x[:, t, :]).then_inc(s.stats, 1)
                freed(dve, s.xn, t, 4)
                done(dve, s.stats, t)

            def variance_in(t, u4):
                u = u4 % 2
                done(dve, s.mean_var, t)
                freed(dve, s.rstd, t)
                dve.tensor_scalar(veps[:, u, :], mean_var[:, u4, 1:2], EPS, None, ALU.add).then_inc(s.veps, 1)

            def aggregate_in(t, u4):
                dve.bn_aggr(mean_var[:, u4, :], stats[:, u4 % 2, :]).then_inc(s.mean_var, 1)

            def normalize(t, u4):
                u = u4 % 2
                done(dve, s.rstd, t)
                freed(dve, s.ps_h, t)
                freed(dve, s.kept, t)
                dve.tensor_scalar(stage[:, u, :], g.x[:, t, :], mean_var[:, u4, 0:1], rstd[:, u, :],
                                  ALU.subtract, ALU.mult).then_inc(s.xn, 1)

            def add_bias(t, u4):
                done(dve, s.ps_v, t)
                slot = (t // SEQ_TILES) * CHUNKS + 1
                dve.tensor_tensor(vo[:, bass.ds(slot, CHUNKS), bass.ds(t % SEQ_TILES, 1), :].rearrange("p c a n -> p c (a n)"),
                                  ps_v[u4 % 2][:].rearrange("p (c n) -> p c n", c=CHUNKS),
                                  w.bv_c[:].rearrange("p (c n) -> p c n", c=CHUNKS), ALU.add).then_inc(s.v, 1)

            pipeline(dve, TILES, [(0, stats_in), (1, variance_in), (0, aggregate_in), (2, normalize), (4, add_bias)],
                     unroll=4)


PAIR_STEPS = 2 * SEQ_TILES
STEPS_C = BATCHES * (HEADS_C // 2) * PAIR_STEPS


def l1_attention_heads(nc, g, w, h_all, vo):
    F32R = mybir.dt.float32r
    with ExitStack() as ctx:
        def sb(name, shape, dt=F32):
            return ctx.enter_context(nc.sbuf_tensor("ch_" + name, shape, dt))

        def pb(name, shape):
            return ctx.enter_context(nc.psum_tensor("ch_" + name, shape, F32))

        w_sorted = sb("w_sorted", [P, 2, INNER])
        w_now = sb("w_now", [P, 2, P])
        q_hl = sb("q_hl", [P, 2, 2, SEQ], F32R)
        k_h = sb("k_h", [P, 2, 2, SEQ], F32R)
        k_l = sb("k_l", [P, 2, 2, SEQ], F32R)
        low = sb("low", [P, 512])
        q_now = sb("q_now", [P, 2, P], F32R)
        neg_top = sb("neg_top", [P, 4, 1])
        prob = sb("prob", [P, 2, SEQ])
        total = sb("total", [P, 4, 1])
        inv = sb("inv", [P, 4, 1])
        prob_t = sb("prob_t", [P, 2, SEQ_TILES, P])
        ps_s = [pb(f"ps_s{u}", [P, SEQ]) for u in range(2)]
        ps_t = [pb(f"ps_t{u}", [P, 512]) for u in range(2)]
        ps_o = pb("ps_o", [P, 512])
        ps_p = pb("ps_p", [P, 512])
        s = sems(ctx, nc, "ch_", "w_sorted w_now ps_p hi lo whole q_now ps_s neg_top prob total ps_ta ps_tb pt_a pt_b ps_o inv o")
        block = ctx.enter_context(nc.Block())

        def job(t):
            return t // 2

        def job_place(t):
            return t // PAIR_STEPS, (t % 8) // 4, (t % PAIR_STEPS) // 8

        def scaled_bias(t, k):
            pair = (t // PAIR_STEPS) % (HEADS_C // 2)
            head = pair * 2 + (t % 8) // 4
            return w.bias_c[:, k, bass.ds(head, 1)]

        @block.tensor
        def _(pe):
            def project(t, u):
                if u % 2:
                    return
                done(pe, s.w_now, job(t))
                freed(pe, s.lo, job(t), 1)
                pair, _, half = job_place(t)
                cols = (pair // (HEADS_C // 2)) * SEQ + half * 512
                pe.matmul(ps_p[:], w_now[:, u // 2, :], h_all[:, bass.ds(cols, 512)], start=True, stop=True) \
                    .then_inc(s.ps_p, 1)

            def scores(t, u):
                hh = u % 2
                pair = t // PAIR_STEPS
                if hh == 0:
                    pe.wait_ge(s.lo, (pair + 1) * 8)
                done(pe, s.q_now, t)
                freed(pe, s.prob, t)
                for half in range(2):
                    out = ps_s[hh][:, half * 512:half * 512 + 512]
                    cols = (pair % 2) * 2 * SEQ + hh * SEQ + half * 512
                    for part, (k, start) in enumerate(((k_h, True), (k_l, False))):
                        flat = k[:].rearrange("p a b n -> p (a b n)")
                        mm = pe.matmul(out, q_now[:, hh, :], flat[:, bass.ds(cols, 512)], start=start, stop=not start)
                mm.then_inc(s.ps_s, 1)

            def transposes(t, u):
                done(pe, s.prob, t)
                for half, free, sem in ((0, s.pt_a, s.ps_ta), (1, s.pt_b, s.ps_tb)):
                    freed(pe, free, t, 1)
                    for j in range(4):
                        c = half * 4 + j
                        mm = pe.transpose(ps_t[half][:, j * P:(j + 1) * P], prob[:, u % 2, c * P:(c + 1) * P], g.ident[:])
                    mm.then_inc(sem, 1)

            def mix(t, u):
                freed(pe, s.o, t, 1)
                done(pe, s.pt_a, t)
                pair = t // PAIR_STEPS
                flat = vo[:].rearrange("p c t n -> p (c t n)")
                base = (pair + 1) * (SEQ_TILES * P) + (u % 2) * DIM_C
                for j in range(SEQ_TILES):
                    if j == 4:
                        done(pe, s.pt_b, t)
                    mm = pe.matmul(ps_o[:, 0:DIM_C], prob_t[:, u % 2, j, :], flat[:, bass.ds(base + j * P, DIM_C)],
                                   start=(j == 0), stop=(j == SEQ_TILES - 1))
                mm.then_inc(s.ps_o, 1)

            pipeline(pe, STEPS_C, [(17, scores), (18, transposes), (19, mix), (1, project)], unroll=4)

        @block.scalar
        def _(act):
            def split_high(t, u):
                if u % 2:
                    return
                done(act, s.ps_p, job(t))
                pair, head, half = job_place(t)
                if not isinstance(t, int) or pair >= 1:
                    act.wait_ge(s.ps_s, (t - PAIR_STEPS) // PAIR_STEPS * PAIR_STEPS + 1)
                dst = (q_hl, k_h)[u // 2][:].rearrange("p a b n -> p (a b n)")
                cols = (pair % 2) * 2 * SEQ + head * SEQ + half * 512
                scale = (float(DIM_C) ** -0.5, 1.0)[u // 2]
                act.activation(dst[:, bass.ds(cols, 512)], ps_p[:], ACT.Identity, bias=scaled_bias(t, u // 2),
                               scale=scale).then_inc(s.hi, 1)

            def exp(t, u):
                done(act, s.neg_top, t)
                if not isinstance(t, int) or t >= 2:
                    act.wait_ge(s.ps_tb, t - 1)
                freed(act, s.inv, t, 4)
                act.activation(prob[:, u % 2, :], ps_s[u % 2][:], ACT.Exp, bias=neg_top[:, u, :],
                               accum_out=total[:, u, :]).then_inc(s.prob, 1)

            def copy_a(t, u):
                done(act, s.ps_ta, t)
                freed(act, s.ps_o, t)
                act.activation(prob_t[:, u % 2, 0:4, :].rearrange("p j n -> p (j n)"), ps_t[0][:], ACT.Copy) \
                    .then_inc(s.pt_a, 1)

            pipeline(act, STEPS_C, [(2, split_high), (18, copy_a), (17, exp)], unroll=4)

        @block.gpsimd
        def _(pool):
            pool.wait_ge(s.w_sorted, 2)

            def stage_weights(t, u):
                if u % 2:
                    return
                if not isinstance(t, int) or t >= 4:
                    pool.wait_ge(s.ps_p, job(t - 2))
                pair = (t // PAIR_STEPS) % (HEADS_C // 2)
                cols = (pair * 2 + (t % 8) // 4) * DIM_C
                pool.tensor_copy(w_now[:, u // 2, :].rearrange("p (a d) -> p a d", a=2),
                                 over(w_sorted[:, u // 2, bass.ds(cols, DIM_C)], 1, 2)).then_inc(s.w_now, 1)

            def stage_q(t, u):
                hh = u % 2
                pair = t // PAIR_STEPS
                if hh == 0:
                    pool.wait_ge(s.lo, (pair + 1) * 8)
                freed(pool, s.ps_s, t)
                flat = q_hl[:].rearrange("p a b n -> p (a b n)")
                cols = (pair % 2) * 2 * SEQ + hh * SEQ + ((t % PAIR_STEPS) // 2) * P
                pool.tensor_copy(q_now[:, hh, :], flat[:, bass.ds(cols, P)]).then_inc(s.q_now, 1)

            pipeline(pool, STEPS_C, [(0, stage_weights), (17, stage_q)], unroll=4)

        @block.vector
        def _(dve):
            dve.wait_ge(w.c_loaded, w.c_count)
            src = w.wqk_c[:].rearrange("p (n k) -> p k n", k=2)
            for k in range(2):
                dve.tensor_copy(w_sorted[:, k, :], src[:, k, :]).then_inc(s.w_sorted, 1)

            def split_low(t, u):
                if u % 2:
                    return
                done(dve, s.hi, job(t))
                pair, head, half = job_place(t)
                cols = (pair % 2) * 2 * SEQ + head * SEQ + half * 512
                if u // 2 == 0:
                    here = q_hl[64:P].rearrange("p a b n -> p (a b n)")[:, bass.ds(cols, 512)]
                    dve.tensor_scalar(low[64:P, :], ps_p[64:P, :], float(DIM_C) ** -0.5, scaled_bias(t, 0)[64:P],
                                      ALU.mult, ALU.add).then_inc(s.whole, 1)
                    done(dve, s.whole, job(t) // 2)
                    dve.tensor_tensor(here, low[64:P, :], here.bitcast(F32), ALU.subtract).then_inc(s.lo, 1)
                else:
                    high = k_h[:].rearrange("p a b n -> p (a b n)")[:, bass.ds(cols, 512)]
                    dst = k_l[:].rearrange("p a b n -> p (a b n)")[:, bass.ds(cols, 512)]
                    dve.scalar_tensor_tensor(out=dst, in0=ps_p[:], scalar=scaled_bias(t, 1), in1=high.bitcast(F32),
                                             op0=ALU.add, op1=ALU.subtract).then_inc(s.lo, 1)

            def top(t, u):
                done(dve, s.ps_s, t)
                freed(dve, s.prob, t, 4)
                dve.tensor_reduce(neg_top[:, u, :], ps_s[u % 2][:], AX_X, ALU.max, negate=True).then_inc(s.neg_top, 1)

            def copy_b(t, u):
                done(dve, s.ps_tb, t)
                freed(dve, s.ps_o, t)
                dve.tensor_copy(prob_t[:, u % 2, 4:8, :].rearrange("p j n -> p (j n)"), ps_t[1][:]).then_inc(s.pt_b, 1)

            def inverse(t, u):
                done(dve, s.prob, t)
                freed(dve, s.o, t, 4)
                dve.reciprocal(inv[:, u, :], total[:, u, :]).then_inc(s.inv, 1)

            def scale_out(t, u):
                done(dve, s.ps_o, t)
                done(dve, s.inv, t)
                pair = t // PAIR_STEPS
                flat = vo[:].rearrange("p c t n -> p (c t n)")
                base = pair * (SEQ_TILES * P) + ((t % PAIR_STEPS) // 2) * P + (u % 2) * DIM_C
                dve.tensor_scalar(flat[:, bass.ds(base, DIM_C)], ps_o[:, 0:DIM_C], inv[:, u, :], None,
                                  ALU.mult).then_inc(s.o, 1)

            pipeline(dve, STEPS_C, [(18, inverse), (20, scale_out), (17, top), (18, copy_b), (2, split_low)],
                     unroll=4)

RSQRT2 = 2 ** -0.5


def l1_attention_out(nc, g, w, xn, vo):
    with ExitStack() as ctx:
        def sb(name, shape, dt=F32):
            return ctx.enter_context(nc.sbuf_tensor("co_" + name, shape, dt))

        def pb(name):
            return ctx.enter_context(nc.psum_tensor("co_" + name, [P, 512], F32))

        o_now = sb("o_now", [P, 2, INNER])
        o_t = sb("o_t", [P, 2, INNER])
        gamma = sb("gamma", [P, P])
        beta = sb("beta", [P, P])
        stats = sb("stats", [P, 2, 6])
        mean_var = sb("mean_var", [P, 4, 2])
        veps = sb("veps", [P, 2, 1])
        rstd = sb("rstd", [P, 2, 1])
        y = sb("y", [P, 2, P])
        scaled = sb("scaled", [P, 2, P])
        base = sb("base", [P, 2, P])
        z = sb("z", [P, 4, P])
        stats2 = sb("stats2", [P, 2, 6])
        mean_var2 = sb("mean_var2", [P, 4, 2])
        veps2 = sb("veps2", [P, 2, 1])
        rstd2 = sb("rstd2", [P, 2, 1])
        r = sb("r", [P, 2, P])
        ps_t = [pb(f"ps_t{u}") for u in range(2)]
        ps_y = [pb(f"ps_y{u}") for u in range(4)]
        s = sems(ctx, nc, "co_", "gamma beta o_now ps_t o_t ps_y stats mean_var veps rstd y scaled base z stats2 "
                 "mean_var2 veps2 rstd2 r x")
        block = ctx.enter_context(nc.Block())

        @block.tensor
        def _(pe):
            def transpose_o(t, u4):
                u = u4 % 2
                done(pe, s.o_now, t)
                freed(pe, s.o_t, t)
                for c in range(CHUNKS):
                    mm = pe.transpose(ps_t[u][:, c * P:(c + 1) * P], o_now[:, u, c * P:(c + 1) * P], g.ident[:])
                mm.then_inc(s.ps_t, 1)

            def project(t, u4):
                u = u4 % 2
                done(pe, s.o_t, t)
                freed(pe, s.y, t, 4)
                for c in range(CHUNKS):
                    pe.matmul(ps_y[u4][:, 0:P], o_t[:, u, c * P:(c + 1) * P], w.wout_c[:, c, :], start=(c == 0), stop=False)
                pe.matmul(ps_y[u4][:, 0:P], g.ones_row[:], w.bout_c[:], start=False, stop=True).then_inc(s.ps_y, 1)

            pipeline(pe, TILES, [(1, transpose_o), (2, project)], unroll=4)

        @block.scalar
        def _(act):
            def stage_o(t, u4):
                u = u4 % 2
                freed(act, s.ps_t, t)
                slot = (t // SEQ_TILES) * CHUNKS
                src = vo[:, bass.ds(slot, CHUNKS), bass.ds(t % SEQ_TILES, 1), :]
                act.activation(o_now[:, u, :].rearrange("p (c n) -> p c n", c=CHUNKS),
                               src.rearrange("p c a n -> p c (a n)"), ACT.Copy).then_inc(s.o_now, 1)

            def copy_o(t, u4):
                u = u4 % 2
                done(act, s.ps_t, t)
                freed(act, s.ps_y, t)
                act.activation(o_t[:, u, :], ps_t[u][:], ACT.Copy).then_inc(s.o_t, 1)

            pipeline(act, TILES, [(0, stage_o), (1, copy_o)], unroll=4)

        @block.gpsimd
        def _(pool):
            def rstd_y(t, u4):
                u = u4 % 2
                done(pool, s.veps, t)
                freed(pool, s.y, t)
                pool.tensor_tensor(rstd[:, u, :], veps[:, u, :], g.minus_half[:], ALU.pow).then_inc(s.rstd, 1)

            def affine(t, u4):
                u = u4 % 2
                done(pool, s.y, t)
                pool.tensor_tensor(scaled[:, u, :], y[:, u, :], gamma[:], ALU.mult).then_inc(s.scaled, 1)
                done(pool, s.scaled, t)
                done(pool, s.base, t)
                freed(pool, s.r, t, 4)
                pool.tensor_tensor(z[:, u4, :], scaled[:, u, :], base[:, u, :], ALU.add).then_inc(s.z, 1)

            def rstd_z(t, u4):
                u = u4 % 2
                done(pool, s.veps2, t)
                freed(pool, s.r, t)
                pool.tensor_tensor(rstd2[:, u, :], veps2[:, u, :], g.minus_half[:], ALU.pow).then_inc(s.rstd2, 1)

            def residual(t, u4):
                done(pool, s.r, t)
                pool.tensor_tensor(g.x[:, t, :], g.x[:, t, :], r[:, u4 % 2, :], ALU.add).then_inc(s.x, 1)

            pipeline(pool, TILES, [(4, rstd_y), (7, rstd_z), (5, affine), (8, residual)], unroll=4)

        @block.vector
        def _(dve):
            dve.tensor_scalar(gamma[:], w.gamma_c[:], RSQRT2, None, ALU.mult).then_inc(s.gamma, 1)
            dve.tensor_scalar(beta[:], w.beta_c[:], RSQRT2, None, ALU.mult).then_inc(s.beta, 1)
            dve.wait_ge(s.gamma, 1)
            dve.wait_ge(s.beta, 1)

            def stats_y(t, u4):
                done(dve, s.ps_y, t)
                dve.bn_stats(stats[:, u4 % 2, :], ps_y[u4][:, 0:P]).then_inc(s.stats, 1)
                freed(dve, s.y, t, 4)
                done(dve, s.stats, t)

            def variance_y(t, u4):
                u = u4 % 2
                done(dve, s.mean_var, t)
                freed(dve, s.rstd, t)
                dve.tensor_scalar(veps[:, u, :], mean_var[:, u4, 1:2], EPS, None, ALU.add).then_inc(s.veps, 1)

            def aggregate_y(t, u4):
                dve.bn_aggr(mean_var[:, u4, :], stats[:, u4 % 2, :]).then_inc(s.mean_var, 1)

            def normalize_y(t, u4):
                u = u4 % 2
                done(dve, s.rstd, t)
                freed(dve, s.scaled, t)
                dve.tensor_scalar(y[:, u, :], ps_y[u4][:, 0:P], mean_var[:, u4, 0:1], rstd[:, u, :],
                                  ALU.subtract, ALU.mult).then_inc(s.y, 1)
                freed(dve, s.z, t)
                dve.scalar_tensor_tensor(out=base[:, u, :], in0=xn[:, t, :], scalar=RSQRT2, in1=beta[:],
                                         op0=ALU.mult, op1=ALU.add).then_inc(s.base, 1)

            def stats_z(t, u4):
                done(dve, s.z, t)
                dve.bn_stats(stats2[:, u4 % 2, :], z[:, u4, :]).then_inc(s.stats2, 1)
                freed(dve, s.r, t, 4)
                done(dve, s.stats2, t)

            def variance_z(t, u4):
                u = u4 % 2
                done(dve, s.mean_var2, t)
                freed(dve, s.rstd2, t)
                dve.tensor_scalar(veps2[:, u, :], mean_var2[:, u4, 1:2], EPS, None, ALU.add).then_inc(s.veps2, 1)

            def aggregate_z(t, u4):
                dve.bn_aggr(mean_var2[:, u4, :], stats2[:, u4 % 2, :]).then_inc(s.mean_var2, 1)

            def normalize_z(t, u4):
                u = u4 % 2
                done(dve, s.rstd2, t)
                freed(dve, s.x, t)
                dve.tensor_scalar(r[:, u, :], z[:, u4, :], mean_var2[:, u4, 0:1], rstd2[:, u, :],
                                  ALU.subtract, ALU.mult).then_inc(s.r, 1)

            pipeline(dve, TILES, [(3, stats_y), (4, variance_y), (3, aggregate_y), (6, stats_z), (7, variance_z),
                                  (6, aggregate_z), (5, normalize_y), (8, normalize_z)], unroll=4)


def l1_ffn(nc, g, w):
    with ExitStack() as ctx:
        h_all = ctx.enter_context(nc.sbuf_tensor("d_h_all", [P, TOKENS], F32))
        weight = ctx.enter_context(nc.sbuf_tensor("d_weight", [P, TILES, EXPERTS], F32))
        mixed = ctx.enter_context(nc.sbuf_tensor("d_mixed", [P, TILES, P], F32))
        with ExitStack() as mid:
            logits = mid.enter_context(nc.sbuf_tensor("d_logits", [P, TILES, EXPERTS], F32))
            router_logits(nc, g, w, h_all, logits)
            route(nc, g, w, logits, weight)
        experts(nc, g, w, h_all, weight, mixed)
        normalize_all(nc, g, "d_out_", mixed, g.x, True)


def router_logits(nc, g, w, h_all, logits):
    with ExitStack() as ctx:
        def sb(name, shape, dt=F32):
            return ctx.enter_context(nc.sbuf_tensor("dr_" + name, shape, dt))

        stats = sb("stats", [P, 2, 6])
        mean_var = sb("mean_var", [P, 4, 2])
        veps = sb("veps", [P, 2, 1])
        rstd = sb("rstd", [P, 2, 1])
        h = sb("h", [P, 2, P])
        h_t = sb("h_t", [P, 2, P])
        ps_h = [ctx.enter_context(nc.psum_tensor(f"dr_ps_h{u}", [P, 512], F32)) for u in range(2)]
        ps_l = [ctx.enter_context(nc.psum_tensor(f"dr_ps_l{u}", [P, 512], F32)) for u in range(2)]
        s = sems(ctx, nc, "dr_", "stats mean_var veps rstd h ps_h h_t h_all ps_l logits")
        block = ctx.enter_context(nc.Block())

        @block.tensor
        def _(pe):
            pe.wait_ge(w.d_loaded, w.d_count)

            def transpose_h(t, u4):
                u = u4 % 2
                done(pe, s.h, t)
                freed(pe, s.h_t, t)
                pe.transpose(ps_h[u][:, 0:P], h[:, u, :], g.ident[:]).then_inc(s.ps_h, 1)

            def project(t, u4):
                u = u4 % 2
                done(pe, s.h_t, t)
                freed(pe, s.logits, t)
                pe.matmul(ps_l[u][:, 0:EXPERTS], h_t[:, u, :], w.router_d[:], start=True, stop=True).then_inc(s.ps_l, 1)

            pipeline(pe, TILES, [(2, transpose_h), (2, project)], unroll=4)

        @block.scalar
        def _(act):
            def copy_h(t, u4):
                u = u4 % 2
                done(act, s.ps_h, t)
                freed(act, s.ps_l, t)
                freed(act, s.h_all, t)
                act.activation(h_t[:, u, :], ps_h[u][:, 0:P], ACT.Copy).then_inc(s.h_t, 1)

            def copy_logits(t, u4):
                done(act, s.ps_l, t)
                act.activation(logits[:, t, :], ps_l[u4 % 2][:, 0:EXPERTS], ACT.Copy).then_inc(s.logits, 1)

            pipeline(act, TILES, [(2, copy_h), (3, copy_logits)], unroll=4)

        @block.gpsimd
        def _(pool):
            def inverse(t, u4):
                u = u4 % 2
                done(pool, s.veps, t)
                freed(pool, s.h, t)
                pool.tensor_tensor(rstd[:, u, :], veps[:, u, :], g.minus_half[:], ALU.pow).then_inc(s.rstd, 1)

            def keep_h(t, u4):
                done(pool, s.h_t, t)
                pool.tensor_copy(h_all[:, bass.ts(t, P)], h_t[:, u4 % 2, :]).then_inc(s.h_all, 1)

            pipeline(pool, TILES, [(1, inverse), (3, keep_h)], unroll=4)

        @block.vector
        def _(dve):
            def stats_of(t, u4):
                dve.bn_stats(stats[:, u4 % 2, :], g.x[:, t, :]).then_inc(s.stats, 1)
                freed(dve, s.h, t, 4)
                done(dve, s.stats, t)

            def variance(t, u4):
                u = u4 % 2
                done(dve, s.mean_var, t)
                freed(dve, s.rstd, t)
                dve.tensor_scalar(veps[:, u, :], mean_var[:, u4, 1:2], EPS, None, ALU.add).then_inc(s.veps, 1)

            def aggregate(t, u4):
                dve.bn_aggr(mean_var[:, u4, :], stats[:, u4 % 2, :]).then_inc(s.mean_var, 1)

            def normalize(t, u4):
                u = u4 % 2
                done(dve, s.rstd, t)
                freed(dve, s.ps_h, t)
                dve.tensor_scalar(h[:, u, :], g.x[:, t, :], mean_var[:, u4, 0:1], rstd[:, u, :],
                                  ALU.subtract, ALU.mult).then_inc(s.h, 1)

            pipeline(dve, TILES, [(0, stats_of), (1, variance), (0, aggregate), (2, normalize)], unroll=4)


def route(nc, g, w, logits, weight):
    with ExitStack() as ctx:
        def sb(name, shape, dt=F32):
            return ctx.enter_context(nc.sbuf_tensor("dw_" + name, shape, dt))

        COLS = TILES * EXPERTS
        best = sb("best", [P, TILES])
        shifted = sb("shifted", [P, TILES, EXPERTS])
        e = sb("e", [P, TILES, EXPERTS])
        total = sb("total", [P, TILES])
        inv = sb("inv", [P, TILES])
        left = sb("left", [P, 2, TILES, EXPERTS])
        top = sb("top", [P, 2, TILES])
        tie = sb("tie", [P, 2, TILES, EXPERTS])
        place = sb("place", [P, 2, TILES, EXPERTS])
        first = sb("first", [P, 2, TILES])
        chosen = sb("chosen", [P, 2, TILES, EXPERTS])
        chosen_bf = sb("chosen_bf", [P, 2, TILES, EXPERTS], BF16)
        counts = sb("counts", [P, 2, 2, TILES, EXPERTS])
        rank = sb("rank", [P, 2, TILES, EXPERTS])
        kept = sb("kept", [P, 2, TILES, EXPERTS])
        valued = sb("valued", [P, 2, TILES, EXPERTS])
        ps_before = [ctx.enter_context(nc.psum_tensor(f"dw_before{k}", [P, COLS], F32)) for k in range(2)]
        ps_count = [ctx.enter_context(nc.psum_tensor(f"dw_count{k}", [P, COLS], F32)) for k in range(2)]
        s = sems(ctx, nc, "dw_", "shifted exp chosen ps_before ps_count step")
        block = ctx.enter_context(nc.Block())

        @block.scalar
        def _(act):
            act.wait_ge(s.shifted, 1)
            act.activation(e[:], shifted[:], ACT.Exp).then_inc(s.exp, 1)

        @block.tensor
        def _(pe):
            pe.wait_ge(w.d_loaded, w.d_count)
            for k in range(2):
                pe.wait_ge(s.chosen, k + 1)
                cols = chosen_bf[:, k, :, :].rearrange("p t e -> p (t e)")
                pe.matmul(ps_before[k][:], w.earlier_d[:], cols, start=True, stop=True).then_inc(s.ps_before, 1)
                pe.matmul(ps_count[k][:], w.ones_d[:], cols, start=True, stop=True).then_inc(s.ps_count, 1)

        @block.vector
        def _(dve):
            steps = [0]

            def then(instruction):
                steps[0] += 1
                instruction.then_inc(s.step, 1)
                dve.wait_ge(s.step, steps[0])

            def by_tile(ap):
                return over(ap, 2, EXPERTS)

            iota = over(w.iota_d[:], 1, TILES)
            then(dve.tensor_reduce(best[:], logits[:], AX_X, ALU.max))
            dve.tensor_tensor(shifted[:], logits[:], by_tile(best[:]), ALU.subtract).then_inc(s.shifted, 1)
            dve.wait_ge(s.exp, 1)
            then(dve.tensor_reduce(total[:], e[:], AX_X, ALU.add))
            then(dve.reciprocal(inv[:], total[:]))
            then(dve.tensor_tensor(left[:, 0], e[:], by_tile(inv[:]), ALU.mult))
            for k in range(2):
                then(dve.tensor_reduce(top[:, k], left[:, k], AX_X, ALU.max))
                then(dve.tensor_tensor(tie[:, k], left[:, k], by_tile(top[:, k]), ALU.is_equal))
                then(dve.tensor_tensor(place[:, k], tie[:, k], iota, ALU.mult))
                then(dve.tensor_reduce(first[:, k], place[:, k], AX_X, ALU.min))
                then(dve.tensor_tensor(chosen[:, k], iota, by_tile(first[:, k]), ALU.is_equal))
                dve.tensor_copy(chosen_bf[:, k], chosen[:, k]).then_inc(s.chosen, 1)
                if k == 0:
                    then(dve.scalar_tensor_tensor(out=left[:, 1].rearrange("p t e -> p (t e)"),
                                                  in0=chosen[:, 0].rearrange("p t e -> p (t e)"), scalar=-2.0,
                                                  in1=left[:, 0].rearrange("p t e -> p (t e)"),
                                                  op0=ALU.mult, op1=ALU.add))
            for k in range(2):
                dve.wait_ge(s.ps_count, k + 1)
                then(dve.tensor_copy(counts[:, 0, k].rearrange("p t e -> p (t e)"), ps_count[k][:]))
            reach, at = 1, 0
            while reach < TILES:
                src, dst = counts[:, at], counts[:, 1 - at]
                dve.tensor_copy(dst[:, :, 0:reach, :], src[:, :, 0:reach, :]).then_inc(s.step, 1)
                steps[0] += 1
                then(dve.tensor_tensor(dst[:, :, reach:, :], src[:, :, reach:, :], src[:, :, :TILES - reach, :], ALU.add))
                reach, at = 2 * reach, 1 - at
            for k in range(2):
                dve.wait_ge(s.ps_before, k + 1)
                before = ps_before[k][:].rearrange("p (t e) -> p t e", e=EXPERTS)
                dve.tensor_copy(rank[:, k, 0:1, :], before[:, 0:1, :]).then_inc(s.step, 1)
                steps[0] += 1
                then(dve.tensor_tensor(rank[:, k, 1:, :], counts[:, at, k, 0:TILES - 1, :], before[:, 1:, :], ALU.add))
            then(dve.tensor_scalar(kept[:], rank[:], float(CAPACITY), None, ALU.is_lt))
            then(dve.tensor_tensor(kept[:], kept[:], chosen[:], ALU.mult))
            for k in range(2):
                then(dve.tensor_tensor(valued[:, k], kept[:, k], by_tile(top[:, k]), ALU.mult))
            then(dve.tensor_tensor(weight[:], valued[:, 0], valued[:, 1], ALU.add))


BLOCK = 512
BLOCKS = TOKENS // BLOCK
UNITS = EXPERTS * BLOCKS


def experts(nc, g, w, h_all, weight, mixed):
    with ExitStack() as ctx:
        def sb(name, shape, dt=F32):
            return ctx.enter_context(nc.sbuf_tensor("de_" + name, shape, dt))

        mats = sb("mats", [P, 2, 3, P])
        silu = sb("silu", [P, 2, BLOCK])
        hidden = sb("hidden", [P, 2, BLOCK])
        ps_gate = [ctx.enter_context(nc.psum_tensor(f"de_ps_gate{u}", [P, BLOCK], F32)) for u in range(2)]
        ps_up = [ctx.enter_context(nc.psum_tensor(f"de_ps_up{u}", [P, BLOCK], F32)) for u in range(2)]
        ps_out = [ctx.enter_context(nc.psum_tensor(f"de_ps_out{u}", [P, BLOCK], F32)) for u in range(2)]
        s = sems(ctx, nc, "de_", "zeroed ps_gate ps_up silu hidden ps_out mixed")
        loaded = [ctx.enter_context(nc.semaphore(f"de_loaded{u}")) for u in range(2)]
        block = ctx.enter_context(nc.Block())

        @block.sync
        def _(sp):
            def load(e, parity):
                for n, m in enumerate((w.gate, w.up, w.down)):
                    sp.dma_start(mats[:, parity, n, :], m[bass.ds(e, 1)].rearrange("a p n -> p (a n)")) \
                        .then_inc(loaded[parity], 16)

            load(0, 0)
            load(1, 1)
            with sp.Fori(2, EXPERTS - 1, 2) as e:
                for parity in range(2):
                    sp.wait_ge(s.ps_out, (e + parity - 1) * BLOCKS)
                    load(e + parity, parity)

        @block.tensor
        def _(pe):
            def hidden_of(t, u16):
                u, parity, blk = u16 % 2, u16 // BLOCKS, u16 % BLOCKS
                if blk == 0:
                    pe.wait_ge(loaded[parity], 48 * (t // (2 * BLOCKS) + 1))
                rhs = h_all[:, blk * BLOCK:(blk + 1) * BLOCK]
                freed(pe, s.silu, t)
                pe.matmul(ps_gate[u][:], mats[:, parity, 0, :], rhs, start=True, stop=True).then_inc(s.ps_gate, 1)
                freed(pe, s.hidden, t)
                pe.matmul(ps_up[u][:], mats[:, parity, 1, :], rhs, start=True, stop=True).then_inc(s.ps_up, 1)

            def out_of(t, u16):
                u, parity = u16 % 2, u16 // BLOCKS
                done(pe, s.hidden, t)
                freed(pe, s.mixed, t)
                for c in range(BLOCK // P):
                    mm = pe.matmul(ps_out[u][:, c * P:(c + 1) * P], hidden[:, u, c * P:(c + 1) * P], mats[:, parity, 2, :],
                                   start=True, stop=True)
                mm.then_inc(s.ps_out, 1)

            pipeline(pe, UNITS, [(0, hidden_of), (1, out_of)], unroll=2 * BLOCKS)

        @block.scalar
        def _(act):
            def silu_of(t, u):
                done(act, s.ps_gate, t)
                freed(act, s.hidden, t)
                act.activation(silu[:, u, :], ps_gate[u][:], ACT.Silu).then_inc(s.silu, 1)

            pipeline(act, UNITS, [(0, silu_of)])

        @block.vector
        def _(dve):
            dve.memset(mixed[:], 0.0).then_inc(s.zeroed, 1)
            dve.wait_ge(s.zeroed, 1)

            def gated(t, u8):
                u = u8 % 2
                done(dve, s.silu, t)
                done(dve, s.ps_up, t)
                freed(dve, s.ps_out, t)
                dve.tensor_tensor(hidden[:, u, :], silu[:, u, :], ps_up[u][:], ALU.mult).then_inc(s.hidden, 1)

            def accumulate(t, u8):
                u = u8 % 2
                done(dve, s.ps_out, t)
                tile = (t % BLOCKS) * (BLOCK // P)
                expert = t // BLOCKS
                w_flat = weight[:].rearrange("p t e -> p (t e)")
                m_flat = mixed[:].rearrange("p t n -> p (t n)")
                if not isinstance(t, int) or t >= BLOCKS:
                    dve.wait_ge(s.mixed, t - BLOCKS + 1)
                for c in range(BLOCK // P):
                    at = m_flat[:, bass.ds((tile + c) * P, P)]
                    m = dve.scalar_tensor_tensor(out=at, in0=ps_out[u][:, c * P:(c + 1) * P],
                                                 scalar=w_flat[:, bass.ds((tile + c) * EXPERTS + expert, 1)],
                                                 in1=at, op0=ALU.mult, op1=ALU.add)
                m.then_inc(s.mixed, 1)

            pipeline(dve, UNITS, [(0, gated), (1, accumulate)], unroll=BLOCKS, depth=BLOCKS)


def build(nc, a, out):
    with ExitStack() as ctx:
        def sb(name, shape, dt=F32):
            return ctx.enter_context(nc.sbuf_tensor(name, shape, dt))

        def row(ap):
            return ap.rearrange("(a n) -> a n", a=1)

        x = sb("x", [P, TILES, P])
        ident = sb("ident", [P, P])
        ones_row = sb("ones_row", [1, P])
        minus_half = sb("minus_half", [P, 1])
        s = sems(ctx, nc, "g_", "ident0 ident_ready consts_ready ones_ready x_loaded small_loaded tab_loaded stored c_loaded b_loaded d_loaded")
        g = Group()
        g.x, g.ident, g.ones_row, g.minus_half = x, ident, ones_row, minus_half
        g.ident_ready, g.consts_ready, g.x_loaded = s.ident_ready, s.consts_ready, s.x_loaded
        small = [("wq_a", a["L0_attn_Wq"], [P, P]), ("wdown", a["L0_attn_Wdown"], [P, LATENT]),
                 ("wup", a["L0_attn_Wup"], [LATENT, 2 * P]), ("wout_a", a["L0_attn_Wout"], [P, P]),
                 ("bq_a", row(a["L0_attn_bq"]), [1, P]), ("bup", row(a["L0_attn_bup"]), [1, 2 * P]),
                 ("bout_a", row(a["L0_attn_bout"]), [1, P]),
                 ("bdown", a["L0_attn_bdown"].rearrange("(n a) -> n a", a=1), [LATENT, 1])]
        for_c = [("wqk_c", a["L1_attn_W_qk"], [P, 2 * INNER]), ("wv_c", a["L1_attn_W_v"], [P, INNER]),
                 ("bv_c", row(a["L1_attn_b_v"]).to_broadcast([P, INNER]), [P, INNER]), ("bout_c", row(a["L1_attn_b_out"]), [1, P]),
                 ("wout_c", a["L1_attn_W_out"].rearrange("(c p) n -> p c n", p=P), [P, CHUNKS, P]),
                 ("gamma_c", row(a["L1_attn_ln_gamma"]).to_broadcast([P, P]), [P, P]),
                 ("beta_c", row(a["L1_attn_ln_beta"]).to_broadcast([P, P]), [P, P])]
        bqk_c = sb("bqk_c", [P, HEADS_C, 2])
        bias_c = sb("bias_c", [P, 2, HEADS_C])
        w = Group()
        w.bias_c, w.c_loaded, w.c_count = bias_c, s.c_loaded, 16 * (len(for_c) + 2)
        w.small_loaded, w.small_count = s.small_loaded, 16 * len(small)
        dst = {n: sb(n, shape) for n, _, shape in small}
        w.wq_a, w.wdown, w.wup, w.wout_a, w.bq_a, w.bup, w.bout_a, w.bdown = (dst[n] for n, _, _ in small)
        dst_c = {n: sb(n, shape) for n, _, shape in for_c}
        w.wqk_c, w.wv_c, w.bv_c, w.bout_c, w.wout_c, w.gamma_c, w.beta_c = (dst_c[n] for n, _, _ in for_c)
        tab = Group()
        tab.rope_a, tab.loaded = sb("rope_a", [P, SEQ_TILES, 2 * DIM_A]), s.tab_loaded
        x_dram = a["L0_attn_x"].rearrange("b (n p) d -> b p n d", p=P)
        out_dram = out.rearrange("b (n p) d -> b p n d", p=P)
        shapes_b = [("rope_b", [P, 4, SEQ_TILES, DIM_B], F32), ("mask_b", [P, (SEQ_TILES + 1) * P], BF16), ("carry", [P, SEQ_TILES], F32),
                    ("centre", [P, P], F32),
                    ("mean_col", [P, 1], F32), ("zeros", [P, P], F32), ("ident_bf", [P, P], BF16)]
        for_d = [("router_d", a["L1_ffn_router_w"], [P, EXPERTS], F32), ("earlier_d", a["tab_earlier"], [P, P], BF16),
                 ("ones_d", a["tab_ones"], [P, P], BF16), ("iota_d", a["tab_iota"], [P, EXPERTS], F32)]
        d = {n: sb(n, shape, dt) for n, _, shape, dt in for_d}
        w.router_d, w.earlier_d, w.ones_d, w.iota_d = (d[n] for n, _, _, _ in for_d)
        w.d_loaded, w.d_count = s.d_loaded, 16 * len(for_d)
        w.gate, w.up, w.down = a["L1_ffn_gate_w"], a["L1_ffn_up_w"], a["L1_ffn_down_w"]

        with nc.Block() as block:
            @block.sync
            def _(sp):
                sp.dma_start(x[:, 0:SEQ_TILES, :], x_dram[0]).then_inc(s.x_loaded, 16)
                for n, src, _ in small:
                    sp.dma_start(dst[n][:], src).then_inc(s.small_loaded, 16)
                sp.dma_start(tab.rope_a[:], a["tab_rope_a"]).then_inc(s.tab_loaded, 16)
                for b in range(1, BATCHES):
                    sp.dma_start(x[:, b * SEQ_TILES:(b + 1) * SEQ_TILES, :], x_dram[b]).then_inc(s.x_loaded, 16)
                for n, src, _ in for_c:
                    sp.dma_start(dst_c[n][:], src).then_inc(s.c_loaded, 16)
                for n, src, _, _ in for_d:
                    sp.dma_start(d[n][:], src).then_inc(s.d_loaded, 16)
                for twice in range(2):
                    sp.dma_start(bqk_c[twice * DIM_C:(twice + 1) * DIM_C],
                                 a["L1_attn_b_qk"].rearrange("(h d k) -> d h k", k=2, d=DIM_C)).then_inc(s.c_loaded, 16)

            @block.gpsimd
            def _(pool):
                pool.memset(ident[:], 0.0).then_inc(s.ident0, 1)
                pool.memset(minus_half[:], -0.5)
                pool.memset(ones_row[:], 1.0).then_inc(s.consts_ready, 1)
                pool.wait_ge(s.ident0, 1)
                pool.affine_select(out=ident[:], in_=ident[:], compare_op=ALU.not_equal, fill=1.0, base=0,
                                   pattern=[[-1, P]], channel_multiplier=1).then_inc(s.ident_ready, 1)

        with ExitStack() as first_two:
            def sb2(name, shape, dt=F32):
                return first_two.enter_context(nc.sbuf_tensor(name, shape, dt))

            b = {n: sb2(n, shape, dt) for n, shape, dt in shapes_b}
            w.wqkv_b = [sb2(f"wqkv_b{n}", [P, 3 * INNER]) for n in range(LAYERS)]
            w.wo_b = [sb2(f"wo_b{n}", [P, CHUNKS, P]) for n in range(LAYERS)]
            w.w1_b = [sb2(f"w1_b{n}", [P, 2 * HID_B]) for n in range(LAYERS)]
            w.w2_b = [sb2(f"w2_b{n}", [P, 3, P]) for n in range(LAYERS)]
            w.b1_b = sb2("b1_b", [1, LAYERS, 2 * HID_B])
            w.b2_b = sb2("b2_b", [1, LAYERS, P])
            w.ln_b = sb2("ln_b", [P, LAYERS, 2])
            w.scales_b = sb2("scales_b", [P, LAYERS, 4, DIM_B])
            tab.rope_b, tab.mask_b = b["rope_b"], b["mask_b"]
            g.carry, g.centre = b["carry"], b["centre"]
            g.mean_col, g.zeros, g.ident_bf = b["mean_col"], b["zeros"], b["ident_bf"]
            loads = [(b[n][:], a["tab_" + n]) for n, _, _ in shapes_b]
            last = HID_B - 2 * P
            half = DIM_B // 2
            for n in range(LAYERS):
                loads += [(w.wqkv_b[n][:], a["L0_ffn_wqkv"][n]),
                          (w.wo_b[n][:], a["L0_ffn_wo"][n].rearrange("(c p) n -> p c n", p=P)),
                          (w.w1_b[n][:], a["L0_ffn_w1"][n]),
                          (w.w2_b[n][:, 0:2, :], a["L0_ffn_w2"][n, 0:2 * P].rearrange("(c p) n -> p c n", p=P)),
                          (w.w2_b[n][0:last, 2, :], a["L0_ffn_w2"][n, 2 * P:HID_B])]
            loads += [(w.b1_b[:], a["L0_ffn_b1"].rearrange("(a l) n -> a l n", a=1)),
                      (w.b2_b[:], a["L0_ffn_b2"].rearrange("(a l) n -> a l n", a=1))]
            for k, name in ((0, "L0_ffn_ln_g"), (1, "L0_ffn_ln_b")):
                loads.append((w.ln_b[:, :, k], a[name].rearrange("l n -> n l")))
            for k, name in ((0, "L0_ffn_q_scale"), (1, "L0_ffn_k_scale")):
                src = a[name].rearrange("(a l) d -> a l d", a=1).to_broadcast([P, LAYERS, DIM_B])
                loads += [(w.scales_b[:, :, 2 * k, :], src), (w.scales_b[:, :, 2 * k + 1, 0:half], src[:, :, half:]),
                          (w.scales_b[:, :, 2 * k + 1, half:], src[:, :, 0:half])]
            w.b_loaded, w.b_count = s.b_loaded, 16 * len(loads)

            with nc.Block() as block:
                @block.gpsimd
                def _(pool):
                    for n in range(LAYERS):
                        pool.memset(w.w2_b[n][:, 2, :], 0.0)

            with nc.Block() as block:
                @block.sync
                def _(sp):
                    for to, src in loads:
                        sp.dma_start(to, src, allow_slow_non_contiguous=True).then_inc(s.b_loaded, 16)

            l0_attention(nc, g, w, tab)
            with nc.Block() as block:
                @block.sync
                def _(sp):
                    sp.wait_ge(w.b_loaded, w.b_count)
            l0_ffn(nc, g, w, tab)

        with nc.Block() as block:
            @block.vector
            def _(dve):
                dve.wait_ge(w.c_loaded, w.c_count)
                dve.tensor_scalar(bias_c[:, 0, :], bqk_c[:, :, 0], float(DIM_C) ** -0.5, None, ALU.mult)
                dve.tensor_copy(bias_c[:, 1, :], bqk_c[:, :, 1])
        l1_attention(nc, g, w)
        l1_ffn(nc, g, w)

        with nc.Block() as block:
            @block.sync
            def _(sp):
                sp.wait_ge(s.x_loaded, 16 * BATCHES)
                sp.wait_ge(s.small_loaded, w.small_count)
                sp.wait_ge(s.tab_loaded, 16)
                sp.wait_ge(s.c_loaded, w.c_count)
                sp.wait_ge(s.d_loaded, w.d_count)
                for b in range(BATCHES):
                    sp.dma_start(out_dram[b], x[:, b * SEQ_TILES:(b + 1) * SEQ_TILES, :]).then_inc(s.stored, 16)
                sp.wait_ge(s.stored, 16 * BATCHES)


def tables():
    import numpy as np

    def by_tile(t):
        return np.ascontiguousarray(t.reshape(SEQ_TILES, P, -1).transpose(1, 0, 2))

    f = np.float32
    pos = np.arange(SEQ, dtype=f)
    inv = (f(1.0) / f(10000.0) ** (np.arange(0, DIM_A, 2, dtype=f) / f(DIM_A))).astype(f)
    angle = pos[:, None] * inv[None, :]
    cos, sin = np.cos(angle), np.sin(angle)
    rope_a = by_tile(np.concatenate([cos, cos, -sin, sin], axis=-1).astype(f))

    half = np.arange(0, DIM_B, 2, dtype=f)
    inv = f(1.0) / f(10000.0) ** (half / f(DIM_B))
    angle = (pos[:, None] * inv[None, :]).astype(f)
    base = ((half + f(0.4 * DIM_B)) / f(1.4 * DIM_B)).astype(f)
    power = ((pos - SEQ // 2) / f(WINDOW // 2)).astype(f)
    scale = (base[None, :] ** power[:, None]).astype(f)
    sign = np.concatenate([-np.ones(DIM_B // 2, f), np.ones(DIM_B // 2, f)])
    cos, sin, scale = (np.concatenate([m, m], axis=-1) for m in (np.cos(angle), np.sin(angle), scale))
    rope_b = np.stack([cos * scale, sign * sin * scale, cos / scale, sign * sin / scale]).astype(f)
    rope_b = np.ascontiguousarray(rope_b.reshape(4, SEQ_TILES, P, DIM_B).transpose(2, 0, 1, 3))

    bf16 = np.dtype("bfloat16")
    i, j = np.arange(P)[:, None] % WINDOW, np.arange(-WINDOW, WINDOW)[None, :]
    seen = (i >= j) & (i <= j + WINDOW)
    mask = np.stack([seen & (j >= 0)] + [seen] * SEQ_TILES, axis=1)
    mask_b = np.where(mask, f(0.0), f(-1e30)).astype(bf16).reshape(P, -1)

    carry = np.ones((P, SEQ_TILES), f)
    carry[:, SEQ_TILES - 1] = 0.0
    feature = np.arange(P)
    centre = (np.eye(P) - 1.0 / P).astype(f)
    iota = np.tile(np.arange(EXPERTS, dtype=f) - EXPERTS, (P, 1))
    earlier = (feature[:, None] < feature[None, :]).astype(bf16)
    return {"tab_iota": iota, "tab_earlier": earlier, "tab_ones": np.ones((P, P), bf16), "tab_rope_a": rope_a, "tab_rope_b": rope_b, "tab_mask_b": mask_b, "tab_carry": carry, 
            "tab_centre": centre, "tab_mean_col": np.full((P, 1), 1.0 / P, f),
            "tab_zeros": np.zeros((P, P), f), "tab_ident_bf": np.eye(P).astype(bf16)}


def kernel(**inputs):
    import numpy as np
    import concourse.bacc as bacc
    from concourse.bass_utils import run_bass_kernel_spmd

    nc = bacc.Bacc("TRN2", target_bir_lowering=False, num_devices=1)
    arrays, aps = {}, {}
    for name, value in [*inputs.items(), *tables().items()]:
        v = np.ascontiguousarray(value)
        arrays[name + "_dram"] = v
        aps[name] = nc.dram_tensor(name + "_dram", v.shape, mybir.dt.from_np(v.dtype), kind="ExternalInput").ap()
    out = nc.dram_tensor("out_dram", (BATCHES, SEQ, P), F32, kind="ExternalOutput").ap()
    build(nc, aps, out)
    r = run_bass_kernel_spmd(nc, [arrays], core_ids=[0])
    return r.results[0]["out_dram"]
```

```python
from collections import namedtuple
from contextlib import ExitStack

import concourse.bass as bass
from concourse import mybir

F32 = mybir.dt.float32
BF16 = mybir.dt.bfloat16
ALU = mybir.AluOpType
ACT = mybir.ActivationFunctionType
AX_X = mybir.AxisListType.X

P = 128
TOKENS = 4096
SEQ = 1024
TILES = TOKENS // P
SEQ_TILES = SEQ // P
BATCHES = TOKENS // SEQ
EPS = 1e-5

HEADS_A = 16
DIM_A = P // HEADS_A
LATENT = 32

LAYERS = 2
HEADS_B = 8
DIM_B = 64
INNER = HEADS_B * DIM_B
WINDOW = 64
KEYS_B = P + WINDOW
CHUNKS = INNER // P
HID_B = int(P * 4 * 2 / 3)

HEADS_C = 8
DIM_C = 64

EXPERTS = 16
CAPACITY = -(-TOKENS * 2 * 5 // (EXPERTS * 4))


class Group:
    pass


def sems(ctx, nc, prefix, names):
    found = [nc.alloc_semaphore(name=prefix + n) for n in names.split()]

    def clear():
        nc.clear_and_free_semaphores(found)
        nc.all_engine_barrier()

    ctx.callback(clear)
    return namedtuple("Semaphores", names)(*found)


def done(eng, sem, t):
    eng.wait_ge(sem, t + 1)


def freed(eng, sem, t, depth=2):
    if isinstance(t, int) and t < depth:
        return
    eng.wait_ge(sem, t - depth + 1)


def pipeline(eng, tiles, steps, unroll=2, depth=4, period=None):
    period = period or unroll
    first = -(-(max(lag for lag, _ in steps) + depth) // unroll) * unroll
    whole = (tiles - first) // unroll
    end = first + unroll * whole

    def one_round(i, k):
        for lag, step in steps:
            if not isinstance(i, int) or 0 <= i + k - lag < tiles:
                step(i + k - lag, (first + k - lag) % period)

    for r in range(first):
        one_round(r - r % unroll, r % unroll)
    if whole == 1:
        for k in range(unroll):
            one_round(first, k)
    elif whole > 1:
        with eng.Fori(first, end - unroll + 1, unroll) as i:
            for k in range(unroll):
                one_round(i, k)
    for r in range(end, tiles + max(lag for lag, _ in steps)):
        one_round(r - r % unroll, r % unroll)


def over(ap, axis, count):
    shape = list(ap.shape)
    shape.insert(axis, count)
    return ap.unsqueeze(axis).to_broadcast(shape)


def l0_attention(nc, g, w, tab):
    with ExitStack() as ctx:
        def sb(name, shape, dt=F32):
            return ctx.enter_context(nc.sbuf_tensor("a_" + name, shape, dt))

        def pb(name, shape, dt=F32):
            return ctx.enter_context(nc.psum_tensor("a_" + name, shape, dt))

        down_up = sb("down_up", [P, 3 * P])
        bias = sb("bias", [1, 3 * P])
        wdown_t = sb("wdown_t", [LATENT, P])
        stats = sb("stats", [P, 2, 6])
        mean_var = sb("mean_var", [P, 4, 2])
        rstd = sb("rstd", [P, 2, 1])
        veps = sb("veps", [P, 2, 1])
        h = sb("h", [P, 2, P])
        h_t = sb("h_t", [P, 2, P])
        qk_raw = sb("qk_raw", [P, 2, 2 * P])
        v = sb("v", [P, 4, P])
        turned_c = sb("turned_c", [P, 2, 2 * P])
        turned_s = sb("turned_s", [P, 2, 2 * P])
        qk = sb("qk", [P, 2, 2 * P])
        prod_qk = sb("prod_qk", [P, 2, HEADS_A * HEADS_A * DIM_A])
        score = sb("score", [P, 2, HEADS_A * HEADS_A])
        top = sb("top", [P, 2, HEADS_A])
        shifted = sb("shifted", [P, 2, HEADS_A * HEADS_A])
        prob = sb("prob", [P, 2, HEADS_A * HEADS_A])
        total = sb("total", [P, 2, HEADS_A])
        inv = sb("inv", [P, 2, HEADS_A])
        prod_pv = sb("prod_pv", [P, 2, HEADS_A * HEADS_A * DIM_A])
        o = sb("o", [P, 2, P])
        o_t = sb("o_t", [P, 2, P])
        stats2 = sb("stats2", [P, 2, 6])
        mean_var2 = sb("mean_var2", [P, 4, 2])
        rstd2 = sb("rstd2", [P, 2, 1])
        veps2 = sb("veps2", [P, 2, 1])
        y = sb("y", [P, 2, P])
        ps_h = pb("ps_h", [P, 512])
        ps_qkv = [pb(f"ps_qkv{u}", [P, 512]) for u in range(2)]
        ps_mix = pb("ps_mix", [P, 512])
        ps_out = [pb(f"ps_out{u}", [P, 512]) for u in range(4)]
        s = sems(ctx, nc, "a_", "wd_t wd_copy fold fold_w fold_b stats mean_var veps rstd h ps_h h_t ps_qkv qk_raw v "
                 "turn1 turn2 turn3 qk prod_qk score top shifted prob total inv prod_pv ps_mix o ps_o o_t "
                 "ps_out stats2 mean_var2 veps2 rstd2 y x")
        block = ctx.enter_context(nc.Block())

        def heads(ap):
            return ap.rearrange("p (h d) -> p h d", d=DIM_A)

        @block.tensor
        def _(pe):
            pe.wait_ge(g.ident_ready, 1)
            pe.wait_ge(w.small_loaded, w.small_count)
            pe.transpose(ps_h[0:LATENT, 0:P], w.wdown[:], g.ident[:]).then_inc(s.wd_t, 1)
            done(pe, s.wd_copy, 0)
            pe.matmul(ps_qkv[0][:, 0:2 * P], wdown_t[:], w.wup[:], start=True, stop=True)
            pe.matmul(ps_mix[0:1, 0:2 * P], w.bdown[:], w.wup[:], start=True, stop=True).then_inc(s.fold, 1)

            def transpose_h(t, u4):
                u = u4 % 2
                done(pe, s.h, t)
                freed(pe, s.h_t, t, 1)
                if isinstance(t, int) and t == 0:
                    done(pe, s.wd_copy, 0)
                freed(pe, s.o_t, t, 6)
                pe.transpose(ps_h[:, 0:P], h[:, u, :], g.ident[:]).then_inc(s.ps_h, 1)

            def project(t, u4):
                u = u4 % 2
                if isinstance(t, int) and t == 0:
                    pe.wait_ge(s.fold_w, 2)
                    pe.wait_ge(s.fold_b, 2)
                done(pe, s.h_t, t)
                freed(pe, s.v, t)
                pe.matmul(ps_qkv[u][:, 0:3 * P], h_t[:, u, :], down_up[:], start=True, stop=False)
                pe.matmul(ps_qkv[u][:, 0:3 * P], g.ones_row[:], bias[:], start=False, stop=True).then_inc(s.ps_qkv, 1)

            def sum_values(t, u4):
                done(pe, s.prod_pv, t)
                freed(pe, s.o, t, 1)
                for head in range(HEADS_A):
                    mm = pe.matmul(ps_mix[:, 0:P], g.ident[:], prod_pv[:, u4 % 2, head * P:(head + 1) * P],
                                   start=(head == 0), stop=(head == HEADS_A - 1))
                mm.then_inc(s.ps_mix, 1)

            def transpose_o(t, u4):
                u = u4 % 2
                done(pe, s.o, t)
                if isinstance(t, int) and t + 5 >= TILES:
                    freed(pe, s.o_t, t, 1)
                if not isinstance(t, int) or t + 5 < TILES:
                    done(pe, s.h_t, t + 5)
                pe.transpose(ps_h[:, 0:P], o[:, u, :], g.ident[:]).then_inc(s.ps_o, 1)

            def project_out(t, u4):
                u = u4 % 2
                done(pe, s.o_t, t)
                freed(pe, s.y, t, 4)
                pe.matmul(ps_out[u4][:, 0:P], o_t[:, u, :], w.wout_a[:], start=True, stop=False)
                pe.matmul(ps_out[u4][:, 0:P], g.ones_row[:], w.bout_a[:], start=False, stop=True).then_inc(s.ps_out, 1)

            pipeline(pe, TILES, [(6, sum_values), (2, transpose_h), (2, project), (7, transpose_o), (7, project_out)], unroll=8, period=4)

        @block.scalar
        def _(act):
            done(act, s.wd_t, 0)
            act.activation(wdown_t[:], ps_h[0:LATENT, 0:P], ACT.Copy).then_inc(s.wd_copy, 1)
            act.wait_ge(w.small_loaded, w.small_count)
            act.activation(down_up[:, 0:P], w.wq_a[:], ACT.Copy).then_inc(s.fold_w, 1)
            act.activation(bias[:, 0:P], w.bq_a[:], ACT.Copy).then_inc(s.fold_b, 1)
            done(act, s.fold, 0)
            kv = "p (h a d) -> p a h d"
            act.activation(down_up[:, P:].rearrange("p (a h d) -> p a h d", a=2, d=DIM_A),
                           ps_qkv[0][:, 0:2 * P].rearrange(kv, a=2, d=DIM_A), ACT.Copy).then_inc(s.fold_w, 1)

            def copy_h(t, u4):
                u = u4 % 2
                done(act, s.ps_h, t)
                freed(act, s.ps_qkv, t)
                act.activation(h_t[:, u, :], ps_h[:, 0:P], ACT.Copy).then_inc(s.h_t, 1)

            def copy_qkv(t, u4):
                u = u4 % 2
                done(act, s.ps_qkv, t)
                freed(act, s.qk, t)
                act.activation(qk_raw[:, u, :], ps_qkv[u][:, 0:2 * P], ACT.Copy).then_inc(s.qk_raw, 1)
                freed(act, s.prod_pv, t, 4)
                act.activation(v[:, u4, :], ps_qkv[u][:, 2 * P:3 * P], ACT.Copy).then_inc(s.v, 1)

            def exp(t, u4):
                u = u4 % 2
                done(act, s.shifted, t)
                freed(act, s.prod_pv, t)
                freed(act, s.total, t)
                act.activation(prob[:, u, :], shifted[:, u, :], ACT.Exp, scale=float(DIM_A) ** -0.5).then_inc(s.prob, 1)

            def copy_o(t, u4):
                u = u4 % 2
                done(act, s.ps_o, t)
                freed(act, s.ps_out, t)
                act.activation(o_t[:, u, :], ps_h[:, 0:P], ACT.Copy).then_inc(s.o_t, 1)

            pipeline(act, TILES, [(5, exp), (2, copy_h), (2, copy_qkv), (7, copy_o)], unroll=8, period=4)

        @block.gpsimd
        def _(pool):
            def rstd_in(t, u4):
                u = u4 % 2
                done(pool, s.veps, t)
                freed(pool, s.h, t)
                pool.tensor_tensor(rstd[:, u, :], veps[:, u, :], g.minus_half[:], ALU.pow).then_inc(s.rstd, 1)

            def rotate(t, u4):
                u = u4 % 2
                n = t % SEQ_TILES
                done(pool, s.qk_raw, t)
                freed(pool, s.qk, t)
                src = qk_raw[:, u, :].rearrange("p (g a d) -> p g a d", a=2, d=DIM_A // 2)
                cos = tab.rope_a[:, n, 0:DIM_A]
                sin = tab.rope_a[:, n, DIM_A:2 * DIM_A].rearrange("p (a d) -> p a d", a=2)
                pool.tensor_tensor(heads(turned_c[:, u, :]), heads(qk_raw[:, u, :]),
                                   over(cos, 1, 2 * HEADS_A), ALU.mult).then_inc(s.turn1, 1)
                dst = turned_s[:, u, :].rearrange("p (g a d) -> p g a d", a=2, d=DIM_A // 2)
                for a, sem in ((0, s.turn2), (1, s.turn3)):
                    pool.tensor_tensor(dst[:, :, a, :], src[:, :, 1 - a, :], over(sin[:, a, :], 1, 2 * HEADS_A),
                                       ALU.mult).then_inc(sem, 1)
                done(pool, s.turn1, t)
                done(pool, s.turn2, t)
                done(pool, s.turn3, t)
                freed(pool, s.prod_qk, t)
                pool.tensor_tensor(qk[:, u, :], turned_c[:, u, :], turned_s[:, u, :], ALU.add).then_inc(s.qk, 1)

            def mix(t, u4):
                u = u4 % 2
                done(pool, s.prob, t)
                done(pool, s.v, t)
                freed(pool, s.ps_mix, t)
                out = prod_pv[:, u, :].rearrange("p (g h d) -> p g h d", g=HEADS_A, h=HEADS_A)
                p = over(prob[:, u, :].rearrange("p (h g) -> p g h", h=HEADS_A), 3, DIM_A)
                vs = over(heads(v[:, u4, :]), 2, HEADS_A)
                pool.tensor_tensor(out, p, vs, ALU.mult).then_inc(s.prod_pv, 1)

            def rstd_out(t, u4):
                u = u4 % 2
                done(pool, s.veps2, t)
                freed(pool, s.y, t)
                pool.tensor_tensor(rstd2[:, u, :], veps2[:, u, :], g.minus_half[:], ALU.pow).then_inc(s.rstd2, 1)

            def residual(t, u4):
                u = u4 % 2
                done(pool, s.y, t)
                pool.tensor_tensor(g.x[:, t, :], g.x[:, t, :], y[:, u, :], ALU.add).then_inc(s.x, 1)

            pool.wait_ge(g.consts_ready, 1)
            pool.wait_ge(tab.loaded, 16)
            pipeline(pool, TILES, [(1, rstd_in), (9, rstd_out), (10, residual), (5, mix), (3, rotate)], unroll=8, period=4)

        @block.vector
        def _(dve):
            done(dve, s.fold, 0)
            dve.tensor_tensor(bias[:, P:].rearrange("p (a h d) -> p a h d", a=2, d=DIM_A),
                              ps_mix[0:1, 0:2 * P].rearrange("p (h a d) -> p a h d", a=2, d=DIM_A),
                              w.bup[:].rearrange("p (h a d) -> p a h d", a=2, d=DIM_A), ALU.add).then_inc(s.fold_b, 1)

            def stats_in(t, u4):
                u = u4 % 2
                dve.bn_stats(stats[:, u, :], g.x[:, t, :]).then_inc(s.stats, 1)
                freed(dve, s.h, t, 4)
                done(dve, s.stats, t)

            def variance_in(t, u4):
                u = u4 % 2
                done(dve, s.mean_var, t)
                freed(dve, s.rstd, t)
                dve.tensor_scalar(veps[:, u, :], mean_var[:, u4, 1:2], EPS, None, ALU.add).then_inc(s.veps, 1)

            def aggregate_in(t, u4):
                u = u4 % 2
                dve.bn_aggr(mean_var[:, u4, :], stats[:, u, :]).then_inc(s.mean_var, 1)

            def normalize(t, u4):
                u = u4 % 2
                done(dve, s.rstd, t)
                freed(dve, s.ps_h, t)
                dve.tensor_scalar(h[:, u, :], g.x[:, t, :], mean_var[:, u4, 0:1], rstd[:, u, :],
                                  ALU.subtract, ALU.mult).then_inc(s.h, 1)

            def scores(t, u4):
                u = u4 % 2
                done(dve, s.qk, t)
                freed(dve, s.score, t)
                out = prod_qk[:, u, :].rearrange("p (h g d) -> p h g d", h=HEADS_A, d=DIM_A)
                q = over(heads(qk[:, u, 0:P]), 2, HEADS_A)
                k = over(heads(qk[:, u, P:]), 1, HEADS_A)
                dve.tensor_tensor(out, q, k, ALU.mult).then_inc(s.prod_qk, 1)
                done(dve, s.prod_qk, t)
                freed(dve, s.shifted, t)
                dve.tensor_reduce(score[:, u, :], prod_qk[:, u, :].rearrange("p (s d) -> p s d", d=DIM_A),
                                  AX_X, ALU.add).then_inc(s.score, 1)
                done(dve, s.score, t)
                dve.tensor_reduce(top[:, u, :], score[:, u, :].rearrange("p (h g) -> p h g", h=HEADS_A),
                                  AX_X, ALU.max).then_inc(s.top, 1)

            def shift(t, u4):
                u = u4 % 2
                done(dve, s.top, t)
                freed(dve, s.prob, t)
                by_head = "p (h g) -> p h g"
                dve.tensor_tensor(shifted[:, u, :].rearrange(by_head, h=HEADS_A),
                                   score[:, u, :].rearrange(by_head, h=HEADS_A),
                                   over(top[:, u, :], 2, HEADS_A), ALU.subtract).then_inc(s.shifted, 1)

            def totals(t, u4):
                u = u4 % 2
                done(dve, s.prob, t)
                dve.tensor_reduce(total[:, u, :], prob[:, u, :].rearrange("p (h g) -> p h g", h=HEADS_A),
                                  AX_X, ALU.add).then_inc(s.total, 1)
                done(dve, s.total, t)
                freed(dve, s.o, t)
                dve.reciprocal(inv[:, u, :], total[:, u, :]).then_inc(s.inv, 1)

            def divide(t, u4):
                u = u4 % 2
                done(dve, s.ps_mix, t)
                done(dve, s.inv, t)
                freed(dve, s.ps_o, t)
                dve.tensor_tensor(heads(o[:, u, :]), heads(ps_mix[:, 0:P]), over(inv[:, u, :], 2, DIM_A),
                                  ALU.mult).then_inc(s.o, 1)

            def stats_out(t, u4):
                u = u4 % 2
                done(dve, s.ps_out, t)
                dve.bn_stats(stats2[:, u, :], ps_out[u4][:, 0:P]).then_inc(s.stats2, 1)
                freed(dve, s.y, t, 4)
                done(dve, s.stats2, t)

            def variance_out(t, u4):
                u = u4 % 2
                done(dve, s.mean_var2, t)
                freed(dve, s.rstd2, t)
                dve.tensor_scalar(veps2[:, u, :], mean_var2[:, u4, 1:2], EPS, None, ALU.add).then_inc(s.veps2, 1)

            def aggregate_out(t, u4):
                u = u4 % 2
                dve.bn_aggr(mean_var2[:, u4, :], stats2[:, u, :]).then_inc(s.mean_var2, 1)

            def normalize_out(t, u4):
                u = u4 % 2
                done(dve, s.rstd2, t)
                freed(dve, s.x, t)
                dve.tensor_scalar(y[:, u, :], ps_out[u4][:, 0:P], mean_var2[:, u4, 0:1], rstd2[:, u, :],
                                  ALU.subtract, ALU.mult).then_inc(s.y, 1)

            dve.wait_ge(g.x_loaded, 16 * BATCHES)
            pipeline(dve, TILES, [(7, divide), (0, stats_in), (1, variance_in), (0, aggregate_in), (2, normalize),
                                  (8, stats_out), (9, variance_out), (8, aggregate_out), (10, normalize_out),
                                  (4, scores), (4, shift), (6, totals)], unroll=8, period=4)


def normalize_all(nc, g, name, src, dst, add):
    with ExitStack() as ctx:
        def sb(n, shape):
            return ctx.enter_context(nc.sbuf_tensor(name + n, shape, F32))

        stats = sb("stats", [P, 4, 6])
        mean_var = sb("mean_var", [P, 4, 2])
        veps = sb("veps", [P, 4, 1])
        rstd = sb("rstd", [P, 4, 1])
        shift = sb("shift", [P, 4, 1])
        y = sb("y", [P, 4, P])
        s = sems(ctx, nc, name, "stats mean_var veps rstd shift y dst")
        block = ctx.enter_context(nc.Block())

        @block.gpsimd
        def _(pool):
            def inverse(t, u):
                done(pool, s.veps, t)
                freed(pool, s.y, t, 4)
                freed(pool, s.shift, t, 4)
                pool.tensor_tensor(rstd[:, u, :], veps[:, u, :], g.minus_half[:], ALU.pow).then_inc(s.rstd, 1)

            pipeline(pool, TILES, [(1, inverse)], unroll=8, period=4)

        @block.scalar
        def _(act):
            def normalize(t, u):
                done(act, s.shift, t)
                if add:
                    freed(act, s.dst, t, 4)
                out = y[:, u, :] if add else dst[:, t, :]
                act.activation(out, src[:, t, :], ACT.Identity, bias=shift[:, u, :], scale=rstd[:, u, :]).then_inc(s.y, 1)

            pipeline(act, TILES, [(3, normalize)], unroll=8, period=4)

        @block.vector
        def _(dve):
            def stats_of(t, u):
                dve.bn_stats(stats[:, u, :], src[:, t, :]).then_inc(s.stats, 1)
                freed(dve, s.shift, t, 4)
                done(dve, s.stats, t)

            def variance(t, u):
                done(dve, s.mean_var, t)
                freed(dve, s.rstd, t, 4)
                dve.tensor_scalar(veps[:, u, :], mean_var[:, u, 1:2], EPS, None, ALU.add).then_inc(s.veps, 1)

            def aggregate(t, u):
                dve.bn_aggr(mean_var[:, u, :], stats[:, u, :]).then_inc(s.mean_var, 1)

            def shift_of(t, u):
                done(dve, s.rstd, t)
                freed(dve, s.y, t, 4)
                dve.scalar_tensor_tensor(out=shift[:, u, :], in0=mean_var[:, u, 0:1], scalar=-1.0, in1=rstd[:, u, :],
                                         op0=ALU.mult, op1=ALU.mult).then_inc(s.shift, 1)

            def residual(t, u):
                done(dve, s.y, t)
                dve.tensor_tensor(dst[:, t, :], dst[:, t, :], y[:, u, :], ALU.add).then_inc(s.dst, 1)

            pipeline(dve, TILES, [(0, stats_of), (1, variance), (0, aggregate), (2, shift_of)] + [(4, residual)] * add,
                     unroll=8, period=4)


def l0_ffn(nc, g, w, tab):
    with ExitStack() as ctx:
        y = ctx.enter_context(nc.sbuf_tensor("b_y", [P, TILES, P], F32))
        normalize_all(nc, g, "b_in_", g.x, y, False)
        for layer in range(LAYERS):
            local_attention(nc, g, w, tab, layer, y)
            gated_ffn(nc, g, w, layer, y)
        normalize_all(nc, g, "b_out_", y, g.x, True)


def shifted_transpose(act, g, s, t, u, n, ps_y, h_t):
    act.activation(h_t[0:64, u, :], ps_y[0:64, 0:P], ACT.Copy)
    act.activation(h_t[64:P, u, 1:P], ps_y[64:P, 0:P - 1], ACT.Copy)
    act.activation(h_t[64:P, 1 - u, 0:1], ps_y[64:P, P - 1:P], ACT.Copy, scale=g.carry[64:P, bass.ds(n, 1)]) \
        .then_inc(s.h_t, 1)


def local_attention(nc, g, w, tab, layer, y):
    F32R = mybir.dt.float32r
    pre = f"l{layer}_"
    WINDOWS = P // WINDOW
    with ExitStack() as ctx:
        def sb(name, shape, dt=F32):
            return ctx.enter_context(nc.sbuf_tensor(pre + name, shape, dt))

        def pb(name, shape=(P, 512)):
            return ctx.enter_context(nc.psum_tensor(pre + name, list(shape), F32))

        w_qkv = w.wqkv_b[layer]
        rot = sb("rot", [P, 4, SEQ_TILES, DIM_B])
        y_now = sb("y_now", [P, 2, P])
        h_t = sb("h_t", [P, 2, P])
        h_parts = sb("h_parts", [P, 2, 2, P], F32R)
        w_kv = sb("w_kv", [P, 2, 2 * INNER], F32R)
        by_cos = sb("by_cos", [P, 2, INNER])
        by_sin = sb("by_sin", [P, 2, INNER])
        square = sb("square", [P, 2, INNER])
        norm = sb("norm", [P, 2, 2 * HEADS_B])
        clipped = sb("clipped", [P, 2, 2 * HEADS_B])
        r_norm = sb("r_norm", [P, 2, 2 * HEADS_B])
        q_sum = sb("q_sum", [P, 2, INNER])
        k_sum = sb("k_sum", [P, 2, INNER])
        q_unit = sb("q_unit", [P, 2, INNER])
        k_unit = sb("k_unit", [P, 2, INNER])
        q_t = sb("q_t", [P, 2, WINDOWS, CHUNKS, P])
        k_t = sb("k_t", [P, 4, CHUNKS, KEYS_B])
        v = sb("v", [P, 4, INNER])
        v_shift = sb("v_shift", [P, 4, INNER])
        top = sb("top", [P, WINDOWS, CHUNKS])
        neg_top = sb("neg_top", [P, WINDOWS, CHUNKS])
        total = sb("total", [P, WINDOWS, CHUNKS])
        inv = sb("inv", [P, WINDOWS, CHUNKS])
        term = sb("term", [P, WINDOWS, 512])
        prob = sb("prob", [P, WINDOWS, 512])
        prob_t = sb("prob_t", [P, 512])
        o_t = sb("o_t", [P, 2, CHUNKS, P])
        ps_qk = [pb(f"ps_qk{k}") for k in range(2)]
        ps_v = pb("ps_v")
        ps_s = [pb(f"ps_s{w}") for w in range(WINDOWS)]
        ps_t = pb("ps_t")
        ps_o = pb("ps_o")
        ps_m = pb("ps_m")
        s = sems(ctx, nc, pre, "rot w_kv first y_now ps_y h_t h_hi h_lo ps_q ps_k square_q square_k cos_q sin_q cos_k sin_k q_sum k_sum "
                 "norm_q norm_k clipped r_norm q_unit k_unit ps_qt ps_kt q_t k_t k_next ps_v v v_before ps_s masked top "
                 "neg_top term inv prob ps_t prob_t ps_o o_t ps_w y")
        block = ctx.enter_context(nc.Block())

        def group(t, win):
            return t * WINDOWS + win

        def blocks(ap):
            return ap.rearrange("p (c n) -> p c n", c=CHUNKS)

        def heads(ap):
            return ap.rearrange("p (h d) -> p h d", d=DIM_B)

        def window(step, win):
            return lambda t, u4: step(t, u4, win)

        @block.tensor
        def _(pe):
            pe.wait_ge(s.first, 3)
            pe.wait_ge(s.w_kv, 2)

            def product(ps, u, cols):
                for k, (h, m) in enumerate(((0, 0), (0, 1), (1, 0))):
                    mm = pe.matmul(ps[:], h_parts[:, u, h, :], w_kv[:, m, cols], start=(k == 0), stop=(k == 2))
                return mm

            def transpose_y(t, u4):
                done(pe, s.y_now, t)
                if isinstance(t, int) and 1 <= t < 6:
                    done(pe, s.h_t, t - 1)
                freed(pe, s.y, t, 6)
                pe.transpose(ps_m[:, 0:P], y_now[:, u4 % 2, :], g.ident[:]).then_inc(s.ps_y, 1)

            def project_q(t, u4):
                done(pe, s.h_t, t)
                freed(pe, s.cos_q, t, 1)
                freed(pe, s.sin_q, t, 1)
                freed(pe, s.square_q, t, 1)
                pe.matmul(ps_qk[0][:], h_t[:, u4 % 2, :], w_qkv[:, 0:INNER], start=True, stop=True).then_inc(s.ps_q, 1)

            def project_k(t, u4):
                freed(pe, s.cos_k, t, 1)
                freed(pe, s.sin_k, t, 1)
                freed(pe, s.square_k, t, 1)
                done(pe, s.h_lo, t)
                product(ps_qk[1], u4 % 2, slice(0, INNER)).then_inc(s.ps_k, 1)

            def project_v(t, u4):
                if isinstance(t, int) and t == 1:
                    done(pe, s.v, 0)
                freed(pe, s.k_t, t)
                done(pe, s.h_lo, t)
                product(ps_v, u4 % 2, slice(INNER, 2 * INNER)).then_inc(s.ps_v, 1)

            def transpose_q(t, u4):
                done(pe, s.q_unit, t)
                if isinstance(t, int) and t + 1 == TILES:
                    freed(pe, s.k_t, t, 1)
                else:
                    done(pe, s.v, t + 1)
                for c in range(CHUNKS):
                    mm = pe.transpose(ps_v[:, c * P:c * P + P], q_unit[:, u4 % 2, c * P:c * P + P], g.ident[:])
                mm.then_inc(s.ps_qt, 1)

            def transpose_k(t, u4):
                done(pe, s.k_unit, t)
                done(pe, s.q_t, t)
                for c in range(CHUNKS):
                    mm = pe.transpose(ps_v[:, c * P:c * P + P], k_unit[:, u4 % 2, c * P:c * P + P], g.ident[:])
                mm.then_inc(s.ps_kt, 1)

            def scores(t, u4, win):
                if win == 0:
                    done(pe, s.k_t, t)
                    freed(pe, s.k_next, t, 1)
                    done(pe, s.q_t, t)
                freed(pe, s.masked, group(t, win))
                for c in range(CHUNKS):
                    mm = pe.matmul(ps_s[win][:, c * P:c * P + P], q_t[:, u4 % 2, win, c, :],
                                   k_t[:, u4, c, win * WINDOW:win * WINDOW + P], start=True, stop=True)
                mm.then_inc(s.ps_s, 1)

            def transpose_p(t, u4, win):
                done(pe, s.prob, group(t, win))
                freed(pe, s.prob_t, group(t, win), 1)
                for c in range(CHUNKS):
                    mm = pe.transpose(ps_t[:, c * P:c * P + P], prob[:, win, c * P:c * P + P], g.ident[:])
                mm.then_inc(s.ps_t, 1)

            def mix(t, u4, win):
                done(pe, s.prob_t, group(t, win))
                freed(pe, s.o_t, group(t, win), 1)
                if win == 0:
                    done(pe, s.v_before, t)
                values = (v_shift, v)[win]
                for c in range(CHUNKS):
                    cols = slice(c * P, c * P + P)
                    mm = pe.matmul(ps_o[:, cols], values[:, u4, cols], prob_t[:, cols], start=True, stop=True)
                mm.then_inc(s.ps_o, 1)

            def project_out(t, u4):
                done(pe, s.o_t, group(t, 1))
                if isinstance(t, int) and t + 5 >= TILES:
                    freed(pe, s.y, t, 1)
                if not isinstance(t, int) or t + 5 < TILES:
                    done(pe, s.h_t, t + 5)
                for c in range(CHUNKS):
                    mm = pe.matmul(ps_m[:, 0:P], o_t[:, u4 % 2, c, :], w.wo_b[layer][:, c, :],
                                   start=(c == 0), stop=(c == CHUNKS - 1))
                mm.then_inc(s.ps_w, 1)

            pipeline(pe, TILES, [
                (4, window(scores, 0)), (5, window(transpose_p, 0)), (1, project_q), (5, window(mix, 0)), (3, transpose_q),
                (6, project_out), (4, window(scores, 1)), (1, project_k), (5, window(transpose_p, 1)), (3, transpose_k),
                (0, transpose_y), (5, window(mix, 1)), (1, project_v)], unroll=8, period=4)

        @block.scalar
        def _(act):
            def copy_h(t, u4):
                done(act, s.ps_y, t)
                freed(act, s.ps_v, t, 1)
                shifted_transpose(act, g, s, t, u4 % 2, t % SEQ_TILES, ps_m, h_t)

            def split_high(t, u4):
                done(act, s.h_t, t)
                freed(act, s.ps_v, t)
                act.activation(h_parts[:, u4 % 2, 0, :], h_t[:, u4 % 2, :], ACT.Copy).then_inc(s.h_hi, 1)

            def square_q(t, u4):
                done(act, s.ps_q, t)
                freed(act, s.norm_q, t, 1)
                act.activation(square[:, 0, :], ps_qk[0][:], ACT.Square).then_inc(s.square_q, 1)

            def square_k(t, u4):
                done(act, s.ps_k, t)
                freed(act, s.norm_k, t, 1)
                act.activation(square[:, 1, :], ps_qk[1][:], ACT.Square).then_inc(s.square_k, 1)

            def copy_q(t, u4):
                done(act, s.ps_qt, t)
                if not isinstance(t, int) or t >= 2:
                    act.wait_ge(s.ps_s, group(t, 0) - 2)
                for h in range(2):
                    rows, queries = slice(h * DIM_B, (h + 1) * DIM_B), slice(h * WINDOW, (h + 1) * WINDOW)
                    e = act.activation(q_t[rows, u4 % 2, :, :, queries],
                                       ps_v[rows, :].rearrange("p (c w a) -> p w c a", c=CHUNKS, w=WINDOWS), ACT.Copy)
                e.then_inc(s.q_t, 1)

            def copy_v(t, u4):
                done(act, s.ps_v, t)
                if not isinstance(t, int) or t >= 4:
                    act.wait_ge(s.ps_o, group(t, 0) - 6)
                act.activation(v[:, u4, :], ps_v[:], ACT.Copy)
                act.activation(v_shift[WINDOW:P, u4, :], ps_v[0:WINDOW, :], ACT.Copy).then_inc(s.v, 1)
                if not isinstance(t, int) or t > 0:
                    act.wait_ge(s.v, t)
                before = 0 if isinstance(t, int) and t == 0 else (u4 + 3) % 4
                if isinstance(t, int) and t == 0:
                    act.wait_ge(s.v, 1)
                act.activation(v_shift[0:WINDOW, u4, :], v[WINDOW:P, before, :], ACT.Copy).then_inc(s.v_before, 1)

            def exp(t, u4, win):
                done(act, s.neg_top, group(t, win))
                for c in range(CHUNKS):
                    e = act.activation(term[:, win, c * P:c * P + P], term[:, win, c * P:c * P + P], ACT.Exp,
                                       bias=neg_top[:, win, c:c + 1], scale=8.0,
                                       accum_out=total[:, win, c:c + 1])
                e.then_inc(s.term, 1)

            def copy_p(t, u4, win):
                done(act, s.ps_t, group(t, win))
                freed(act, s.ps_o, group(t, win), 1)
                act.activation(prob_t[:], ps_t[:], ACT.Copy).then_inc(s.prob_t, 1)

            def copy_o(t, u4, win):
                done(act, s.ps_o, group(t, win))
                if win == 0:
                    freed(act, s.ps_w, t)
                for h in range(2):
                    rows, queries = slice(h * DIM_B, (h + 1) * DIM_B), slice(h * WINDOW, (h + 1) * WINDOW)
                    e = act.activation(o_t[rows, u4 % 2, :, win * WINDOW:(win + 1) * WINDOW],
                                       blocks(ps_o[rows, :])[:, :, queries], ACT.Copy)
                e.then_inc(s.o_t, 1)

            pipeline(act, TILES, [
                (5, window(copy_p, 0)), (1, split_high), (1, square_q), (4, window(exp, 0)), (3, copy_q), (5, window(copy_o, 0)),
                (1, square_k), (5, window(copy_p, 1)), (4, window(exp, 1)), (0, copy_h), (5, window(copy_o, 1)),
                (1, copy_v)], unroll=8, period=4)

        @block.gpsimd
        def _(pool):
            pool.memset(h_t[64:P, 0, 0:1], 0.0).then_inc(s.first, 1)
            pool.wait_ge(s.first, 1)
            pool.memset(k_t[:, 0, :, 0:WINDOW], 0.0).then_inc(s.first, 1)
            pool.wait_ge(s.first, 2)
            pool.memset(q_t[:], 0.0).then_inc(s.first, 1)

            def sum_of(t, u4, k, dst, cos_sem, sin_sem, read_sem, sem):
                done(pool, cos_sem, t)
                done(pool, sin_sem, t)
                freed(pool, read_sem, t)
                pool.tensor_tensor(dst[:, u4 % 2, :], by_cos[:, k, :], by_sin[:, k, :], ALU.add).then_inc(sem, 1)

            def sum_q(t, u4):
                sum_of(t, u4, 0, q_sum, s.cos_q, s.sin_q, s.q_unit, s.q_sum)

            def sum_k(t, u4):
                sum_of(t, u4, 1, k_sum, s.cos_k, s.sin_k, s.k_unit, s.k_sum)

            def inverse_norm(t, u4):
                done(pool, s.clipped, t)
                freed(pool, s.q_unit, t)
                freed(pool, s.k_unit, t)
                pool.tensor_tensor(r_norm[:, u4 % 2, :], clipped[:, u4 % 2, :],
                                   g.minus_half[:].to_broadcast([P, 2 * HEADS_B]), ALU.pow).then_inc(s.r_norm, 1)

            def scale_q(t, u4):
                done(pool, s.r_norm, t)
                done(pool, s.q_sum, t)
                freed(pool, s.ps_qt, t)
                pool.tensor_tensor(heads(q_unit[:, u4 % 2, :]), heads(q_sum[:, u4 % 2, :]),
                                   over(r_norm[:, u4 % 2, 0:HEADS_B], 2, DIM_B), ALU.mult).then_inc(s.q_unit, 1)

            def probabilities(t, u4, win):
                done(pool, s.inv, group(t, win))
                freed(pool, s.ps_t, group(t, win))
                pool.tensor_tensor(blocks(prob[:, win, :]), blocks(term[:, win, :]), over(inv[:, win, :], 2, P),
                                   ALU.mult).then_inc(s.prob, 1)

            pipeline(pool, TILES, [
                (2, inverse_norm), (1, sum_q), (4, window(probabilities, 0)), (2, scale_q), (1, sum_k),
                (4, window(probabilities, 1))], unroll=8, period=4)

        @block.vector
        def _(dve):
            dve.wait_ge(w.b_loaded, w.b_count)
            dve.tensor_copy(w_kv[:, 0], w_qkv[:, INNER:]).then_inc(s.w_kv, 1)
            dve.wait_ge(s.w_kv, 1)
            dve.tensor_tensor(w_kv[:, 1], w_qkv[:, INNER:], w_kv[:, 0].bitcast(F32), ALU.subtract).then_inc(s.w_kv, 1)
            for n in range(4):
                dve.tensor_tensor(rot[:, n], tab.rope_b[:, n], over(w.scales_b[:, layer, n, :], 1, SEQ_TILES),
                                  ALU.mult).then_inc(s.rot, 1)
            dve.wait_ge(s.rot, 4)
            dve.wait_ge(s.first, 3)

            def split_low(t, u4):
                done(dve, s.h_hi, t)
                freed(dve, s.ps_v, t)
                dve.tensor_tensor(h_parts[:, u4 % 2, 1, :], h_t[:, u4 % 2, :], h_parts[:, u4 % 2, 0, :].bitcast(F32),
                                  ALU.subtract).then_inc(s.h_lo, 1)

            def stage_y(t, u4):
                freed(dve, s.ps_y, t)
                dve.tensor_copy(y_now[:, u4 % 2, :], y[:, t, :]).then_inc(s.y_now, 1)

            def rotate(t, k, ps_sem, square_sem, cos_sem, sin_sem, read_sem):
                done(dve, ps_sem, t)
                done(dve, square_sem, t)
                freed(dve, read_sem, t, 1)
                tables = rot[:].rearrange("p k n d -> p k (n d)")
                at = (t % SEQ_TILES) * DIM_B
                dve.tensor_tensor(heads(by_cos[:, k, :]), heads(ps_qk[k][:]),
                                  over(tables[:, 2 * k, bass.ds(at, DIM_B)], 1, HEADS_B), ALU.mult).then_inc(cos_sem, 1)
                halves = "p (h a d) -> p a h d"
                src, dst = (x.rearrange(halves, a=2, d=DIM_B // 2) for x in (ps_qk[k][:], by_sin[:, k, :]))
                for a in range(2):
                    sin = tables[:, 2 * k + 1, bass.ds(at + a * (DIM_B // 2), DIM_B // 2)]
                    e = dve.tensor_tensor(dst[:, a], src[:, 1 - a], over(sin, 1, HEADS_B), ALU.mult)
                e.then_inc(sin_sem, 1)

            def rotate_q(t, u4):
                rotate(t, 0, s.ps_q, s.square_q, s.cos_q, s.sin_q, s.q_sum)

            def rotate_k(t, u4):
                rotate(t, 1, s.ps_k, s.square_k, s.cos_k, s.sin_k, s.k_sum)

            def norm_q(t, u4):
                freed(dve, s.clipped, t)
                dve.tensor_reduce(norm[:, u4 % 2, 0:HEADS_B], heads(square[:, 0, :]), AX_X, ALU.add).then_inc(s.norm_q, 1)

            def norm_k(t, u4):
                dve.tensor_reduce(norm[:, u4 % 2, HEADS_B:], heads(square[:, 1, :]), AX_X, ALU.add).then_inc(s.norm_k, 1)

            def clip_norm(t, u4):
                done(dve, s.norm_q, t)
                done(dve, s.norm_k, t)
                freed(dve, s.r_norm, t)
                dve.tensor_scalar(clipped[:, u4 % 2, :], norm[:, u4 % 2, :], 1e-24, None, ALU.max).then_inc(s.clipped, 1)

            def scale_k(t, u4):
                done(dve, s.r_norm, t)
                done(dve, s.k_sum, t)
                freed(dve, s.ps_kt, t)
                dve.tensor_tensor(heads(k_unit[:, u4 % 2, :]), heads(k_sum[:, u4 % 2, :]),
                                  over(r_norm[:, u4 % 2, HEADS_B:], 2, DIM_B), ALU.mult).then_inc(s.k_unit, 1)

            def copy_k(t, u4):
                done(dve, s.ps_kt, t)
                if not isinstance(t, int) or t >= 4:
                    dve.wait_ge(s.ps_s, group(t, 0) - 6)
                dve.tensor_copy(k_t[:, u4, :, WINDOW:], blocks(ps_v[:])).then_inc(s.k_t, 1)

            def keys_before(t, u4):
                if not isinstance(t, int) or t >= 3:
                    dve.wait_ge(s.ps_s, group(t, 0) - 4)
                done(dve, s.k_t, t)
                dve.tensor_copy(k_t[:, (u4 + 1) % 4, :, 0:WINDOW], k_t[:, u4, :, P:P + WINDOW]).then_inc(s.k_next, 1)

            def tops(t, u4, win):
                done(dve, s.ps_s, group(t, win))
                freed(dve, s.prob, group(t, win))
                at = (t % SEQ_TILES) * P if win == 0 else SEQ_TILES * P
                mask = over(tab.mask_b[:, bass.ds(at, P)], 1, CHUNKS)
                dve.tensor_tensor(blocks(term[:, win, :]), blocks(ps_s[win][:]), mask, ALU.add).then_inc(s.masked, 1)
                done(dve, s.masked, group(t, win))
                dve.tensor_reduce(top[:, win, :], blocks(term[:, win, :]), AX_X, ALU.max).then_inc(s.top, 1)
                done(dve, s.top, group(t, win))
                dve.tensor_scalar(neg_top[:, win, :], top[:, win, :], -8.0, None, ALU.mult).then_inc(s.neg_top, 1)

            def inverse(t, u4, win):
                done(dve, s.term, group(t, win))
                freed(dve, s.prob, group(t, win))
                dve.reciprocal(inv[:, win, :], total[:, win, :]).then_inc(s.inv, 1)

            def residual(t, u4):
                done(dve, s.ps_w, t)
                dve.tensor_tensor(y[:, t, :], y[:, t, :], ps_m[:, 0:P], ALU.add).then_inc(s.y, 1)

            pipeline(dve, TILES, [
                (4, window(tops, 0)), (2, clip_norm), (1, split_low), (1, rotate_q), (4, window(inverse, 0)), (1, norm_q),
                (6, residual), (0, stage_y), (4, window(tops, 1)), (3, copy_k), (3, keys_before), (2, scale_k),
                (1, rotate_k), (1, norm_k), (4, window(inverse, 1))], unroll=8, period=4)


def gated_ffn(nc, g, w, layer, y):
    F32R = mybir.dt.float32r
    pre = f"f{layer}_"
    PAD = 3 * P
    with ExitStack() as ctx:
        def sb(name, shape, dt=F32):
            return ctx.enter_context(nc.sbuf_tensor(pre + name, shape, dt))

        def pb(name, shape=(P, 512)):
            return ctx.enter_context(nc.psum_tensor(pre + name, list(shape), F32))

        w1 = w.w1_b[layer]
        w1_g = sb("w1_g", [P, 2, 2 * HID_B], F32R)
        beta = sb("beta", [P, P])
        offset = sb("offset", [P, 2 * HID_B])
        y_now = sb("y_now", [P, 2, P])
        h_t = sb("h_t", [P, 2, P])
        centred = sb("centred", [P, 4, 2, P], F32R)
        square = sb("square", [P, 2, P])
        veps = sb("veps", [P, 2, 1])
        rstd = sb("rstd", [P, 2, 1])
        gate = sb("gate", [P, 2, HID_B])
        gelu = sb("gelu", [P, 2, HID_B])
        linear = sb("linear", [P, 2, HID_B])
        hidden = sb("hidden", [P, 2, PAD])
        hidden_t = sb("hidden_t", [P, 2, PAD])
        ps_y = pb("ps_y")
        ps_c = pb("ps_c")
        ps_n = pb("ps_n")
        ps_a = pb("ps_a")
        ps_g = pb("ps_g")
        ps_t = pb("ps_t")
        ps_o = [pb(f"ps_o{u}") for u in range(2)]
        s = sems(ctx, nc, pre, "w1_g beta offset ps_off first y_now ps_y h_t ps_c centred centred_low square ps_n veps rstd ps_a ps_g "
                 "gate linear gelu hidden ps_t hidden_t ps_o y")
        block = ctx.enter_context(nc.Block())

        @block.tensor
        def _(pe):
            pe.wait_ge(s.beta, 1)
            for ps, cols in ((ps_a, slice(0, HID_B)), (ps_g, slice(HID_B, 2 * HID_B))):
                pe.matmul(ps[:, 0:HID_B], beta[:], w1[:, cols], start=True, stop=False)
                mm = pe.matmul(ps[:, 0:HID_B], g.ones_row[:], w.b1_b[:, layer, cols], start=False, stop=True)
            mm.then_inc(s.ps_off, 1)
            pe.wait_ge(s.offset, 2)
            pe.wait_ge(s.w1_g, 2)
            pe.wait_ge(s.first, 3)

            def transpose_y(t, u4):
                done(pe, s.y_now, t)
                freed(pe, s.h_t, t, 1)
                pe.transpose(ps_y[:, 0:P], y_now[:, u4 % 2, :], g.ident[:]).then_inc(s.ps_y, 1)

            def centre(t, u4):
                done(pe, s.h_t, t)
                freed(pe, s.square, t, 1)
                freed(pe, s.centred_low, t, 1)
                pe.matmul(ps_c[:, 0:P], g.centre[:], h_t[:, u4 % 2, :], start=True, stop=True).then_inc(s.ps_c, 1)

            def variance(t, u4):
                done(pe, s.square, t)
                freed(pe, s.veps, t, 1)
                pe.matmul(ps_n[:, 0:1], square[:, u4 % 2, :], g.mean_col[:], start=True, stop=True).then_inc(s.ps_n, 1)

            def expand(t, u4):
                def product(ps, cols):
                    for k, (c, m) in enumerate(((0, 0), (0, 1), (1, 0))):
                        mm = pe.matmul(ps[:, 0:HID_B + 1], centred[:, u4, c, :], w1_g[:, m, cols], start=(k == 0), stop=(k == 2))
                    return mm

                done(pe, s.centred_low, t)
                freed(pe, s.gate, t, 1)
                product(ps_g, slice(HID_B - 1, 2 * HID_B)).then_inc(s.ps_g, 1)
                freed(pe, s.linear, t, 1)
                product(ps_a, slice(0, HID_B + 1)).then_inc(s.ps_a, 1)

            def transpose_hidden(t, u4):
                done(pe, s.hidden, t)
                freed(pe, s.hidden_t, t, 1)
                for c in range(3):
                    mm = pe.transpose(ps_t[:, c * P:c * P + P], hidden[:, u4 % 2, c * P:c * P + P], g.ident[:])
                mm.then_inc(s.ps_t, 1)

            def contract(t, u4):
                done(pe, s.hidden_t, t)
                freed(pe, s.y, t)
                for c in range(3):
                    mm = pe.matmul(ps_o[u4 % 2][:, 0:P], hidden_t[:, u4 % 2, c * P:c * P + P], w.w2_b[layer][:, c, :],
                              start=(c == 0), stop=(c == 2))
                mm.then_inc(s.ps_o, 1)

            pipeline(pe, TILES, [(1, transpose_y), (5, transpose_hidden), (2, variance), (3, expand), (1, centre),
                                 (5, contract)], unroll=8, period=4)

        @block.scalar
        def _(act):
            done(act, s.ps_off, 0)
            act.activation(offset[:, 0:HID_B], ps_a[:, 0:HID_B], ACT.Copy).then_inc(s.offset, 1)
            act.activation(offset[:, HID_B:], ps_g[:, 0:HID_B], ACT.Copy).then_inc(s.offset, 1)

            def copy_h(t, u4):
                done(act, s.ps_y, t)
                freed(act, s.ps_c, t, 1)
                shifted_transpose(act, g, s, t, u4 % 2, t % SEQ_TILES, ps_y, h_t)

            def copy_centred(t, u4):
                done(act, s.ps_c, t)
                freed(act, s.ps_a, t, 4)
                act.activation(centred[:, u4, 0, :], ps_c[:, 0:P], ACT.Copy).then_inc(s.centred, 1)
                freed(act, s.ps_n, t)
                act.activation(square[:, u4 % 2, :], ps_c[:, 0:P], ACT.Square).then_inc(s.square, 1)

            def gelu_of(t, u4):
                done(act, s.gate, t)
                freed(act, s.hidden, t)
                act.activation(gelu[:, u4 % 2, :], gate[:, u4 % 2, :], ACT.Gelu).then_inc(s.gelu, 1)

            def copy_hidden(t, u4):
                done(act, s.ps_t, t)
                freed(act, s.ps_o, t)
                act.activation(hidden_t[:, u4 % 2, :], ps_t[:, 0:PAD], ACT.Copy).then_inc(s.hidden_t, 1)

            pipeline(act, TILES, [(1, copy_h), (5, copy_hidden), (4, gelu_of), (1, copy_centred)], unroll=8, period=4)

        @block.gpsimd
        def _(pool):
            pool.memset(h_t[64:P, 0, 0:1], 0.0).then_inc(s.first, 1)
            pool.wait_ge(s.first, 1)
            pool.memset(hidden[:], 0.0).then_inc(s.first, 1)
            pool.wait_ge(s.first, 2)
            pool.memset(hidden[:, :, HID_B:HID_B + 1], 1.0).then_inc(s.first, 1)
            pool.wait_ge(s.first, 3)

            def stage_y(t, u4):
                freed(pool, s.ps_y, t)
                pool.tensor_copy(y_now[:, u4 % 2, :], y[:, t, :]).then_inc(s.y_now, 1)

            def inverse(t, u4):
                done(pool, s.veps, t)
                freed(pool, s.linear, t)
                pool.tensor_tensor(rstd[:, u4 % 2, :], veps[:, u4 % 2, :], g.minus_half[:], ALU.pow).then_inc(s.rstd, 1)

            def gated(t, u4):
                done(pool, s.gelu, t)
                done(pool, s.linear, t)
                freed(pool, s.ps_t, t)
                pool.tensor_tensor(hidden[:, u4 % 2, 0:HID_B], linear[:, u4 % 2, :], gelu[:, u4 % 2, :], ALU.mult) \
                    .then_inc(s.hidden, 1)

            pipeline(pool, TILES, [(0, stage_y), (2, inverse), (4, gated)], unroll=8, period=4)

        @block.vector
        def _(dve):
            dve.wait_ge(w.b_loaded, w.b_count)
            dve.tensor_scalar(w1_g[:, 0], w1[:], w.ln_b[:, layer, 0:1], None, ALU.mult).then_inc(s.w1_g, 1)
            dve.tensor_scalar(beta[:], g.zeros[:], w.ln_b[:, layer, 1:2], None, ALU.add).then_inc(s.beta, 1)
            dve.wait_ge(s.w1_g, 1)
            dve.scalar_tensor_tensor(out=w1_g[:, 1], in0=w1[:], scalar=w.ln_b[:, layer, 0:1], in1=w1_g[:, 0].bitcast(F32),
                                     op0=ALU.mult, op1=ALU.subtract).then_inc(s.w1_g, 1)
            dve.wait_ge(s.offset, 2)

            def add_eps(t, u4):
                done(dve, s.ps_n, t)
                freed(dve, s.rstd, t)
                dve.tensor_scalar(veps[:, u4 % 2, :], ps_n[:, 0:1], EPS, None, ALU.add).then_inc(s.veps, 1)

            def centred_low(t, u4):
                done(dve, s.square, t)
                freed(dve, s.ps_a, t, 4)
                dve.tensor_tensor(centred[:, u4, 1, :], ps_c[:, 0:P], centred[:, u4, 0, :].bitcast(F32), ALU.subtract) \
                    .then_inc(s.centred_low, 1)

            def scale_hidden(t, u4):
                done(dve, s.rstd, t)
                done(dve, s.ps_g, t)
                freed(dve, s.gelu, t)
                dve.scalar_tensor_tensor(out=gate[:, u4 % 2, :], in0=ps_g[:, 1:HID_B + 1], scalar=rstd[:, u4 % 2, :],
                                         in1=offset[:, HID_B:], op0=ALU.mult, op1=ALU.add).then_inc(s.gate, 1)
                done(dve, s.ps_a, t)
                freed(dve, s.hidden, t)
                dve.scalar_tensor_tensor(out=linear[:, u4 % 2, :], in0=ps_a[:, 0:HID_B], scalar=rstd[:, u4 % 2, :],
                                         in1=offset[:, 0:HID_B], op0=ALU.mult, op1=ALU.add).then_inc(s.linear, 1)

            def residual(t, u4):
                done(dve, s.ps_o, t)
                dve.tensor_tensor(y[:, t, :], y[:, t, :], ps_o[u4 % 2][:, 0:P], ALU.add).then_inc(s.y, 1)

            pipeline(dve, TILES, [(6, residual), (2, add_eps), (3, scale_hidden), (1, centred_low)], unroll=8, period=4)


def l1_attention(nc, g, w):
    with ExitStack() as outer:
        def keep(name, shape, dt=F32):
            return outer.enter_context(nc.sbuf_tensor("c_" + name, shape, dt))

        xn = keep("xn", [P, TILES, P])
        vo = keep("vo", [P, BATCHES * CHUNKS + 1, SEQ_TILES, P])
        with ExitStack() as mid:
            h_all = mid.enter_context(nc.sbuf_tensor("c_h_all", [P, TOKENS], F32))
            l1_attention_values(nc, g, w, xn, h_all, vo)
            l1_attention_heads(nc, g, w, h_all, vo)
        l1_attention_out(nc, g, w, xn, vo)


def l1_attention_values(nc, g, w, xn, h_all, vo):
    with ExitStack() as ctx:
        def sb(name, shape, dt=F32):
            return ctx.enter_context(nc.sbuf_tensor("cv_" + name, shape, dt))

        stats = sb("stats", [P, 2, 6])
        mean_var = sb("mean_var", [P, 4, 2])
        veps = sb("veps", [P, 2, 1])
        rstd = sb("rstd", [P, 2, 1])
        stage = sb("stage", [P, 2, P])
        h_t = sb("h_t", [P, 2, P])
        ps_h = [ctx.enter_context(nc.psum_tensor(f"cv_ps_h{u}", [P, 512], F32)) for u in range(2)]
        ps_v = [ctx.enter_context(nc.psum_tensor(f"cv_ps_v{u}", [P, 512], F32)) for u in range(2)]
        s = sems(ctx, nc, "cv_", "stats mean_var veps rstd xn kept ps_h h_t h_all ps_v v")
        block = ctx.enter_context(nc.Block())

        @block.tensor
        def _(pe):
            pe.wait_ge(w.c_loaded, w.c_count)

            def project(t, u4):
                u = u4 % 2
                done(pe, s.h_t, t)
                freed(pe, s.v, t)
                pe.matmul(ps_v[u][:], h_t[:, u, :], w.wv_c[:], start=True, stop=True).then_inc(s.ps_v, 1)

            def transpose_in(t, u4):
                u = u4 % 2
                done(pe, s.xn, t)
                freed(pe, s.h_t, t)
                pe.transpose(ps_h[u][:, 0:P], stage[:, u, :], g.ident[:]).then_inc(s.ps_h, 1)

            pipeline(pe, TILES, [(3, transpose_in), (4, project)], unroll=8, period=4)

        @block.scalar
        def _(act):
            def copy_h(t, u4):
                u = u4 % 2
                done(act, s.ps_h, t)
                freed(act, s.ps_v, t)
                freed(act, s.h_all, t)
                act.activation(h_t[:, u, :], ps_h[u][:, 0:P], ACT.Copy).then_inc(s.h_t, 1)

            def keep_h(t, u4):
                done(act, s.h_t, t)
                act.activation(h_all[:, bass.ts(t, P)], h_t[:, u4 % 2, :], ACT.Copy).then_inc(s.h_all, 1)

            pipeline(act, TILES, [(3, copy_h), (4, keep_h)], unroll=8, period=4)

        @block.gpsimd
        def _(pool):
            def rstd_in(t, u4):
                u = u4 % 2
                done(pool, s.veps, t)
                freed(pool, s.xn, t)
                pool.tensor_tensor(rstd[:, u, :], veps[:, u, :], g.minus_half[:], ALU.pow).then_inc(s.rstd, 1)

            def keep_xn(t, u4):
                done(pool, s.xn, t)
                pool.tensor_copy(xn[:, t, :], stage[:, u4 % 2, :]).then_inc(s.kept, 1)

            pipeline(pool, TILES, [(1, rstd_in), (2, keep_xn)], unroll=8, period=4)

        @block.vector
        def _(dve):
            def stats_in(t, u4):
                u = u4 % 2
                dve.bn_stats(stats[:, u, :], g.x[:, t, :]).then_inc(s.stats, 1)
                freed(dve, s.xn, t, 4)
                done(dve, s.stats, t)

            def variance_in(t, u4):
                u = u4 % 2
                done(dve, s.mean_var, t)
                freed(dve, s.rstd, t)
                dve.tensor_scalar(veps[:, u, :], mean_var[:, u4, 1:2], EPS, None, ALU.add).then_inc(s.veps, 1)

            def aggregate_in(t, u4):
                dve.bn_aggr(mean_var[:, u4, :], stats[:, u4 % 2, :]).then_inc(s.mean_var, 1)

            def normalize(t, u4):
                u = u4 % 2
                done(dve, s.rstd, t)
                freed(dve, s.ps_h, t)
                freed(dve, s.kept, t)
                dve.tensor_scalar(stage[:, u, :], g.x[:, t, :], mean_var[:, u4, 0:1], rstd[:, u, :],
                                  ALU.subtract, ALU.mult).then_inc(s.xn, 1)

            def add_bias(t, u4):
                done(dve, s.ps_v, t)
                slot = (t // SEQ_TILES) * CHUNKS + 1
                dve.tensor_tensor(vo[:, bass.ds(slot, CHUNKS), bass.ds(t % SEQ_TILES, 1), :].rearrange("p c a n -> p c (a n)"),
                                  ps_v[u4 % 2][:].rearrange("p (c n) -> p c n", c=CHUNKS),
                                  w.bv_c[:].rearrange("p (c n) -> p c n", c=CHUNKS), ALU.add).then_inc(s.v, 1)

            pipeline(dve, TILES, [(0, stats_in), (1, variance_in), (0, aggregate_in), (2, normalize), (4, add_bias)],
                     unroll=8, period=4)


PAIR_STEPS = 2 * SEQ_TILES
STEPS_C = BATCHES * (HEADS_C // 2) * PAIR_STEPS


def l1_attention_heads(nc, g, w, h_all, vo):
    F32R = mybir.dt.float32r
    with ExitStack() as ctx:
        def sb(name, shape, dt=F32):
            return ctx.enter_context(nc.sbuf_tensor("ch_" + name, shape, dt))

        def pb(name, shape):
            return ctx.enter_context(nc.psum_tensor("ch_" + name, shape, F32))

        w_sorted = sb("w_sorted", [P, HEADS_C, P])
        w_now = sb("w_now", [P, P])
        q_hl = sb("q_hl", [P, 2, 2, SEQ], F32R)
        k_h = sb("k_h", [P, 2, 2, SEQ], F32R)
        k_l = sb("k_l", [P, 2, 2, SEQ], F32R)
        q_now = sb("q_now", [P, 2, P], F32R)
        neg_top = sb("neg_top", [P, 4, 1])
        prob = sb("prob", [P, 2, SEQ])
        total = sb("total", [P, 4, 1])
        inv = sb("inv", [P, 4, 1])
        prob_t = sb("prob_t", [P, 2, SEQ_TILES, P])
        ps_s = [pb(f"ps_s{u}", [P, SEQ]) for u in range(2)]
        ps_t = [pb(f"ps_t{u}", [P, 512]) for u in range(2)]
        ps_o = pb("ps_o", [P, 512])
        ps_p = pb("ps_p", [P, 512])
        s = sems(ctx, nc, "ch_", "w_sorted w_now ps_p q_hi k_hi q_lo k_lo q_now ps_s neg_top prob total ps_ta ps_tb pt_a pt_b ps_o inv o")
        block = ctx.enter_context(nc.Block())

        def job(t):
            return t // 4

        def job_place(t):
            return t // PAIR_STEPS, (t % 8) // 4, (t % PAIR_STEPS) // 8

        def job_columns(t):
            pair, head, half = job_place(t)
            return bass.ds((pair % 2) * 2 * SEQ + head * SEQ + half * 512, 512)

        def head_of(t):
            return (t // PAIR_STEPS) % (HEADS_C // 2) * 2 + (t % 8) // 4

        def flat(ap):
            return ap.rearrange("p a b n -> p (a b n)")

        TOP, BOTTOM = slice(0, DIM_C), slice(DIM_C, P)

        def bias(t, rows):
            return w.bias_c[rows, 0 if rows is TOP else 1, bass.ds(head_of(t), 1)]

        @block.tensor
        def _(pe):
            def project(t, u):
                if u:
                    return
                done(pe, s.w_now, job(t))
                freed(pe, s.q_lo, job(t), 1)
                freed(pe, s.k_lo, job(t), 1)
                pair, _, half = job_place(t)
                cols = (pair // (HEADS_C // 2)) * SEQ + half * 512
                pe.matmul(ps_p[:], w_now[:], h_all[:, bass.ds(cols, 512)], start=True, stop=True).then_inc(s.ps_p, 1)

            def scores(t, u):
                hh = u % 2
                pair = t // PAIR_STEPS
                if hh == 0:
                    pe.wait_ge(s.q_lo, (pair + 1) * 4)
                    pe.wait_ge(s.k_lo, (pair + 1) * 4)
                done(pe, s.q_now, t)
                freed(pe, s.prob, t)
                for half in range(2):
                    out = ps_s[hh][:, half * 512:half * 512 + 512]
                    cols = (pair % 2) * 2 * SEQ + hh * SEQ + half * 512
                    for part, (k, start) in enumerate(((k_h, True), (k_l, False))):
                        mm = pe.matmul(out, q_now[:, hh, :], flat(k[:])[:, bass.ds(cols, 512)], start=start,
                                       stop=not start)
                mm.then_inc(s.ps_s, 1)

            def transposes(t, u):
                done(pe, s.prob, t)
                for half, free, sem in ((0, s.pt_a, s.ps_ta), (1, s.pt_b, s.ps_tb)):
                    freed(pe, free, t, 1)
                    for j in range(4):
                        c = half * 4 + j
                        mm = pe.transpose(ps_t[half][:, j * P:(j + 1) * P], prob[:, u % 2, c * P:(c + 1) * P], g.ident[:])
                    mm.then_inc(sem, 1)

            def mix(t, u):
                freed(pe, s.o, t, 1)
                done(pe, s.pt_a, t)
                pair = t // PAIR_STEPS
                values = vo[:].rearrange("p c t n -> p (c t n)")
                base = (pair + 1) * (SEQ_TILES * P) + (u % 2) * DIM_C
                for j in range(SEQ_TILES):
                    if j == 4:
                        done(pe, s.pt_b, t)
                    mm = pe.matmul(ps_o[:, 0:DIM_C], prob_t[:, u % 2, j, :], values[:, bass.ds(base + j * P, DIM_C)],
                                   start=(j == 0), stop=(j == SEQ_TILES - 1))
                mm.then_inc(s.ps_o, 1)

            pipeline(pe, STEPS_C, [(17, scores), (18, transposes), (19, mix), (1, project)], unroll=8, period=4)

        @block.scalar
        def _(act):
            def split_high(t, u):
                cols = job_columns(t)
                if u == 0:
                    done(act, s.ps_p, job(t))
                    if not isinstance(t, int) or t >= 2 * PAIR_STEPS:
                        act.wait_ge(s.ps_s, (t - PAIR_STEPS) // PAIR_STEPS * PAIR_STEPS + 1)
                    act.activation(flat(q_hl[TOP])[:, cols], ps_p[TOP, :], ACT.Identity, bias=bias(t, TOP)).then_inc(s.q_hi, 1)
                if u == 1:
                    for rows in (TOP, BOTTOM):
                        e = act.activation(flat(k_h[rows])[:, cols], ps_p[BOTTOM, :], ACT.Identity, bias=bias(t, BOTTOM))
                    e.then_inc(s.k_hi, 1)

            def exp(t, u):
                done(act, s.neg_top, t)
                if not isinstance(t, int) or t >= 2:
                    act.wait_ge(s.ps_tb, t - 1)
                freed(act, s.inv, t, 4)
                act.activation(prob[:, u % 2, :], ps_s[u % 2][:], ACT.Exp, bias=neg_top[:, u, :],
                               accum_out=total[:, u, :]).then_inc(s.prob, 1)

            def copy_a(t, u):
                done(act, s.ps_ta, t)
                freed(act, s.ps_o, t)
                act.activation(prob_t[:, u % 2, 0:4, :].rearrange("p j n -> p (j n)"), ps_t[0][:], ACT.Copy) \
                    .then_inc(s.pt_a, 1)

            pipeline(act, STEPS_C, [(2, split_high), (18, copy_a), (17, exp)], unroll=8, period=4)

        @block.gpsimd
        def _(pool):
            pool.wait_ge(s.w_sorted, 2)

            def stage_weights(t, u):
                if u:
                    return
                if not isinstance(t, int) or t >= 4:
                    pool.wait_ge(s.ps_p, job(t))
                pool.tensor_copy(w_now[:], w_sorted[:].rearrange("p h n -> p (h n)")[:, bass.ds(head_of(t) * P, P)]) \
                    .then_inc(s.w_now, 1)

            def stage_q(t, u):
                hh = u % 2
                pair = t // PAIR_STEPS
                if hh == 0:
                    pool.wait_ge(s.q_lo, (pair + 1) * 4)
                freed(pool, s.ps_s, t)
                cols = (pair % 2) * 2 * SEQ + hh * SEQ + ((t % PAIR_STEPS) // 2) * P
                pool.tensor_copy(q_now[:, hh, :], flat(q_hl[:])[:, bass.ds(cols, P)]).then_inc(s.q_now, 1)

            pipeline(pool, STEPS_C, [(0, stage_weights), (17, stage_q)], unroll=8, period=4)

        @block.vector
        def _(dve):
            dve.wait_ge(w.c_loaded, w.c_count)
            src = w.wqk_c[:].rearrange("p (h d k) -> p k h d", k=2, d=DIM_C)
            dst = w_sorted[:].rearrange("p h (k d) -> p k h d", k=2)
            dve.tensor_scalar(dst[:, 0], src[:, 0], float(DIM_C) ** -0.5, None, ALU.mult).then_inc(s.w_sorted, 1)
            dve.tensor_copy(dst[:, 1], src[:, 1]).then_inc(s.w_sorted, 1)

            def split_low(t, u):
                cols = job_columns(t)
                if u == 1:
                    done(dve, s.q_hi, job(t))
                    dve.scalar_tensor_tensor(out=flat(q_hl[BOTTOM])[:, cols], in0=ps_p[TOP, :], scalar=bias(t, TOP),
                                             in1=flat(q_hl[TOP])[:, cols].bitcast(F32), op0=ALU.add, op1=ALU.subtract) \
                        .then_inc(s.q_lo, 1)
                if u == 2:
                    done(dve, s.k_hi, job(t))
                    for rows in (TOP, BOTTOM):
                        e = dve.scalar_tensor_tensor(out=flat(k_l[rows])[:, cols], in0=ps_p[BOTTOM, :], scalar=bias(t, BOTTOM),
                                                     in1=flat(k_h[BOTTOM])[:, cols].bitcast(F32), op0=ALU.add,
                                                     op1=ALU.subtract)
                    e.then_inc(s.k_lo, 1)

            def top(t, u):
                done(dve, s.ps_s, t)
                freed(dve, s.prob, t, 4)
                dve.tensor_reduce(neg_top[:, u, :], ps_s[u % 2][:], AX_X, ALU.max, negate=True).then_inc(s.neg_top, 1)

            def copy_b(t, u):
                done(dve, s.ps_tb, t)
                freed(dve, s.ps_o, t)
                dve.tensor_copy(prob_t[:, u % 2, 4:8, :].rearrange("p j n -> p (j n)"), ps_t[1][:]).then_inc(s.pt_b, 1)

            def inverse(t, u):
                done(dve, s.prob, t)
                freed(dve, s.o, t, 4)
                dve.reciprocal(inv[:, u, :], total[:, u, :]).then_inc(s.inv, 1)

            def scale_out(t, u):
                done(dve, s.ps_o, t)
                done(dve, s.inv, t)
                pair = t // PAIR_STEPS
                outputs = vo[:].rearrange("p c t n -> p (c t n)")
                base = pair * (SEQ_TILES * P) + ((t % PAIR_STEPS) // 2) * P + (u % 2) * DIM_C
                dve.tensor_scalar(outputs[:, bass.ds(base, DIM_C)], ps_o[:, 0:DIM_C], inv[:, u, :], None,
                                  ALU.mult).then_inc(s.o, 1)

            pipeline(dve, STEPS_C, [(18, inverse), (20, scale_out), (17, top), (18, copy_b), (2, split_low)],
                     unroll=8, period=4)

RSQRT2 = 2 ** -0.5


def l1_attention_out(nc, g, w, xn, vo):
    with ExitStack() as ctx:
        def sb(name, shape, dt=F32):
            return ctx.enter_context(nc.sbuf_tensor("co_" + name, shape, dt))

        def pb(name):
            return ctx.enter_context(nc.psum_tensor("co_" + name, [P, 512], F32))

        o_now = sb("o_now", [P, 2, INNER])
        o_t = sb("o_t", [P, 2, INNER])
        gamma = sb("gamma", [P, P])
        beta = sb("beta", [P, P])
        stats = sb("stats", [P, 2, 6])
        mean_var = sb("mean_var", [P, 4, 2])
        veps = sb("veps", [P, 2, 1])
        rstd = sb("rstd", [P, 2, 1])
        y = sb("y", [P, 2, P])
        scaled = sb("scaled", [P, 2, P])
        base = sb("base", [P, 2, P])
        z = sb("z", [P, 4, P])
        stats2 = sb("stats2", [P, 2, 6])
        mean_var2 = sb("mean_var2", [P, 4, 2])
        veps2 = sb("veps2", [P, 2, 1])
        rstd2 = sb("rstd2", [P, 2, 1])
        r = sb("r", [P, 2, P])
        ps_t = [pb(f"ps_t{u}") for u in range(2)]
        ps_y = [pb(f"ps_y{u}") for u in range(4)]
        s = sems(ctx, nc, "co_", "gamma beta o_now ps_t o_t ps_y stats mean_var veps rstd y scaled base z stats2 "
                 "mean_var2 veps2 rstd2 r x")
        block = ctx.enter_context(nc.Block())

        @block.tensor
        def _(pe):
            def transpose_o(t, u4):
                u = u4 % 2
                done(pe, s.o_now, t)
                freed(pe, s.o_t, t)
                for c in range(CHUNKS):
                    mm = pe.transpose(ps_t[u][:, c * P:(c + 1) * P], o_now[:, u, c * P:(c + 1) * P], g.ident[:])
                mm.then_inc(s.ps_t, 1)

            def project(t, u4):
                u = u4 % 2
                done(pe, s.o_t, t)
                freed(pe, s.y, t, 4)
                for c in range(CHUNKS):
                    pe.matmul(ps_y[u4][:, 0:P], o_t[:, u, c * P:(c + 1) * P], w.wout_c[:, c, :], start=(c == 0), stop=False)
                pe.matmul(ps_y[u4][:, 0:P], g.ones_row[:], w.bout_c[:], start=False, stop=True).then_inc(s.ps_y, 1)

            pipeline(pe, TILES, [(1, transpose_o), (2, project)], unroll=8, period=4)

        @block.scalar
        def _(act):
            def stage_o(t, u4):
                u = u4 % 2
                freed(act, s.ps_t, t)
                slot = (t // SEQ_TILES) * CHUNKS
                src = vo[:, bass.ds(slot, CHUNKS), bass.ds(t % SEQ_TILES, 1), :]
                act.activation(o_now[:, u, :].rearrange("p (c n) -> p c n", c=CHUNKS),
                               src.rearrange("p c a n -> p c (a n)"), ACT.Copy).then_inc(s.o_now, 1)

            def copy_o(t, u4):
                u = u4 % 2
                done(act, s.ps_t, t)
                freed(act, s.ps_y, t)
                act.activation(o_t[:, u, :], ps_t[u][:], ACT.Copy).then_inc(s.o_t, 1)

            pipeline(act, TILES, [(0, stage_o), (1, copy_o)], unroll=8, period=4)

        @block.gpsimd
        def _(pool):
            def rstd_y(t, u4):
                u = u4 % 2
                done(pool, s.veps, t)
                freed(pool, s.y, t)
                pool.tensor_tensor(rstd[:, u, :], veps[:, u, :], g.minus_half[:], ALU.pow).then_inc(s.rstd, 1)

            def affine(t, u4):
                u = u4 % 2
                done(pool, s.y, t)
                pool.tensor_tensor(scaled[:, u, :], y[:, u, :], gamma[:], ALU.mult).then_inc(s.scaled, 1)
                done(pool, s.scaled, t)
                done(pool, s.base, t)
                freed(pool, s.r, t, 4)
                pool.tensor_tensor(z[:, u4, :], scaled[:, u, :], base[:, u, :], ALU.add).then_inc(s.z, 1)

            def rstd_z(t, u4):
                u = u4 % 2
                done(pool, s.veps2, t)
                freed(pool, s.r, t)
                pool.tensor_tensor(rstd2[:, u, :], veps2[:, u, :], g.minus_half[:], ALU.pow).then_inc(s.rstd2, 1)

            def residual(t, u4):
                done(pool, s.r, t)
                pool.tensor_tensor(g.x[:, t, :], g.x[:, t, :], r[:, u4 % 2, :], ALU.add).then_inc(s.x, 1)

            pipeline(pool, TILES, [(4, rstd_y), (7, rstd_z), (5, affine), (8, residual)], unroll=8, period=4)

        @block.vector
        def _(dve):
            dve.tensor_scalar(gamma[:], w.gamma_c[:], RSQRT2, None, ALU.mult).then_inc(s.gamma, 1)
            dve.tensor_scalar(beta[:], w.beta_c[:], RSQRT2, None, ALU.mult).then_inc(s.beta, 1)
            dve.wait_ge(s.gamma, 1)
            dve.wait_ge(s.beta, 1)

            def stats_y(t, u4):
                done(dve, s.ps_y, t)
                dve.bn_stats(stats[:, u4 % 2, :], ps_y[u4][:, 0:P]).then_inc(s.stats, 1)
                freed(dve, s.y, t, 4)
                done(dve, s.stats, t)

            def variance_y(t, u4):
                u = u4 % 2
                done(dve, s.mean_var, t)
                freed(dve, s.rstd, t)
                dve.tensor_scalar(veps[:, u, :], mean_var[:, u4, 1:2], EPS, None, ALU.add).then_inc(s.veps, 1)

            def aggregate_y(t, u4):
                dve.bn_aggr(mean_var[:, u4, :], stats[:, u4 % 2, :]).then_inc(s.mean_var, 1)

            def normalize_y(t, u4):
                u = u4 % 2
                done(dve, s.rstd, t)
                freed(dve, s.scaled, t)
                dve.tensor_scalar(y[:, u, :], ps_y[u4][:, 0:P], mean_var[:, u4, 0:1], rstd[:, u, :],
                                  ALU.subtract, ALU.mult).then_inc(s.y, 1)
                freed(dve, s.z, t)
                dve.scalar_tensor_tensor(out=base[:, u, :], in0=xn[:, t, :], scalar=RSQRT2, in1=beta[:],
                                         op0=ALU.mult, op1=ALU.add).then_inc(s.base, 1)

            def stats_z(t, u4):
                done(dve, s.z, t)
                dve.bn_stats(stats2[:, u4 % 2, :], z[:, u4, :]).then_inc(s.stats2, 1)
                freed(dve, s.r, t, 4)
                done(dve, s.stats2, t)

            def variance_z(t, u4):
                u = u4 % 2
                done(dve, s.mean_var2, t)
                freed(dve, s.rstd2, t)
                dve.tensor_scalar(veps2[:, u, :], mean_var2[:, u4, 1:2], EPS, None, ALU.add).then_inc(s.veps2, 1)

            def aggregate_z(t, u4):
                dve.bn_aggr(mean_var2[:, u4, :], stats2[:, u4 % 2, :]).then_inc(s.mean_var2, 1)

            def normalize_z(t, u4):
                u = u4 % 2
                done(dve, s.rstd2, t)
                freed(dve, s.x, t)
                dve.tensor_scalar(r[:, u, :], z[:, u4, :], mean_var2[:, u4, 0:1], rstd2[:, u, :],
                                  ALU.subtract, ALU.mult).then_inc(s.r, 1)

            pipeline(dve, TILES, [(3, stats_y), (4, variance_y), (3, aggregate_y), (6, stats_z), (7, variance_z),
                                  (6, aggregate_z), (5, normalize_y), (8, normalize_z)], unroll=8, period=4)


def l1_ffn(nc, g, w):
    with ExitStack() as ctx:
        h_parts = ctx.enter_context(nc.sbuf_tensor("d_h_parts", [P, 2, TOKENS], mybir.dt.float32r))
        weight = ctx.enter_context(nc.sbuf_tensor("d_weight", [P, TILES, EXPERTS], F32))
        mixed = ctx.enter_context(nc.sbuf_tensor("d_mixed", [P, TILES, P], F32))
        with ExitStack() as mid:
            logits = mid.enter_context(nc.sbuf_tensor("d_logits", [P, TILES, EXPERTS], F32))
            router_logits(nc, g, w, h_parts, logits)
            route(nc, g, w, logits, weight)
        experts(nc, g, w, h_parts, weight, mixed)
        normalize_all(nc, g, "d_out_", mixed, g.x, True)


def router_logits(nc, g, w, h_parts, logits):
    with ExitStack() as ctx:
        def sb(name, shape, dt=F32):
            return ctx.enter_context(nc.sbuf_tensor("dr_" + name, shape, dt))

        stats = sb("stats", [P, 2, 6])
        mean_var = sb("mean_var", [P, 4, 2])
        veps = sb("veps", [P, 2, 1])
        rstd = sb("rstd", [P, 2, 1])
        h = sb("h", [P, 2, P])
        h_t = sb("h_t", [P, 2, P])
        ps_h = [ctx.enter_context(nc.psum_tensor(f"dr_ps_h{u}", [P, 512], F32)) for u in range(2)]
        ps_l = [ctx.enter_context(nc.psum_tensor(f"dr_ps_l{u}", [P, 512], F32)) for u in range(2)]
        s = sems(ctx, nc, "dr_", "stats mean_var veps rstd h ps_h h_t h_hi h_lo ps_l logits")
        block = ctx.enter_context(nc.Block())

        @block.tensor
        def _(pe):
            pe.wait_ge(w.d_loaded, w.d_count)

            def transpose_h(t, u4):
                u = u4 % 2
                done(pe, s.h, t)
                freed(pe, s.h_t, t)
                pe.transpose(ps_h[u][:, 0:P], h[:, u, :], g.ident[:]).then_inc(s.ps_h, 1)

            def project(t, u4):
                u = u4 % 2
                done(pe, s.h_t, t)
                freed(pe, s.logits, t)
                pe.matmul(ps_l[u][:, 0:EXPERTS], h_t[:, u, :], w.router_d[:], start=True, stop=True).then_inc(s.ps_l, 1)

            pipeline(pe, TILES, [(3, transpose_h), (3, project)], unroll=8, period=4)

        @block.scalar
        def _(act):
            def copy_h(t, u4):
                u = u4 % 2
                done(act, s.ps_h, t)
                freed(act, s.ps_l, t)
                freed(act, s.h_lo, t)
                act.activation(h_t[:, u, :], ps_h[u][:, 0:P], ACT.Copy).then_inc(s.h_t, 1)

            def copy_logits(t, u4):
                done(act, s.ps_l, t)
                act.activation(logits[:, t, :], ps_l[u4 % 2][:, 0:EXPERTS], ACT.Copy).then_inc(s.logits, 1)

            def keep_h(t, u4):
                done(act, s.h_t, t)
                act.activation(h_parts[:, 0, bass.ts(t, P)], h_t[:, u4 % 2, :], ACT.Copy).then_inc(s.h_hi, 1)

            pipeline(act, TILES, [(3, copy_h), (4, keep_h), (4, copy_logits)], unroll=8, period=4)

        @block.gpsimd
        def _(pool):
            def inverse(t, u4):
                u = u4 % 2
                done(pool, s.veps, t)
                freed(pool, s.h, t)
                pool.tensor_tensor(rstd[:, u, :], veps[:, u, :], g.minus_half[:], ALU.pow).then_inc(s.rstd, 1)

            pipeline(pool, TILES, [(1, inverse)], unroll=8, period=4)

        @block.vector
        def _(dve):
            def stats_of(t, u4):
                dve.bn_stats(stats[:, u4 % 2, :], g.x[:, t, :]).then_inc(s.stats, 1)
                freed(dve, s.h, t, 4)
                done(dve, s.stats, t)

            def variance(t, u4):
                u = u4 % 2
                done(dve, s.mean_var, t)
                freed(dve, s.rstd, t)
                dve.tensor_scalar(veps[:, u, :], mean_var[:, u4, 1:2], EPS, None, ALU.add).then_inc(s.veps, 1)

            def aggregate(t, u4):
                dve.bn_aggr(mean_var[:, u4, :], stats[:, u4 % 2, :]).then_inc(s.mean_var, 1)

            def normalize(t, u4):
                u = u4 % 2
                done(dve, s.rstd, t)
                freed(dve, s.ps_h, t)
                dve.tensor_scalar(h[:, u, :], g.x[:, t, :], mean_var[:, u4, 0:1], rstd[:, u, :],
                                  ALU.subtract, ALU.mult).then_inc(s.h, 1)

            def keep_low(t, u4):
                done(dve, s.h_hi, t)
                dve.tensor_tensor(h_parts[:, 1, bass.ts(t, P)], h_t[:, u4 % 2, :],
                                  h_parts[:, 0, bass.ts(t, P)].bitcast(F32), ALU.subtract).then_inc(s.h_lo, 1)

            pipeline(dve, TILES, [(0, stats_of), (1, variance), (0, aggregate), (2, normalize), (4, keep_low)], unroll=8, period=4)


def route(nc, g, w, logits, weight):
    with ExitStack() as ctx:
        def sb(name, shape, dt=F32):
            return ctx.enter_context(nc.sbuf_tensor("dw_" + name, shape, dt))

        COLS = TILES * EXPERTS
        best = sb("best", [P, TILES])
        shifted = sb("shifted", [P, TILES, EXPERTS])
        e = sb("e", [P, TILES, EXPERTS])
        total = sb("total", [P, TILES])
        inv = sb("inv", [P, TILES])
        left = sb("left", [P, 2, TILES, EXPERTS])
        top = sb("top", [P, 2, TILES])
        tie = sb("tie", [P, 2, TILES, EXPERTS])
        place = sb("place", [P, 2, TILES, EXPERTS])
        first = sb("first", [P, 2, TILES])
        chosen = sb("chosen", [P, 2, TILES, EXPERTS])
        chosen_bf = sb("chosen_bf", [P, 2, TILES, EXPERTS], BF16)
        counts = sb("counts", [P, 2, 2, TILES, EXPERTS])
        rank = sb("rank", [P, 2, TILES, EXPERTS])
        kept = sb("kept", [P, 2, TILES, EXPERTS])
        valued = sb("valued", [P, 2, TILES, EXPERTS])
        ps_before = [ctx.enter_context(nc.psum_tensor(f"dw_before{k}", [P, COLS], F32)) for k in range(2)]
        ps_count = [ctx.enter_context(nc.psum_tensor(f"dw_count{k}", [P, COLS], F32)) for k in range(2)]
        s = sems(ctx, nc, "dw_", "shifted exp chosen ps_before ps_count step")
        block = ctx.enter_context(nc.Block())

        @block.scalar
        def _(act):
            act.wait_ge(s.shifted, 1)
            act.activation(e[:], shifted[:], ACT.Exp).then_inc(s.exp, 1)

        @block.tensor
        def _(pe):
            pe.wait_ge(w.d_loaded, w.d_count)
            for k in range(2):
                pe.wait_ge(s.chosen, k + 1)
                cols = chosen_bf[:, k, :, :].rearrange("p t e -> p (t e)")
                pe.matmul(ps_before[k][:], w.earlier_d[:], cols, start=True, stop=True).then_inc(s.ps_before, 1)
                pe.matmul(ps_count[k][:], w.ones_d[:], cols, start=True, stop=True).then_inc(s.ps_count, 1)

        @block.vector
        def _(dve):
            steps = [0]

            def then(instruction):
                steps[0] += 1
                instruction.then_inc(s.step, 1)
                dve.wait_ge(s.step, steps[0])

            def by_tile(ap):
                return over(ap, 2, EXPERTS)

            iota = over(w.iota_d[:], 1, TILES)
            then(dve.tensor_reduce(best[:], logits[:], AX_X, ALU.max))
            dve.tensor_tensor(shifted[:], logits[:], by_tile(best[:]), ALU.subtract).then_inc(s.shifted, 1)
            dve.wait_ge(s.exp, 1)
            then(dve.tensor_reduce(total[:], e[:], AX_X, ALU.add))
            then(dve.reciprocal(inv[:], total[:]))
            then(dve.tensor_tensor(left[:, 0], e[:], by_tile(inv[:]), ALU.mult))
            for k in range(2):
                then(dve.tensor_reduce(top[:, k], left[:, k], AX_X, ALU.max))
                then(dve.tensor_tensor(tie[:, k], left[:, k], by_tile(top[:, k]), ALU.is_equal))
                then(dve.tensor_tensor(place[:, k], tie[:, k], iota, ALU.mult))
                then(dve.tensor_reduce(first[:, k], place[:, k], AX_X, ALU.min))
                then(dve.tensor_tensor(chosen[:, k], iota, by_tile(first[:, k]), ALU.is_equal))
                dve.tensor_copy(chosen_bf[:, k], chosen[:, k]).then_inc(s.chosen, 1)
                if k == 0:
                    then(dve.scalar_tensor_tensor(out=left[:, 1].rearrange("p t e -> p (t e)"),
                                                  in0=chosen[:, 0].rearrange("p t e -> p (t e)"), scalar=-2.0,
                                                  in1=left[:, 0].rearrange("p t e -> p (t e)"),
                                                  op0=ALU.mult, op1=ALU.add))
            for k in range(2):
                dve.wait_ge(s.ps_count, k + 1)
                then(dve.tensor_copy(counts[:, 0, k].rearrange("p t e -> p (t e)"), ps_count[k][:]))
            reach, at = 1, 0
            while reach < TILES:
                src, dst = counts[:, at], counts[:, 1 - at]
                dve.tensor_copy(dst[:, :, 0:reach, :], src[:, :, 0:reach, :]).then_inc(s.step, 1)
                steps[0] += 1
                then(dve.tensor_tensor(dst[:, :, reach:, :], src[:, :, reach:, :], src[:, :, :TILES - reach, :], ALU.add))
                reach, at = 2 * reach, 1 - at
            for k in range(2):
                dve.wait_ge(s.ps_before, k + 1)
                before = ps_before[k][:].rearrange("p (t e) -> p t e", e=EXPERTS)
                dve.tensor_copy(rank[:, k, 0:1, :], before[:, 0:1, :]).then_inc(s.step, 1)
                steps[0] += 1
                then(dve.tensor_tensor(rank[:, k, 1:, :], counts[:, at, k, 0:TILES - 1, :], before[:, 1:, :], ALU.add))
            then(dve.tensor_scalar(kept[:], rank[:], float(CAPACITY), None, ALU.is_lt))
            then(dve.tensor_tensor(kept[:], kept[:], chosen[:], ALU.mult))
            for k in range(2):
                then(dve.tensor_tensor(valued[:, k], kept[:, k], by_tile(top[:, k]), ALU.mult))
            then(dve.tensor_tensor(weight[:], valued[:, 0], valued[:, 1], ALU.add))


BLOCK = 512
BLOCKS = TOKENS // BLOCK
UNITS = EXPERTS * BLOCKS


def experts(nc, g, w, h_parts, weight, mixed):
    F32R = mybir.dt.float32r
    with ExitStack() as ctx:
        def sb(name, shape, dt=F32):
            return ctx.enter_context(nc.sbuf_tensor("de_" + name, shape, dt))

        mats = sb("mats", [P, 2, 3, P])
        parts = sb("parts", [P, 2, 2, 2, P], F32R)
        silu = sb("silu", [P, 2, BLOCK])
        hidden = sb("hidden", [P, 2, BLOCK])
        ps_gate = [ctx.enter_context(nc.psum_tensor(f"de_ps_gate{u}", [P, BLOCK], F32)) for u in range(2)]
        ps_up = [ctx.enter_context(nc.psum_tensor(f"de_ps_up{u}", [P, BLOCK], F32)) for u in range(2)]
        ps_out = [ctx.enter_context(nc.psum_tensor(f"de_ps_out{u}", [P, BLOCK], F32)) for u in range(2)]
        s = sems(ctx, nc, "de_", "zeroed w_hi w_lo ps_gate ps_up silu hidden ps_out mixed")
        loaded = [ctx.enter_context(nc.semaphore(f"de_loaded{u}")) for u in range(2)]
        block = ctx.enter_context(nc.Block())
        UNROLL = 2 * BLOCKS

        @block.sync
        def _(sp):
            def load(e, parity):
                for n, m in enumerate((w.gate, w.up, w.down)):
                    sp.dma_start(mats[:, parity, n, :], m[bass.ds(e, 1)].rearrange("a p n -> p (a n)")) \
                        .then_inc(loaded[parity], 16)

            load(0, 0)
            load(1, 1)
            with sp.Fori(2, EXPERTS - 1, 2) as e:
                for parity in range(2):
                    sp.wait_ge(s.ps_out, (e + parity - 1) * BLOCKS)
                    load(e + parity, parity)

        @block.tensor
        def _(pe):
            def product(out, parity, n, block):
                cols = slice(block * BLOCK, (block + 1) * BLOCK)
                for k, (m, h) in enumerate(((0, 0), (0, 1), (1, 0))):
                    mm = pe.matmul(out, parts[:, parity, m, n, :], h_parts[:, h, cols], start=(k == 0), stop=(k == 2))
                return mm

            def hidden_of(t, u16):
                u, parity, blk = u16 % 2, u16 // BLOCKS, u16 % BLOCKS
                if blk == 0:
                    pe.wait_ge(s.w_lo, t // BLOCKS + 1)
                freed(pe, s.silu, t)
                product(ps_gate[u][:], parity, 0, blk).then_inc(s.ps_gate, 1)
                freed(pe, s.hidden, t)
                product(ps_up[u][:], parity, 1, blk).then_inc(s.ps_up, 1)

            def out_of(t, u16):
                u, parity = u16 % 2, u16 // BLOCKS
                done(pe, s.hidden, t)
                freed(pe, s.mixed, t)
                for c in range(BLOCK // P):
                    mm = pe.matmul(ps_out[u][:, c * P:(c + 1) * P], hidden[:, u, c * P:(c + 1) * P], mats[:, parity, 2, :],
                                   start=True, stop=True)
                mm.then_inc(s.ps_out, 1)

            pipeline(pe, UNITS, [(2, hidden_of), (3, out_of)], unroll=UNROLL)

        @block.scalar
        def _(act):
            def split_high(t, u16):
                parity = u16 // BLOCKS
                if u16 % BLOCKS == 0:
                    act.wait_ge(loaded[parity], 48 * (t // UNROLL + 1))
                    if not isinstance(t, int) or t >= 2 * BLOCKS:
                        act.wait_ge(s.ps_up, t - BLOCKS)
                    act.activation(parts[:, parity, 0], mats[:, parity, 0:2], ACT.Copy).then_inc(s.w_hi, 1)

            def silu_of(t, u16):
                u = u16 % 2
                done(act, s.ps_gate, t)
                freed(act, s.hidden, t)
                act.activation(silu[:, u, :], ps_gate[u][:], ACT.Silu).then_inc(s.silu, 1)

            pipeline(act, UNITS, [(0, split_high), (2, silu_of)], unroll=UNROLL)

        @block.vector
        def _(dve):
            dve.memset(mixed[:], 0.0).then_inc(s.zeroed, 1)
            dve.wait_ge(s.zeroed, 1)

            def split_low(t, u16):
                parity = u16 // BLOCKS
                if u16 % BLOCKS == 0:
                    dve.wait_ge(s.w_hi, t // BLOCKS + 1)
                    dve.tensor_tensor(parts[:, parity, 1], mats[:, parity, 0:2], parts[:, parity, 0].bitcast(F32),
                                      ALU.subtract).then_inc(s.w_lo, 1)

            def gated(t, u16):
                u = u16 % 2
                done(dve, s.silu, t)
                done(dve, s.ps_up, t)
                freed(dve, s.ps_out, t)
                dve.tensor_tensor(hidden[:, u, :], silu[:, u, :], ps_up[u][:], ALU.mult).then_inc(s.hidden, 1)

            def accumulate(t, u16):
                u = u16 % 2
                done(dve, s.ps_out, t)
                tile = (u16 % BLOCKS) * (BLOCK // P)
                w_flat = weight[:].rearrange("p t e -> p (t e)")
                if not isinstance(t, int) or t >= BLOCKS:
                    dve.wait_ge(s.mixed, t - BLOCKS + 1)
                for c in range(BLOCK // P):
                    m = dve.scalar_tensor_tensor(out=mixed[:, tile + c, :], in0=ps_out[u][:, c * P:(c + 1) * P],
                                                 scalar=w_flat[:, bass.ds((tile + c) * EXPERTS + t // BLOCKS, 1)],
                                                 in1=mixed[:, tile + c, :], op0=ALU.mult, op1=ALU.add)
                m.then_inc(s.mixed, 1)

            pipeline(dve, UNITS, [(0, split_low), (2, gated), (3, accumulate)], unroll=UNROLL)


def build(nc, a, out):
    with ExitStack() as ctx:
        def sb(name, shape, dt=F32):
            return ctx.enter_context(nc.sbuf_tensor(name, shape, dt))

        def row(ap):
            return ap.rearrange("(a n) -> a n", a=1)

        x = sb("x", [P, TILES, P])
        ident = sb("ident", [P, P])
        ones_row = sb("ones_row", [1, P])
        minus_half = sb("minus_half", [P, 1])
        s = sems(ctx, nc, "g_", "ident0 ident_ready consts_ready ones_ready x_loaded small_loaded tab_loaded stored c_loaded b_loaded d_loaded")
        g = Group()
        g.x, g.ident, g.ones_row, g.minus_half = x, ident, ones_row, minus_half
        g.ident_ready, g.consts_ready, g.x_loaded = s.ident_ready, s.consts_ready, s.x_loaded
        small = [("wq_a", a["L0_attn_Wq"], [P, P]), ("wdown", a["L0_attn_Wdown"], [P, LATENT]),
                 ("wup", a["L0_attn_Wup"], [LATENT, 2 * P]), ("wout_a", a["L0_attn_Wout"], [P, P]),
                 ("bq_a", row(a["L0_attn_bq"]), [1, P]), ("bup", row(a["L0_attn_bup"]), [1, 2 * P]),
                 ("bout_a", row(a["L0_attn_bout"]), [1, P]),
                 ("bdown", a["L0_attn_bdown"].rearrange("(n a) -> n a", a=1), [LATENT, 1])]
        for_c = [("wqk_c", a["L1_attn_W_qk"], [P, 2 * INNER]), ("wv_c", a["L1_attn_W_v"], [P, INNER]),
                 ("bv_c", row(a["L1_attn_b_v"]).to_broadcast([P, INNER]), [P, INNER]), ("bout_c", row(a["L1_attn_b_out"]), [1, P]),
                 ("wout_c", a["L1_attn_W_out"].rearrange("(c p) n -> p c n", p=P), [P, CHUNKS, P]),
                 ("gamma_c", row(a["L1_attn_ln_gamma"]).to_broadcast([P, P]), [P, P]),
                 ("beta_c", row(a["L1_attn_ln_beta"]).to_broadcast([P, P]), [P, P])]
        bqk_c = sb("bqk_c", [P, HEADS_C, 2])
        bias_c = sb("bias_c", [P, 2, HEADS_C])
        w = Group()
        w.bias_c, w.c_loaded, w.c_count = bias_c, s.c_loaded, 16 * (len(for_c) + 2)
        w.small_loaded, w.small_count = s.small_loaded, 16 * len(small)
        dst = {n: sb(n, shape) for n, _, shape in small}
        w.wq_a, w.wdown, w.wup, w.wout_a, w.bq_a, w.bup, w.bout_a, w.bdown = (dst[n] for n, _, _ in small)
        dst_c = {n: sb(n, shape) for n, _, shape in for_c}
        w.wqk_c, w.wv_c, w.bv_c, w.bout_c, w.wout_c, w.gamma_c, w.beta_c = (dst_c[n] for n, _, _ in for_c)
        tab = Group()
        tab.rope_a, tab.loaded = sb("rope_a", [P, SEQ_TILES, 2 * DIM_A]), s.tab_loaded
        x_dram = a["L0_attn_x"].rearrange("b (n p) d -> b p n d", p=P)
        out_dram = out.rearrange("b (n p) d -> b p n d", p=P)
        shapes_b = [("rope_b", [P, 4, SEQ_TILES, DIM_B], F32), ("mask_b", [P, (SEQ_TILES + 1) * P], BF16), ("carry", [P, SEQ_TILES], F32),
                    ("centre", [P, P], F32),
                    ("mean_col", [P, 1], F32), ("zeros", [P, P], F32), ("ident_bf", [P, P], BF16)]
        for_d = [("router_d", a["L1_ffn_router_w"], [P, EXPERTS], F32), ("earlier_d", a["tab_earlier"], [P, P], BF16),
                 ("ones_d", a["tab_ones"], [P, P], BF16), ("iota_d", a["tab_iota"], [P, EXPERTS], F32)]
        d = {n: sb(n, shape, dt) for n, _, shape, dt in for_d}
        w.router_d, w.earlier_d, w.ones_d, w.iota_d = (d[n] for n, _, _, _ in for_d)
        w.d_loaded, w.d_count = s.d_loaded, 16 * len(for_d)
        w.gate, w.up, w.down = a["L1_ffn_gate_w"], a["L1_ffn_up_w"], a["L1_ffn_down_w"]

        with nc.Block() as block:
            @block.sync
            def _(sp):
                sp.dma_start(x[:, 0:SEQ_TILES, :], x_dram[0]).then_inc(s.x_loaded, 16)
                for n, src, _ in small:
                    sp.dma_start(dst[n][:], src).then_inc(s.small_loaded, 16)
                sp.dma_start(tab.rope_a[:], a["tab_rope_a"]).then_inc(s.tab_loaded, 16)
                for b in range(1, BATCHES):
                    sp.dma_start(x[:, b * SEQ_TILES:(b + 1) * SEQ_TILES, :], x_dram[b]).then_inc(s.x_loaded, 16)
                for n, src, _ in for_c:
                    sp.dma_start(dst_c[n][:], src).then_inc(s.c_loaded, 16)
                for n, src, _, _ in for_d:
                    sp.dma_start(d[n][:], src).then_inc(s.d_loaded, 16)
                for twice in range(2):
                    sp.dma_start(bqk_c[twice * DIM_C:(twice + 1) * DIM_C],
                                 a["L1_attn_b_qk"].rearrange("(h d k) -> d h k", k=2, d=DIM_C)).then_inc(s.c_loaded, 16)

            @block.gpsimd
            def _(pool):
                pool.memset(ident[:], 0.0).then_inc(s.ident0, 1)
                pool.memset(minus_half[:], -0.5)
                pool.memset(ones_row[:], 1.0).then_inc(s.consts_ready, 1)
                pool.wait_ge(s.ident0, 1)
                pool.affine_select(out=ident[:], in_=ident[:], compare_op=ALU.not_equal, fill=1.0, base=0,
                                   pattern=[[-1, P]], channel_multiplier=1).then_inc(s.ident_ready, 1)

        with ExitStack() as first_two:
            def sb2(name, shape, dt=F32):
                return first_two.enter_context(nc.sbuf_tensor(name, shape, dt))

            b = {n: sb2(n, shape, dt) for n, shape, dt in shapes_b}
            w.wqkv_b = [sb2(f"wqkv_b{n}", [P, 3 * INNER]) for n in range(LAYERS)]
            w.wo_b = [sb2(f"wo_b{n}", [P, CHUNKS, P]) for n in range(LAYERS)]
            w.w1_b = [sb2(f"w1_b{n}", [P, 2 * HID_B]) for n in range(LAYERS)]
            w.w2_b = [sb2(f"w2_b{n}", [P, 3, P]) for n in range(LAYERS)]
            w.b1_b = sb2("b1_b", [1, LAYERS, 2 * HID_B])
            w.ln_b = sb2("ln_b", [P, LAYERS, 2])
            w.scales_b = sb2("scales_b", [P, LAYERS, 4, DIM_B])
            tab.rope_b, tab.mask_b = b["rope_b"], b["mask_b"]
            g.carry, g.centre = b["carry"], b["centre"]
            g.mean_col, g.zeros, g.ident_bf = b["mean_col"], b["zeros"], b["ident_bf"]
            loads = [(b[n][:], a["tab_" + n]) for n, _, _ in shapes_b]
            last = HID_B - 2 * P
            half = DIM_B // 2
            for n in range(LAYERS):
                loads += [(w.wqkv_b[n][:], a["L0_ffn_wqkv"][n]),
                          (w.wo_b[n][:], a["L0_ffn_wo"][n].rearrange("(c p) n -> p c n", p=P)),
                          (w.w1_b[n][:], a["L0_ffn_w1"][n]),
                          (w.w2_b[n][:, 0:2, :], a["L0_ffn_w2"][n, 0:2 * P].rearrange("(c p) n -> p c n", p=P)),
                          (w.w2_b[n][0:last, 2, :], a["L0_ffn_w2"][n, 2 * P:HID_B]),
                          (w.w2_b[n][last:last + 1, 2, :], a["L0_ffn_b2"][n:n + 1, :])]
            loads.append((w.b1_b[:], a["L0_ffn_b1"].rearrange("(a l) n -> a l n", a=1)))
            for k, name in ((0, "L0_ffn_ln_g"), (1, "L0_ffn_ln_b")):
                loads.append((w.ln_b[:, :, k], a[name].rearrange("l n -> n l")))
            for k, name in ((0, "L0_ffn_q_scale"), (1, "L0_ffn_k_scale")):
                src = a[name].rearrange("(a l) d -> a l d", a=1).to_broadcast([P, LAYERS, DIM_B])
                loads += [(w.scales_b[:, :, 2 * k, :], src), (w.scales_b[:, :, 2 * k + 1, 0:half], src[:, :, half:]),
                          (w.scales_b[:, :, 2 * k + 1, half:], src[:, :, 0:half])]
            w.b_loaded, w.b_count = s.b_loaded, 16 * len(loads)

            with nc.Block() as block:
                @block.gpsimd
                def _(pool):
                    for n in range(LAYERS):
                        pool.memset(w.w2_b[n][:, 2, :], 0.0)

            with nc.Block() as block:
                @block.sync
                def _(sp):
                    for to, src in loads:
                        sp.dma_start(to, src, allow_slow_non_contiguous=True).then_inc(s.b_loaded, 16)

            l0_attention(nc, g, w, tab)
            with nc.Block() as block:
                @block.sync
                def _(sp):
                    sp.wait_ge(w.b_loaded, w.b_count)
            l0_ffn(nc, g, w, tab)

        with nc.Block() as block:
            @block.vector
            def _(dve):
                dve.wait_ge(w.c_loaded, w.c_count)
                dve.tensor_scalar(bias_c[:, 0, :], bqk_c[:, :, 0], float(DIM_C) ** -0.5, None, ALU.mult)
                dve.tensor_copy(bias_c[:, 1, :], bqk_c[:, :, 1])
        l1_attention(nc, g, w)
        l1_ffn(nc, g, w)

        with nc.Block() as block:
            @block.sync
            def _(sp):
                sp.wait_ge(s.x_loaded, 16 * BATCHES)
                sp.wait_ge(s.small_loaded, w.small_count)
                sp.wait_ge(s.tab_loaded, 16)
                sp.wait_ge(s.c_loaded, w.c_count)
                sp.wait_ge(s.d_loaded, w.d_count)
                for b in range(BATCHES):
                    sp.dma_start(out_dram[b], x[:, b * SEQ_TILES:(b + 1) * SEQ_TILES, :]).then_inc(s.stored, 16)
                sp.wait_ge(s.stored, 16 * BATCHES)


def tables():
    import numpy as np

    def by_tile(t):
        return np.ascontiguousarray(t.reshape(SEQ_TILES, P, -1).transpose(1, 0, 2))

    f = np.float32
    pos = np.arange(SEQ, dtype=f)
    inv = (f(1.0) / f(10000.0) ** (np.arange(0, DIM_A, 2, dtype=f) / f(DIM_A))).astype(f)
    angle = pos[:, None] * inv[None, :]
    cos, sin = np.cos(angle), np.sin(angle)
    rope_a = by_tile(np.concatenate([cos, cos, -sin, sin], axis=-1).astype(f))

    half = np.arange(0, DIM_B, 2, dtype=f)
    inv = f(1.0) / f(10000.0) ** (half / f(DIM_B))
    angle = (pos[:, None] * inv[None, :]).astype(f)
    base = ((half + f(0.4 * DIM_B)) / f(1.4 * DIM_B)).astype(f)
    power = ((pos - SEQ // 2) / f(WINDOW // 2)).astype(f)
    scale = (base[None, :] ** power[:, None]).astype(f)
    sign = np.concatenate([-np.ones(DIM_B // 2, f), np.ones(DIM_B // 2, f)])
    cos, sin, scale = (np.concatenate([m, m], axis=-1) for m in (np.cos(angle), np.sin(angle), scale))
    rope_b = np.stack([cos * scale, sign * sin * scale, cos / scale, sign * sin / scale]).astype(f)
    rope_b = np.ascontiguousarray(rope_b.reshape(4, SEQ_TILES, P, DIM_B).transpose(2, 0, 1, 3))

    bf16 = np.dtype("bfloat16")
    i, j = np.arange(P)[:, None] % WINDOW, np.arange(-WINDOW, WINDOW)[None, :]
    seen = (i >= j) & (i <= j + WINDOW)
    mask = np.stack([seen & (j >= 0)] + [seen] * SEQ_TILES, axis=1)
    mask_b = np.where(mask, f(0.0), f(-1e30)).astype(bf16).reshape(P, -1)

    carry = np.ones((P, SEQ_TILES), f)
    carry[:, SEQ_TILES - 1] = 0.0
    feature = np.arange(P)
    centre = (np.eye(P) - 1.0 / P).astype(f)
    iota = np.tile(np.arange(EXPERTS, dtype=f) - EXPERTS, (P, 1))
    earlier = (feature[:, None] < feature[None, :]).astype(bf16)
    return {"tab_iota": iota, "tab_earlier": earlier, "tab_ones": np.ones((P, P), bf16), "tab_rope_a": rope_a, "tab_rope_b": rope_b, "tab_mask_b": mask_b, "tab_carry": carry, 
            "tab_centre": centre, "tab_mean_col": np.full((P, 1), 1.0 / P, f),
            "tab_zeros": np.zeros((P, P), f), "tab_ident_bf": np.eye(P).astype(bf16)}


def kernel(**inputs):
    import numpy as np
    import concourse.bacc as bacc
    from concourse.bass_utils import run_bass_kernel_spmd

    nc = bacc.Bacc("TRN2", target_bir_lowering=False, num_devices=1)
    arrays, aps = {}, {}
    for name, value in [*inputs.items(), *tables().items()]:
        v = np.ascontiguousarray(value)
        arrays[name + "_dram"] = v
        aps[name] = nc.dram_tensor(name + "_dram", v.shape, mybir.dt.from_np(v.dtype), kind="ExternalInput").ap()
    out = nc.dram_tensor("out_dram", (BATCHES, SEQ, P), F32, kind="ExternalOutput").ap()
    build(nc, aps, out)
    r = run_bass_kernel_spmd(nc, [arrays], core_ids=[0])
    return r.results[0]["out_dram"]
```
